# Optimizing a Trainium2 kernel written in Bass

```python
import numpy as np
import jax
import jax.numpy as jnp

def _softmax(x, axis=-1):
    return jax.nn.softmax(x, axis=axis)

def _gelu(x):
    return jax.nn.gelu(x, approximate=True)

def _silu(x):
    return jax.nn.silu(x)

def _sigmoid(x):
    return jax.nn.sigmoid(x)

def _layernorm(x, axis=-1, eps=1e-05):
    m = jnp.mean(x, axis=axis, keepdims=True)
    v = jnp.var(x, axis=axis, keepdims=True)
    return (x - m) / jnp.sqrt(v + eps)

def _scatter_add(tgt, idx, src, axis=0):
    return tgt.at[idx].add(src)

def _segment_sum(src, seg, n):
    return jax.ops.segment_sum(src, seg, n)
kernel_name = 'mk_decoder_postln_d1_seqx_r8_05881a'

def setup_inputs(seed: int=0):
    np.random.seed(seed)
    _w = jnp.asarray

    def _rec_inputs():
        import jax
        import jax.numpy as jnp
        _rk = jax.random.key(seed)
        x = -0.0003929 + 0.9999 * jax.random.normal(jax.random.fold_in(_rk, 1), (4, 256, 128), jnp.float32)
        _lenS = 256 - jax.random.randint(jax.random.fold_in(_rk, 7), (4,), 0, max(1, 256 // 4) + 1, jnp.int32)
        _lenS2 = 256 - jax.random.randint(jax.random.fold_in(_rk, 8), (4,), 0, max(1, 256 // 4) + 1, jnp.int32)
        _ctx_1024P = jax.random.normal(jax.random.fold_in(_rk, 11), (4, 16, 128), jnp.float32)
        _ctx_1024c = jax.random.dirichlet(jax.random.fold_in(_rk, 511), 0.3 * jnp.ones((16,), jnp.float32), (4, 256))
        _ctx_1024t = jnp.einsum('bsk,bkd->bsd', _ctx_1024c, _ctx_1024P)
        _ctx_1024t = _ctx_1024t * jax.lax.rsqrt(jnp.mean(jnp.square(_ctx_1024t)) + 1e-12) * 0.953939
        ctx_1024 = 2.81802e-05 + 1.00001 * (_ctx_1024t + 0.3 * jax.random.normal(jax.random.fold_in(_rk, 611), (4, 256, 128), jnp.float32))
        return (x, ctx_1024, _lenS2)
    x, ctx_1024, _lenS2 = _rec_inputs()

    def _L0_attn_setup():
        import jax, jax.numpy as jnp
        import numpy as np
        EPS = 1e-06

        def rmsnorm(x, w, eps=EPS):
            return x * jax.lax.rsqrt(jnp.mean(x * x, axis=-1, keepdims=True) + eps) * w

        def bitlinear(x, w, eps=EPS):
            xn = x * jax.lax.rsqrt(jnp.mean(x * x, axis=-1, keepdims=True) + eps)
            s = 127.0 / jnp.clip(jnp.max(jnp.abs(xn), axis=-1, keepdims=True), 1e-05, None)
            xq = xn + jax.lax.stop_gradient(jnp.clip(jnp.round(xn * s), -128.0, 127.0) / s - xn)
            ws = 1.0 / jnp.clip(jnp.mean(jnp.abs(w)), 1e-05, None)
            wq = w + jax.lax.stop_gradient(jnp.clip(jnp.round(w * ws), -1.0, 1.0) / ws - w)
            return xq @ wq.T

        def swish(x):
            return x * jax.nn.sigmoid(x)

        def hgrn_scan(i, f):
            B, L, D = i.shape

            def step(h, xf):
                i_t, f_t = xf
                h = f_t * h + i_t
                return (h, h)
            _, o = jax.lax.scan(step, jnp.zeros((B, D), i.dtype), (i.swapaxes(0, 1), f.swapaxes(0, 1)))
            return o.swapaxes(0, 1)
        B, L, H = (4, 512, 128)
        I = 352
        key = jax.random.key(seed)
        ks = jax.random.split(key, 12)
        w = lambda k, o, i_: jax.random.normal(k, (o, i_), jnp.float32) * 0.02
        return {'hidden_states': jax.random.normal(ks[0], (B, L, H), jnp.float32), 'lower_bound': jax.random.uniform(ks[1], (H,), jnp.float32), 'attn_norm_w': jnp.ones((H,), jnp.float32), 'w_i': w(ks[2], H, H), 'w_f': w(ks[3], H, H), 'w_g': w(ks[4], H, H), 'g_norm_w': jnp.ones((H,), jnp.float32), 'w_o': w(ks[5], H, H), 'mlp_norm_w': jnp.ones((H,), jnp.float32), 'w_gate': w(ks[6], 2 * I, H), 'w_down': w(ks[7], H, I)}
    _L0_attn_all = _L0_attn_setup()
    _L0_attn_in = {k: v for k, v in _L0_attn_all.items() if k in ('lower_bound', 'attn_norm_w', 'w_i', 'w_f', 'w_g', 'g_norm_w', 'w_o', 'mlp_norm_w', 'w_gate', 'w_down')}
    del _L0_attn_all

    def _L0_xattn_setup():
        import jax, jax.numpy as jnp
        import numpy as np
        NEG = -10000000000000.0
        key = jax.random.key(seed)
        ks = jax.random.split(key, 7)
        B, L, D, E = (8, 256, 128, 128)
        Q = jax.random.normal(ks[0], (B, L, D), dtype=jnp.float32)
        K = jax.random.normal(ks[1], (B, L, D), dtype=jnp.float32)
        V = jax.random.normal(ks[2], (B, L, D), dtype=jnp.float32)
        query_pad_idxs = jax.random.randint(ks[3], (B,), 0, L)
        key_pad_idxs = jax.random.randint(ks[4], (B,), 0, L)
        W = jax.random.normal(ks[5], (E, D), dtype=jnp.float32) / np.sqrt(D)
        b = jax.random.normal(ks[6], (E,), dtype=jnp.float32) * 0.01
        return {'Q': Q, 'K': K, 'V': V, 'query_pad_idxs': query_pad_idxs, 'key_pad_idxs': key_pad_idxs, 'W': W, 'b': b}
    _L0_xattn_all = _L0_xattn_setup()
    _L0_xattn_in = {k: v for k, v in _L0_xattn_all.items() if k in ('W', 'b')}
    del _L0_xattn_all

    def _L0_ffn_setup():
        import jax, jax.numpy as jnp
        import numpy as np
        from jax import lax
        D = 128
        H = 512
        E = 8
        TOPK = 2
        key = jax.random.key(seed)
        ks = jax.random.split(key, 7)
        s = 0.02
        return {'x': jax.random.normal(ks[0], (2, 256, D), dtype=jnp.float32), 'W1': jax.random.normal(ks[1], (E, D, H), dtype=jnp.float32) * s, 'b1': jnp.zeros((E, H), dtype=jnp.float32), 'W2': jax.random.normal(ks[2], (E, H, D), dtype=jnp.float32) * s, 'b2': jnp.zeros((E, D), dtype=jnp.float32), 'Wr': jax.random.normal(ks[3], (D, E), dtype=jnp.float32) * s, 'br': jnp.zeros((E,), dtype=jnp.float32)}
    _L0_ffn_all = _L0_ffn_setup()
    _L0_ffn_in = {k: v for k, v in _L0_ffn_all.items() if k in ('W1', 'b1', 'W2', 'b2', 'Wr', 'br')}
    del _L0_ffn_all
    return {'x': x, 'ctx_1024': ctx_1024, '_lenS2': _lenS2, 'L0_attn_lower_bound': _L0_attn_in['lower_bound'], 'L0_attn_attn_norm_w': _L0_attn_in['attn_norm_w'], 'L0_attn_w_i': _L0_attn_in['w_i'], 'L0_attn_w_f': _L0_attn_in['w_f'], 'L0_attn_w_g': _L0_attn_in['w_g'], 'L0_attn_g_norm_w': _L0_attn_in['g_norm_w'], 'L0_attn_w_o': _L0_attn_in['w_o'], 'L0_attn_mlp_norm_w': _L0_attn_in['mlp_norm_w'], 'L0_attn_w_gate': _L0_attn_in['w_gate'], 'L0_attn_w_down': _L0_attn_in['w_down'], 'L0_xattn_W': _L0_xattn_in['W'], 'L0_xattn_b': _L0_xattn_in['b'], 'L0_ffn_W1': _L0_ffn_in['W1'], 'L0_ffn_b1': _L0_ffn_in['b1'], 'L0_ffn_W2': _L0_ffn_in['W2'], 'L0_ffn_b2': _L0_ffn_in['b2'], 'L0_ffn_Wr': _L0_ffn_in['Wr'], 'L0_ffn_br': _L0_ffn_in['br']}

def reference(x, ctx_1024, _lenS2, L0_attn_lower_bound, L0_attn_attn_norm_w, L0_attn_w_i, L0_attn_w_f, L0_attn_w_g, L0_attn_g_norm_w, L0_attn_w_o, L0_attn_mlp_norm_w, L0_attn_w_gate, L0_attn_w_down, L0_xattn_W, L0_xattn_b, L0_ffn_W1, L0_ffn_b1, L0_ffn_W2, L0_ffn_b2, L0_ffn_Wr, L0_ffn_br):
    import jax
    import jax.numpy as jnp

    def _L0_attn_ref(hidden_states, lower_bound, attn_norm_w, w_i, w_f, w_g, g_norm_w, w_o, mlp_norm_w, w_gate, w_down):
        import jax, jax.numpy as jnp
        import numpy as np
        EPS = 1e-06

        def rmsnorm(x, w, eps=EPS):
            return x * jax.lax.rsqrt(jnp.mean(x * x, axis=-1, keepdims=True) + eps) * w

        def bitlinear(x, w, eps=EPS):
            xn = x * jax.lax.rsqrt(jnp.mean(x * x, axis=-1, keepdims=True) + eps)
            s = 127.0 / jnp.clip(jnp.max(jnp.abs(xn), axis=-1, keepdims=True), 1e-05, None)
            xq = xn + jax.lax.stop_gradient(jnp.clip(jnp.round(xn * s), -128.0, 127.0) / s - xn)
            ws = 1.0 / jnp.clip(jnp.mean(jnp.abs(w)), 1e-05, None)
            wq = w + jax.lax.stop_gradient(jnp.clip(jnp.round(w * ws), -1.0, 1.0) / ws - w)
            return xq @ wq.T

        def swish(x):
            return x * jax.nn.sigmoid(x)

        def hgrn_scan(i, f):
            B, L, D = i.shape

            def step(h, xf):
                i_t, f_t = xf
                h = f_t * h + i_t
                return (h, h)
            _, o = jax.lax.scan(step, jnp.zeros((B, D), i.dtype), (i.swapaxes(0, 1), f.swapaxes(0, 1)))
            return o.swapaxes(0, 1)
        B, L, H = (4, 512, 128)
        I = 352
        residual = hidden_states
        x = rmsnorm(hidden_states, attn_norm_w)
        i = bitlinear(x, w_i)
        f = jax.nn.sigmoid(bitlinear(x, w_f))
        f = lower_bound + (1.0 - lower_bound) * f
        i = swish(i) * (1.0 - f)
        o = hgrn_scan(i, f)
        g = bitlinear(x, w_g)
        o = rmsnorm(o, g_norm_w) * swish(g)
        o = bitlinear(o, w_o)
        residual = o + residual
        h = rmsnorm(residual, mlp_norm_w)
        y = bitlinear(h, w_gate)
        gate, y = jnp.split(y, 2, axis=-1)
        z = bitlinear(swish(gate) * y, w_down)
        return residual + z

    def _L0_xattn_ref(Q, K, V, query_pad_idxs, key_pad_idxs, W, b):
        import jax, jax.numpy as jnp
        import numpy as np
        NEG = -10000000000000.0
        B, Lq, D = Q.shape
        Lk = K.shape[1]
        scale = 1.0 / jnp.sqrt(jnp.asarray(D, dtype=Q.dtype))
        scores = jnp.einsum('bqd,bkd->bqk', Q, K) * scale
        qpos = jnp.arange(Lq)[None, :, None]
        kpos = jnp.arange(Lk)[None, None, :]
        mask = (qpos >= query_pad_idxs[:, None, None]) & (kpos >= key_pad_idxs[:, None, None])
        scores = jnp.where(mask, jnp.asarray(NEG, scores.dtype), scores)
        attn = jax.nn.softmax(scores, axis=2)
        out = jnp.einsum('bqk,bkd->bqd', attn, V)
        return out @ W.T + b

    def _L0_ffn_ref(x, W1, b1, W2, b2, Wr, br):
        import jax, jax.numpy as jnp
        import numpy as np
        from jax import lax
        D = 128
        H = 512
        E = 8
        TOPK = 2
        B, S, _ = x.shape
        xf = x.reshape(-1, D)
        logits = xf @ Wr + br
        topv, _ = lax.top_k(logits, TOPK)
        thresh = topv[:, TOPK - 1:TOPK]
        masked = jnp.where(logits >= thresh, logits, -jnp.inf)
        weights = jax.nn.softmax(masked, axis=-1)
        h = jax.nn.gelu(jnp.einsum('td,edh->eth', xf, W1) + b1[:, None, :], approximate=False)
        expert_out = jnp.einsum('eth,ehd->etd', h, W2) + b2[:, None, :]
        out = jnp.einsum('etd,te->td', expert_out, weights)
        return out.reshape(B, S, D)
    x = _layernorm(x + _L0_attn_ref(x, L0_attn_lower_bound, L0_attn_attn_norm_w, L0_attn_w_i, L0_attn_w_f, L0_attn_w_g, L0_attn_g_norm_w, L0_attn_w_o, L0_attn_mlp_norm_w, L0_attn_w_gate, L0_attn_w_down), axis=-1)
    x = _layernorm(x + _L0_xattn_ref(x, ctx_1024, ctx_1024, _lenS2, _lenS2, L0_xattn_W, L0_xattn_b), axis=-1)
    x = _layernorm(x + _L0_ffn_ref(x, L0_ffn_W1, L0_ffn_b1, L0_ffn_W2, L0_ffn_b2, L0_ffn_Wr, L0_ffn_br), axis=-1)
    return x

_drawn_inputs = setup_inputs


def setup_inputs(seed=0):
    import zlib

    import numpy as np

    out = dict(_drawn_inputs(seed))
    spreads = {'L0_attn_attn_norm_w': (1.0, 0.6),
     'L0_attn_g_norm_w': (1.0, 0.6),
     'L0_attn_mlp_norm_w': (1.0, 0.2),
     'L0_ffn_b1': (0.0, 0.469),
     'L0_ffn_b2': (0.0, 0.1),
     'L0_ffn_br': (0.0, 0.1)}
    factors = {'L0_attn_w_f': 6.285, 'L0_xattn_b': 4.226}
    for name, (base, spread) in spreads.items():
        noise = np.random.default_rng([zlib.crc32(name.encode()), seed]).standard_normal(out[name].shape)
        drawn = base * np.exp(spread * noise) if base else spread * noise
        out[name] = jnp.asarray(drawn.astype(out[name].dtype))
    for name, factor in factors.items():
        out[name] = (out[name] * factor).astype(out[name].dtype)
    return out
```

```python
import concourse.bass as bass
from concourse import mybir
from contextlib import ExitStack

BATCH, SEQ, D = 4, 256, 128
P = 128
TILES = SEQ // P
INNER = 352
EXPERTS, HIDDEN = 8, 512
CHUNKS = HIDDEN // P
BITLINEAR = ("w_i", "w_f", "w_g", "w_o")
EPS = 1e-6
LN_EPS = 1e-5
CLIP = 1e-5
QMAX = 127.0
ROUND = 1.5 * 2.0 ** 23
SCALE = float(D) ** -0.5
NEG = -1e13


class Steps:

    def __init__(self, sem):
        self.sem, self.count = sem, 0

    def mark(self, instruction):
        instruction.then_inc(self.sem, 1)
        self.count += 1
        return self.count


def decoder_layer(nc, x, ctx_mem, pads, lower_bound, attn_norm_w, w_i, w_f, w_g, g_norm_w, w_o,
                  mlp_norm_w, w_gate, w_down, xattn_w, xattn_b, w1, b1, w2, b2, wr, br, out):
    fp32, bf16, int32 = mybir.dt.float32, mybir.dt.bfloat16, mybir.dt.int32
    ALU, ACT, AX = mybir.AluOpType, mybir.ActivationFunctionType, mybir.AxisListType.X
    AXY = mybir.AxisListType.XY
    GATE_ROWS = 2 * INNER
    GATE_BLOCKS = -(-GATE_ROWS // P)
    GATE_TAIL = GATE_ROWS - (GATE_BLOCKS - 1) * P
    DOWN = [(c, min(P, INNER - c * P)) for c in range(-(-INNER // P))]
    WCOLS = 4 * D + GATE_BLOCKS * D + INNER

    stack = ExitStack()
    with stack:
        def sb(name, shape, dt=fp32):
            return stack.enter_context(nc.sbuf_tensor(name, shape, dt))

        def pb(name, shape, dt=fp32):
            return stack.enter_context(nc.psum_tensor(name, shape, dt))

        def sem(name):
            return stack.enter_context(nc.semaphore(name))

        ident = sb("ident", [P, P])
        ones = sb("ones", [P, P])
        half = sb("half", [P, TILES])
        minus_half = sb("minus_half", [P, TILES])
        qpos = sb("qpos", [P, TILES])
        kpos = sb("kpos", [P, SEQ])
        qpos_i = sb("qpos_i", [P, TILES], int32)
        kpos_i = sb("kpos_i", [P, SEQ], int32)
        round_up = sb("round_up", [P, 1])
        round_down = sb("round_down", [P, 1])
        wraw = sb("wraw", [P, WCOLS])
        wmagic = sb("wmagic", [P, WCOLS])
        attn_raw = wraw[:, 0:4 * D].rearrange("p (k d) -> p k d", k=4)
        gate_raw = wraw[:, 4 * D:4 * D + GATE_BLOCKS * D].rearrange("p (k d) -> p k d", k=GATE_BLOCKS)
        down_raw = wraw[:, 4 * D + GATE_BLOCKS * D:WCOLS]
        attn_T = sb("attn_T", [P, 4 * D], bf16)
        gate_T = sb("gate_T", [P, GATE_ROWS], bf16)
        down_T = sb("down_T", [P, len(DOWN), D], bf16)
        wabs = sb("wabs", [P, 6])
        wmean = sb("wmean", [P, 6])
        wscale = sb("wscale", [P, 6])
        norm_w = sb("norm_w", [P, 3, D])
        gw_half = sb("gw_half", [P, D])
        xb_bias = sb("xb_bias", [P, D])
        br_bc = sb("br_bc", [P, EXPERTS])
        lb = sb("lb", [P, 1])
        f_gain = sb("f_gain", [P, 1])
        f_base = sb("f_base", [P, 1])
        xw_raw = sb("xw_raw", [P, D])
        xw_T = sb("xw_T", [P, D])
        wr_sb = sb("wr_sb", [P, EXPERTS])
        b2_sb = sb("b2_sb", [EXPERTS, D])
        b1_rows = sb("b1_rows", [EXPERTS * CHUNKS, P])
        b1_T = sb("b1_T", [P, EXPERTS * CHUNKS])
        w1_sb = sb("w1_sb", [P, EXPERTS, HIDDEN])
        w2_sb = sb("w2_sb", [P, EXPERTS, CHUNKS, D])
        xt = sb("xt", [P, TILES, D])
        ctx = sb("ctx", [P, TILES, D])
        pad_i = sb("pad_i", [P, 1], int32)
        pad_f = sb("pad_f", [P, 1])
        qneg = sb("qneg", [P, TILES])
        negmask = sb("negmask", [P, TILES, SEQ])
        NORMS = ("in", "out", "mlp", "z")
        stat = {t: {n: sb(f"{n}_{t}", [P, TILES]) for n in
                    ("ssx", "ssu", "peak", "tail", "var", "peakq", "root", "step", "inv", "rroot", "deq")}
                for t in NORMS}
        junk = sb("junk", [P, 16, INNER])
        u_in = sb("u_in", [P, TILES, D])
        q = {t: sb(f"q_{t}", [P, TILES, D if t != "z" else INNER]) for t in NORMS}
        qT = {t: sb(f"qT_{t}", [P, SEQ], bf16) for t in ("in", "out", "mlp")}
        qT_z = sb("qT_z", [P, TILES, len(DOWN), P], bf16)
        deq3 = sb("deq3", [P, TILES, 3])
        ifg = sb("ifg", [P, TILES, 3, D])
        th = sb("th", [P, TILES, 3, D])
        si2 = sb("si2", [P, TILES, D])
        sg2 = sb("sg2", [P, TILES, D])
        gain = sb("gain", [P, TILES, D])
        f_T = sb("f_T", [P, SEQ])
        omf_T = sb("omf_T", [P, SEQ])
        i_T = sb("i_T", [P, SEQ])
        o_T = sb("o_T", [P, SEQ])
        u_out = sb("u_out", [P, TILES, D])
        res = sb("res", [P, TILES, D])
        xres = sb("xres", [P, TILES, D])
        u_mlp = sb("u_mlp", [P, TILES, D])
        deqh = sb("deqh", [P, TILES])
        deqg = sb("deqg", [P, TILES])
        zt = sb("zt", [P, TILES, INNER])
        za = sb("za", [P, TILES, INNER])
        z = sb("z", [P, TILES, INNER])
        pre = [sb(f"pre{k}", [P, TILES, D]) for k in range(2)]
        bn = [sb(f"bn{k}", [P, TILES, 6]) for k in range(3)]
        mv = [sb(f"mv{k}", [P, TILES, 2]) for k in range(3)]
        lnv = [sb(f"lnv{k}", [P, TILES]) for k in range(3)]
        rstd = [sb(f"rstd{k}", [P, TILES]) for k in range(3)]
        x1 = sb("x1", [P, TILES, D])
        x1b = sb("x1b", [P, TILES, D])
        x1_T = sb("x1_T", [P, SEQ])
        ctx_T = sb("ctx_T", [P, SEQ])
        sc = sb("sc", [P, TILES, SEQ])
        negmax = sb("negmax", [P, TILES])
        prob = sb("prob", [P, TILES, SEQ])
        psum_row = sb("psum_row", [P, TILES])
        rsum = sb("rsum", [P, TILES])
        prob_T = sb("prob_T", [P, TILES, SEQ])
        att_T = sb("att_T", [P, SEQ])
        x2 = sb("x2", [P, TILES, D])
        x2_T = sb("x2_T", [P, SEQ])
        lg = sb("lg", [P, TILES, EXPERTS])
        top = sb("top", [P, TILES, 8])
        negtop = sb("negtop", [P, TILES])
        eg = sb("eg", [P, TILES, EXPERTS])
        em = sb("em", [P, TILES, EXPERTS])
        esum = sb("esum", [P, TILES])
        ersum = sb("ersum", [P, TILES])
        gate_w = sb("gate_w", [P, TILES, EXPERTS])
        gate_wT = sb("gate_wT", [EXPERTS, SEQ])
        hid = sb("hid", [P, 2, CHUNKS, SEQ])
        acc = sb("acc", [P, TILES, D])
        yout = sb("yout", [P, TILES, D])

        T = pb("T", [P, 512])
        M = pb("M", [P, 2, 512])
        H = pb("H", [P, 2, CHUNKS, SEQ])
        Y = pb("Y", [P, TILES, D])

        x_loaded, ctx_loaded, pad_loaded = sem("x_loaded"), sem("ctx_loaded"), sem("pad_loaded")
        wattn_loaded, wgate_loaded, wdown_loaded = sem("wattn_loaded"), sem("wgate_loaded"), sem("wdown_loaded")
        norm_loaded, small_loaded = sem("norm_loaded"), sem("small_loaded")
        w1_loaded = [sem(f"w1_loaded{e}") for e in range(EXPERTS)]
        w2_loaded = [sem(f"w2_loaded{e}") for e in range(EXPERTS)]
        stored = sem("stored")
        pad_zeroed, pool_step, ident_ready, ones_ready, masks_consts = (
            sem("pad_zeroed"), sem("pool_step"), sem("ident_ready"), sem("ones_ready"), sem("mask_consts"))
        wabs_ready, wtot_ready, wscale_ready = sem("wabs_ready"), sem("wtot_ready"), sem("wscale_ready")
        wmagic_ready, wclip_ready, wT_ready, wT_moved = (
            sem("wmagic_ready"), sem("wclip_ready"), sem("wT_ready"), sem("wT_moved"))
        vec_step, act_step = sem("vec_step"), sem("act_step")
        u_ready = {t: sem(f"u_ready_{t}") for t in NORMS}
        squares = {t: sem(f"squares_{t}") for t in NORMS}
        var_ready = {t: sem(f"var_ready_{t}") for t in NORMS}
        root_ready = {t: sem(f"root_ready_{t}") for t in NORMS}
        q_ready = {t: sem(f"q_ready_{t}") for t in NORMS}
        qT_ready = {t: sem(f"qT_ready_{t}") for t in NORMS}
        qT_moved = {t: sem(f"qT_moved_{t}") for t in NORMS}
        ifg_done, ifg_ready, th_ready, si_ready, sg_ready, gain_ready = (
            sem("ifg_done"), sem("ifg_ready"), sem("th_ready"), sem("si_ready"), sem("sg_ready"), sem("gain_ready"))
        if_T_ready, scan_done, o_ready, wo_done = sem("if_T_ready"), sem("scan_done"), sem("o_ready"), sem("wo_done")
        if_T_read = sem("if_T_read")
        res_ready, xres_ready = sem("res_ready"), sem("xres_ready")
        gate_done, deqh_ready, zt_ready, z_ready, down_done = (
            sem("gate_done"), sem("deqh_ready"), sem("zt_ready"), sem("z_ready"), sem("down_done"))
        ln_var, ln_rstd = [sem(f"ln_var{k}") for k in range(3)], [sem(f"ln_rstd{k}") for k in range(3)]
        x1_ready, x1b_ready, x1T_ready, x1T_moved = sem("x1_ready"), sem("x1b_ready"), sem("x1T_ready"), sem("x1T_moved")
        ctxT_ready, ctxT_moved = sem("ctxT_ready"), sem("ctxT_moved")
        mask_ready, scores_done, sc_ready, prob_ready = sem("mask_ready"), sem("scores_done"), sem("sc_ready"), sem("prob_ready")
        probT_ready, probT_moved, att_done, attT_moved, proj_done = (
            sem("probT_ready"), sem("probT_moved"), sem("att_done"), sem("attT_moved"), sem("proj_done"))
        x2_ready, x2T_ready, x2T_moved = sem("x2_ready"), sem("x2T_ready"), sem("x2T_moved")
        logits_done, logits_moved, negtop_ready, eg_ready, gatew_ready = (
            sem("logits_done"), sem("logits_moved"), sem("negtop_ready"), sem("eg_ready"), sem("gatew_ready"))
        gwT_ready, gwT_moved, b2_done = sem("gwT_ready"), sem("gwT_moved"), sem("b2_done")
        acc_started = sem("acc_started")
        fc1_done, gelu_done, fc2_done, combined = sem("fc1_done"), sem("gelu_done"), sem("fc2_done"), sem("combined")
        out_ready = sem("out_ready")

        block = stack.enter_context(nc.Block())

        def tiles_of(dram, g):
            return dram[g].rearrange("(j p) d -> p j d", p=P)

        @block.sync
        def _(sp):
            sp.dma_start(xt[:], tiles_of(x, 0)).then_inc(x_loaded, 16)
            for k, w in enumerate((attn_norm_w, g_norm_w, mlp_norm_w)):
                sp.dma_start(norm_w[:, k, :], w.partition_broadcast(P)).then_inc(norm_loaded, 16)
            for k, w in enumerate((w_i, w_f, w_g, w_o)):
                sp.dma_start(attn_raw[:, k, :], w).then_inc(wattn_loaded, 16)
            sp.wait_ge(pad_zeroed, 1)
            sp.dma_start(gate_raw[:, 0:GATE_BLOCKS - 1, :],
                         w_gate[0:(GATE_BLOCKS - 1) * P, :].rearrange("(k p) d -> p k d", p=P)).then_inc(wgate_loaded, 16)
            sp.dma_start(gate_raw[0:GATE_TAIL, GATE_BLOCKS - 1, :],
                         w_gate[(GATE_BLOCKS - 1) * P:GATE_ROWS, :]).then_inc(wgate_loaded, 16)
            sp.dma_start(down_raw, w_down).then_inc(wdown_loaded, 16)
            for e in range(EXPERTS):
                sp.dma_start(w1_sb[:, e, :], w1[e]).then_inc(w1_loaded[e], 16)
                sp.dma_start(w2_sb[:, e, :, :], w2[e].rearrange("(c p) d -> p c d", p=P)).then_inc(w2_loaded[e], 16)
            for g in range(BATCH):
                if g + 1 < BATCH:
                    sp.wait_ge(xres_ready, g + 1)
                    sp.dma_start(xt[:], tiles_of(x, g + 1)).then_inc(x_loaded, 16)
                sp.wait_ge(out_ready, TILES * (g + 1))
                sp.dma_start(tiles_of(out, g), yout[:]).then_inc(stored, 16)
            sp.wait_ge(stored, 16 * BATCH)

        @block.gpsimd
        def _(pool):
            step = Steps(pool_step)
            nc.gpsimd.memset(gate_raw[GATE_TAIL:P, GATE_BLOCKS - 1, :], 0.0).then_inc(pad_zeroed, 1)
            pool.wait_ge(pad_zeroed, 1)
            n = step.mark(nc.gpsimd.memset(ident[:], 0.0))
            nc.gpsimd.memset(ones[:], 1.0).then_inc(ones_ready, 1)
            step.mark(nc.gpsimd.memset(half[:], 0.5))
            consts = step.mark(nc.gpsimd.memset(minus_half[:], -0.5))
            pool.wait_ge(pool_step, n)
            nc.gpsimd.affine_select(out=ident[:], in_=ident[:], compare_op=ALU.not_equal, fill=1.0, base=0,
                                    pattern=[[-1, P]], channel_multiplier=1).then_inc(ident_ready, 1)
            step.mark(nc.gpsimd.iota(qpos_i[:], pattern=[[P, TILES]], base=0, channel_multiplier=1))
            n = step.mark(nc.gpsimd.iota(kpos_i[:], pattern=[[1, SEQ]], base=0, channel_multiplier=0))
            pool.wait_ge(pool_step, n)
            step.mark(nc.gpsimd.tensor_copy(qpos[:], qpos_i[:]))
            n = step.mark(nc.gpsimd.tensor_copy(kpos[:], kpos_i[:]))
            pool.wait_ge(norm_loaded, 48)
            n = step.mark(nc.gpsimd.tensor_scalar(gw_half[:], norm_w[:, 1, :], 0.5, None, ALU.mult))
            pool.wait_ge(pool_step, n)

            def root(t, g):
                pool.wait_ge(var_ready[t], g + 1)
                nc.gpsimd.tensor_tensor(stat[t]["root"][:], stat[t]["var"][:], half[:], ALU.pow).then_inc(root_ready[t], 1)

            def inverse_root(k, g):
                pool.wait_ge(ln_var[k], g + 1)
                nc.gpsimd.tensor_tensor(rstd[k][:], lnv[k][:], minus_half[:], ALU.pow).then_inc(ln_rstd[k], 1)

            for g in range(BATCH):
                root("in", g)
                pool.wait_ge(pad_loaded, 16 * (g + 1))
                if g:
                    pool.wait_ge(sc_ready, TILES * g)
                n = step.mark(nc.gpsimd.tensor_copy(pad_f[:], pad_i[:]))
                pool.wait_ge(pool_step, n)
                n = step.mark(nc.gpsimd.tensor_scalar(qneg[:], qpos[:], pad_f[:], NEG / SCALE, ALU.is_ge, ALU.mult))
                pool.wait_ge(pool_step, n)
                for j in range(TILES):
                    nc.gpsimd.tensor_scalar(negmask[:, j, :], kpos[:], pad_f[:], qneg[:, j:j + 1],
                                            ALU.is_ge, ALU.mult).then_inc(mask_ready, 1)
                pool.wait_ge(sg_ready, g + 1)
                nc.gpsimd.tensor_tensor(gain[:], sg2[:], gw_half[:].unsqueeze(1).to_broadcast([P, TILES, D]),
                                        ALU.mult).then_inc(gain_ready, 1)
                root("out", g)
                pool.wait_ge(res_ready, TILES * (g + 1))
                nc.gpsimd.tensor_tensor(xres[:], res[:], xt[:], ALU.add).then_inc(xres_ready, 1)
                root("mlp", g)
                root("z", g)
                inverse_root(0, g)
                pool.wait_ge(x1_ready, TILES * (g + 1))
                nc.gpsimd.tensor_tensor(x1b[:], x1[:], xb_bias[:].unsqueeze(1).to_broadcast([P, TILES, D]),
                                        ALU.add).then_inc(x1b_ready, 1)
                inverse_root(1, g)
                inverse_root(2, g)

        @block.scalar
        def _(act):
            step = Steps(act_step)
            act.dma_start(pad_i[:], pads[0:1].partition_broadcast(P)).then_inc(pad_loaded, 16)
            act.dma_start(ctx[:], tiles_of(ctx_mem, 0)).then_inc(ctx_loaded, 16)
            act.dma_start(lb[:], lower_bound.rearrange("(p a) -> p a", a=1)).then_inc(small_loaded, 16)
            act.dma_start(xb_bias[:], xattn_b.partition_broadcast(P)).then_inc(small_loaded, 16)
            act.dma_start(br_bc[:], br.partition_broadcast(P)).then_inc(small_loaded, 16)
            act.dma_start(xw_raw[:], xattn_w).then_inc(small_loaded, 16)
            act.dma_start(wr_sb[:], wr).then_inc(small_loaded, 16)
            act.dma_start(b2_sb[:], b2).then_inc(small_loaded, 16)
            act.dma_start(b1_rows[:], b1.rearrange("e (c p) -> (e c) p", p=P)).then_inc(small_loaded, 16)

            act.wait_ge(wscale_ready, 2)
            for k in range(4):
                nc.scalar.activation(wmagic[:, k * D:(k + 1) * D], wraw[:, k * D:(k + 1) * D], ACT.Identity,
                                     bias=round_up[:], scale=wscale[:, k:k + 1]).then_inc(wmagic_ready, 1)
            a, b = 4 * D, 4 * D + GATE_BLOCKS * D
            nc.scalar.activation(wmagic[:, a:b], wraw[:, a:b], ACT.Identity, bias=round_up[:],
                                 scale=wscale[:, 4:5]).then_inc(wmagic_ready, 1)
            nc.scalar.activation(wmagic[:, b:WCOLS], wraw[:, b:WCOLS], ACT.Identity, bias=round_up[:],
                                 scale=wscale[:, 5:6]).then_inc(wmagic_ready, 1)

            def square_sums(t, g, source, into, slot, width):
                for j in range(TILES):
                    nc.scalar.activation(junk[:, slot + j, 0:width], source[:, j, :], ACT.Square,
                                         accum_out=stat[t][into][:, j:j + 1]).then_inc(squares[t], 1)

            def strip_round(t, g, width=SEQ):
                act.wait_ge(qT_ready[t], g + 1)
                nc.scalar.activation(qT[t][:], T[:, 0:width], ACT.Identity, bias=round_down[:]).then_inc(qT_moved[t], 1)

            for g in range(BATCH):
                act.wait_ge(x_loaded, 16 * (g + 1))
                if g:
                    act.wait_ge(squares["z"], TILES * g)
                square_sums("in", g, xt, "ssx", 0, D)
                act.wait_ge(u_ready["in"], g + 1)
                square_sums("in", g, u_in, "ssu", 2, D)
                strip_round("in", g)
                act.wait_ge(ifg_ready, g + 1)
                nc.scalar.activation(th[:], ifg[:], ACT.Tanh, scale=0.5).then_inc(th_ready, 1)
                act.wait_ge(ctx_loaded, 16 * (g + 1))
                act.wait_ge(ctxT_ready, g + 1)
                nc.scalar.activation(ctx_T[:], M[:, 1, 0:SEQ], ACT.Copy).then_inc(ctxT_moved, 1)
                act.wait_ge(o_ready, g + 1)
                for j in range(TILES):
                    nc.scalar.activation(junk[:, 4 + j, 0:D], M[:, 0, j * D:(j + 1) * D], ACT.Square,
                                         accum_out=stat["out"]["ssx"][:, j:j + 1]).then_inc(squares["out"], 1)
                act.wait_ge(u_ready["out"], g + 1)
                square_sums("out", g, u_out, "ssu", 6, D)
                strip_round("out", g)
                act.wait_ge(res_ready, TILES * (g + 1))
                square_sums("mlp", g, res, "ssx", 8, D)
                act.wait_ge(u_ready["mlp"], g + 1)
                square_sums("mlp", g, u_mlp, "ssu", 10, D)
                strip_round("mlp", g)
                act.wait_ge(deqh_ready, g + 1)
                for j in range(TILES):
                    act.wait_ge(gate_done, 2 * (TILES * g + j) + 1)
                    nc.scalar.activation(zt[:, j, :], M[:, 0, 0:INNER], ACT.Tanh,
                                         scale=deqh[:, j:j + 1]).then_inc(zt_ready, 1)
                for j in range(TILES):
                    act.wait_ge(z_ready, TILES * g + j + 1)
                    nc.scalar.activation(junk[:, 12 + j, :], z[:, j, :], ACT.Square,
                                         accum_out=stat["z"]["ssu"][:, j:j + 1]).then_inc(squares["z"], 1)
                for j in range(TILES):
                    act.wait_ge(qT_ready["z"], TILES * g + j + 1)
                    for c, rows in DOWN:
                        nc.scalar.activation(qT_z[0:rows, j, c, :], T[0:rows, c * P:(c + 1) * P], ACT.Identity,
                                             bias=round_down[0:rows, :]).then_inc(qT_moved["z"], 1)
                act.wait_ge(x1T_ready, g + 1)
                nc.scalar.activation(x1_T[:], T[:, 0:SEQ], ACT.Copy).then_inc(x1T_moved, 1)
                for j in range(TILES):
                    act.wait_ge(sc_ready, TILES * g + j + 1)
                    nc.scalar.activation(prob[:, j, :], sc[:, j, :], ACT.Exp, bias=negmax[:, j:j + 1], scale=-1.0,
                                         accum_out=psum_row[:, j:j + 1]).then_inc(prob_ready, 1)
                act.wait_ge(probT_ready, g + 1)
                nc.scalar.activation(prob_T[:], T[:].rearrange("p (t q) -> p t q", t=TILES), ACT.Copy).then_inc(probT_moved, 1)
                act.wait_ge(att_done, g + 1)
                nc.scalar.activation(att_T[:], M[:, 0, 0:SEQ], ACT.Copy).then_inc(attT_moved, 1)
                act.wait_ge(x2T_ready, g + 1)
                nc.scalar.activation(x2_T[:], T[:, 0:SEQ], ACT.Copy).then_inc(x2T_moved, 1)
                act.wait_ge(negtop_ready, g + 1)
                for j in range(TILES):
                    nc.scalar.activation(eg[:, j, :], lg[:, j, :], ACT.Exp, bias=negtop[:, j:j + 1]).then_inc(eg_ready, 1)
                for e in range(EXPERTS):
                    n = g * EXPERTS + e
                    if n >= 2:
                        act.wait_ge(fc2_done, n - 1)
                    for c in range(CHUNKS):
                        if c % 2 == 0:
                            act.wait_ge(fc1_done, 2 * n + c // 2 + 1)
                        nc.scalar.activation(hid[:, e % 2, c, :], H[:, e % 2, c, :], ACT.Gelu,
                                             bias=b1_T[:, e * CHUNKS + c:e * CHUNKS + c + 1]).then_inc(gelu_done, 1)
                if g + 1 < BATCH:
                    act.wait_ge(mask_ready, TILES * (g + 1))
                    act.dma_start(pad_i[:], pads[g + 1:g + 2].partition_broadcast(P)).then_inc(pad_loaded, 16)
                    act.wait_ge(att_done, g + 1)
                    act.dma_start(ctx[:], tiles_of(ctx_mem, g + 1)).then_inc(ctx_loaded, 16)

        @block.vector
        def _(dve):
            step = Steps(vec_step)
            v = nc.vector
            v.memset(round_up[:], ROUND)
            v.memset(round_down[:], -ROUND)

            def prepare_weights():
                dve.wait_ge(wattn_loaded, 64)
                v.tensor_reduce(wabs[:, 0:4], attn_raw, AX, ALU.add, apply_absolute_value=True).then_inc(wabs_ready, 1)
                dve.wait_ge(wgate_loaded, 32)
                v.tensor_reduce(wabs[:, 4:5], gate_raw, AXY, ALU.add, apply_absolute_value=True).then_inc(wabs_ready, 1)
                dve.wait_ge(wdown_loaded, 16)
                v.tensor_reduce(wabs[:, 5:6], down_raw, AX, ALU.add, apply_absolute_value=True).then_inc(wabs_ready, 1)
                dve.wait_ge(wtot_ready, 1)
                step.mark(v.tensor_scalar(wmean[:, 0:4], M[:, 0, 0:4], 1.0 / (D * D), CLIP, ALU.mult, ALU.max))
                n = step.mark(v.tensor_scalar(wmean[:, 4:6], M[:, 0, 4:6], 1.0 / (D * INNER), CLIP, ALU.mult, ALU.bypass))
                dve.wait_ge(vec_step, n)
                n = step.mark(v.tensor_scalar(wmean[:, 4:5], wmean[:, 4:5], 0.5, CLIP, ALU.mult, ALU.max))
                n = step.mark(v.tensor_scalar(wmean[:, 5:6], wmean[:, 5:6], CLIP, None, ALU.max))
                dve.wait_ge(vec_step, n)
                v.reciprocal(wscale[:], wmean[:]).then_inc(wscale_ready, 1)
                dve.wait_ge(small_loaded, 16 * 7)
                n = step.mark(v.tensor_scalar(f_gain[:], lb[:], -0.5, 0.5, ALU.mult, ALU.add))
                dve.wait_ge(vec_step, n)
                v.tensor_scalar(f_base[:], lb[:], f_gain[:], None, ALU.add).then_inc(wscale_ready, 1)
                for k in range(6):
                    a, b = [(0, D), (D, 2 * D), (2 * D, 3 * D), (3 * D, 4 * D), (4 * D, 4 * D + GATE_BLOCKS * D),
                            (4 * D + GATE_BLOCKS * D, WCOLS)][k]
                    dve.wait_ge(wmagic_ready, k + 1)
                    v.tensor_scalar(wmagic[:, a:b], wmagic[:, a:b], ROUND + 1.0, ROUND - 1.0,
                                    ALU.min, ALU.max).then_inc(wclip_ready, 1)
                dve.wait_ge(wT_ready, 1)
                v.tensor_scalar(attn_T[:], T[:], -ROUND, None, ALU.add).then_inc(wT_moved, 1)
                dve.wait_ge(wT_ready, 2)
                v.tensor_scalar(gate_T[:, 0:512], M[:, 1, :], -ROUND, None, ALU.add).then_inc(wT_moved, 1)
                dve.wait_ge(wT_ready, 3)
                v.tensor_scalar(gate_T[:, 512:GATE_ROWS], T[:, 0:GATE_ROWS - 512], -ROUND, None, ALU.add).then_inc(wT_moved, 1)
                dve.wait_ge(wT_ready, 4)
                for c, rows in DOWN:
                    last = v.tensor_scalar(down_T[0:rows, c, :], M[0:rows, 1, c * D:(c + 1) * D], -ROUND, None, ALU.add)
                last.then_inc(wT_moved, 1)
                dve.wait_ge(wT_ready, 5)
                v.tensor_copy(xw_T[:], T[:, 0:D])
                v.tensor_copy(b1_T[:], T[:, D:D + EXPERTS * CHUNKS]).then_inc(wT_moved, 1)

            def peak(t, source):
                return step.mark(v.tensor_reduce(stat[t]["peak"][:], source, AX, ALU.max, apply_absolute_value=True))

            def quantise(t, g, u, width, peak_step, double):
                s = stat[t]
                dve.wait_ge(vec_step, peak_step)
                step.mark(v.tensor_scalar(s["peakq"][:], s["peak"][:], 1.0 / QMAX, None, ALU.mult))
                dve.wait_ge(squares[t], (4 if double else 2) * (g + 1))
                if double:
                    n = step.mark(v.tensor_scalar(s["tail"][:], s["ssx"][:], EPS / D, EPS * EPS, ALU.mult, ALU.add))
                    dve.wait_ge(vec_step, n)
                    v.scalar_tensor_tensor(s["var"][:], s["ssu"][:], 1.0 / D, s["tail"][:], ALU.mult,
                                           ALU.add).then_inc(var_ready[t], 1)
                else:
                    v.tensor_scalar(s["var"][:], s["ssu"][:], 1.0 / width, EPS, ALU.mult, ALU.add).then_inc(var_ready[t], 1)
                dve.wait_ge(root_ready[t], g + 1)
                n = step.mark(v.scalar_tensor_tensor(s["step"][:], s["root"][:], CLIP / QMAX, s["peakq"][:], ALU.mult, ALU.max))
                m = step.mark(v.reciprocal(s["rroot"][:], s["root"][:]))
                dve.wait_ge(vec_step, n)
                n = step.mark(v.reciprocal(s["inv"][:], s["step"][:]))
                dve.wait_ge(vec_step, n)
                for j in range(TILES):
                    v.tensor_scalar(q[t][:, j, :], u[:, j, :], s["inv"][:, j:j + 1], ROUND, ALU.mult,
                                    ALU.add).then_inc(q_ready[t], 1)
                return step.mark(v.tensor_tensor(s["deq"][:], s["step"][:], s["rroot"][:], ALU.mult))

            def layernorm(k, g, source, into, ready, per):
                dve.wait_ge(vec_step, ready)
                for j in range(TILES):
                    n = step.mark(v.bn_stats(bn[k][:, j, :], source[:, j, :]))
                dve.wait_ge(vec_step, n)
                for j in range(TILES):
                    n = step.mark(v.bn_aggr(mv[k][:, j, :], bn[k][:, j, :]))
                dve.wait_ge(vec_step, n)
                v.tensor_scalar(lnv[k][:], mv[k][:, :, 1], LN_EPS, None, ALU.add).then_inc(ln_var[k], 1)
                dve.wait_ge(ln_rstd[k], g + 1)
                for j in range(TILES):
                    v.tensor_scalar(into[:, j, :], source[:, j, :], mv[k][:, j, 0:1], rstd[k][:, j:j + 1],
                                    ALU.subtract, ALU.mult).then_inc(per, 1)

            for g in range(BATCH):
                dve.wait_ge(x_loaded, 16 * (g + 1))
                if g == 0:
                    dve.wait_ge(norm_loaded, 48)
                v.tensor_tensor(u_in[:], xt[:], norm_w[:, 0, :].unsqueeze(1).to_broadcast([P, TILES, D]),
                                ALU.mult).then_inc(u_ready["in"], 1)
                dve.wait_ge(u_ready["in"], g + 1)
                n = peak("in", u_in[:])
                if g == 0:
                    prepare_weights()
                n = quantise("in", g, u_in, D, n, True)
                dve.wait_ge(vec_step, n)
                for k in range(3):
                    n = step.mark(v.tensor_scalar(deq3[:, :, k], stat["in"]["deq"][:], wmean[:, k:k + 1], None, ALU.mult))
                dve.wait_ge(vec_step, n)
                dve.wait_ge(ifg_done, g + 1)
                v.tensor_tensor(ifg[:], M[:, :, 0:3 * D].rearrange("p j (k d) -> p j k d", k=3),
                                deq3[:].unsqueeze(3).to_broadcast([P, TILES, 3, D]), ALU.mult).then_inc(ifg_ready, 1)
                dve.wait_ge(th_ready, g + 1)
                v.scalar_tensor_tensor(si2[:], th[:, :, 0, :], 1.0, ifg[:, :, 0, :], ALU.add, ALU.mult).then_inc(si_ready, 1)
                v.scalar_tensor_tensor(sg2[:], th[:, :, 2, :], 1.0, ifg[:, :, 2, :], ALU.add, ALU.mult).then_inc(sg_ready, 1)
                dve.wait_ge(if_T_ready, g + 1)
                n = step.mark(v.tensor_scalar(f_T[:], T[:, SEQ:2 * SEQ], f_gain[:], f_base[:], ALU.mult, ALU.add))
                dve.wait_ge(vec_step, n)
                n = step.mark(v.tensor_scalar(omf_T[:], f_T[:], -0.5, 0.5, ALU.mult, ALU.add))
                dve.wait_ge(vec_step, n)
                v.tensor_tensor(i_T[:], T[:, 0:SEQ], omf_T[:], ALU.mult).then_inc(if_T_read, 1)
                dve.wait_ge(if_T_read, g + 1)
                v.tensor_tensor_scan(o_T[:], f_T[:], i_T[:], 0.0, ALU.mult, ALU.add).then_inc(scan_done, 1)
                dve.wait_ge(squares["out"], 4 * g + 2)
                dve.wait_ge(gain_ready, g + 1)
                v.tensor_tensor(u_out[:], M[:, 0, 0:SEQ].rearrange("p (j d) -> p j d", j=TILES), gain[:],
                                ALU.mult).then_inc(u_ready["out"], 1)
                dve.wait_ge(u_ready["out"], g + 1)
                n = peak("out", u_out[:])
                n = quantise("out", g, u_out, D, n, True)
                dve.wait_ge(vec_step, n)
                n = step.mark(v.tensor_scalar(stat["out"]["deq"][:], stat["out"]["deq"][:], wmean[:, 3:4], None, ALU.mult))
                dve.wait_ge(vec_step, n)
                dve.wait_ge(wo_done, g + 1)
                for j in range(TILES):
                    v.scalar_tensor_tensor(res[:, j, :], M[:, 1, j * D:(j + 1) * D], stat["out"]["deq"][:, j:j + 1],
                                           xt[:, j, :], ALU.mult, ALU.add).then_inc(res_ready, 1)
                dve.wait_ge(res_ready, TILES * (g + 1))
                v.tensor_tensor(u_mlp[:], res[:], norm_w[:, 2, :].unsqueeze(1).to_broadcast([P, TILES, D]),
                                ALU.mult).then_inc(u_ready["mlp"], 1)
                dve.wait_ge(u_ready["mlp"], g + 1)
                n = peak("mlp", u_mlp[:])
                n = quantise("mlp", g, u_mlp, D, n, True)
                dve.wait_ge(vec_step, n)
                n = step.mark(v.tensor_scalar(deqg[:], stat["mlp"]["deq"][:], wmean[:, 4:5], None, ALU.mult))
                dve.wait_ge(vec_step, n)
                v.tensor_scalar(deqh[:], deqg[:], 0.5, None, ALU.mult).then_inc(deqh_ready, 1)
                dve.wait_ge(deqh_ready, g + 1)
                n = step.mark(v.tensor_tensor(deqg[:], deqg[:], deqh[:], ALU.mult))
                for j in range(TILES):
                    dve.wait_ge(zt_ready, TILES * g + j + 1)
                    k = step.mark(v.scalar_tensor_tensor(za[:, j, :], zt[:, j, :], 1.0, M[:, 0, 0:INNER], ALU.add, ALU.mult))
                    dve.wait_ge(vec_step, k)
                    dve.wait_ge(gate_done, 2 * (TILES * g + j) + 2)
                    v.scalar_tensor_tensor(z[:, j, :], M[:, 1, 0:INNER], deqg[:, j:j + 1], za[:, j, :], ALU.mult,
                                           ALU.mult).then_inc(z_ready, 1)
                dve.wait_ge(z_ready, TILES * (g + 1))
                n = peak("z", z[:])
                n = quantise("z", g, z, INNER, n, False)
                dve.wait_ge(vec_step, n)
                n = step.mark(v.tensor_scalar(stat["z"]["deq"][:], stat["z"]["deq"][:], wmean[:, 5:6], None, ALU.mult))
                dve.wait_ge(vec_step, n)
                dve.wait_ge(xres_ready, g + 1)
                dve.wait_ge(down_done, g + 1)
                for j in range(TILES):
                    n = step.mark(v.scalar_tensor_tensor(pre[0][:, j, :], M[:, 0, j * D:(j + 1) * D],
                                                         stat["z"]["deq"][:, j:j + 1], xres[:, j, :], ALU.mult, ALU.add))
                layernorm(0, g, pre[0], x1, n, x1_ready)
                for j in range(TILES):
                    dve.wait_ge(mask_ready, TILES * g + j + 1)
                    dve.wait_ge(scores_done, TILES * g + j + 1)
                    v.tensor_tensor_reduce(out=sc[:, j, :], in0=M[:, j, 0:SEQ], in1=negmask[:, j, :], scale=-SCALE,
                                           scalar=3.0e38, op0=ALU.add, op1=ALU.min,
                                           accum_out=negmax[:, j:j + 1]).then_inc(sc_ready, 1)
                dve.wait_ge(prob_ready, TILES * (g + 1))
                n = step.mark(v.reciprocal(rsum[:], psum_row[:]))
                dve.wait_ge(vec_step, n)
                dve.wait_ge(x1b_ready, g + 1)
                dve.wait_ge(proj_done, g + 1)
                for j in range(TILES):
                    n = step.mark(v.scalar_tensor_tensor(pre[1][:, j, :], M[:, 1, j * D:(j + 1) * D], rsum[:, j:j + 1],
                                                         x1b[:, j, :], ALU.mult, ALU.add))
                if g:
                    dve.wait_ge(combined, TILES * EXPERTS * g)
                layernorm(1, g, pre[1], x2, n, x2_ready)
                dve.wait_ge(logits_done, g + 1)
                v.tensor_tensor(lg[:], M[:, 0, 0:TILES * EXPERTS].rearrange("p (j e) -> p j e", j=TILES),
                                br_bc[:].unsqueeze(1).to_broadcast([P, TILES, EXPERTS]), ALU.add).then_inc(logits_moved, 1)
                dve.wait_ge(logits_moved, g + 1)
                for j in range(TILES):
                    n = step.mark(v.max(top[:, j, :], lg[:, j, :]))
                dve.wait_ge(vec_step, n)
                v.tensor_scalar(negtop[:], top[:, :, 0], -1.0, None, ALU.mult).then_inc(negtop_ready, 1)
                for j in range(TILES):
                    dve.wait_ge(eg_ready, TILES * g + j + 1)
                    n = step.mark(v.scalar_tensor_tensor(em[:, j, :], lg[:, j, :], top[:, j, 1:2], eg[:, j, :],
                                                         ALU.is_ge, ALU.mult, accum_out=esum[:, j:j + 1]))
                dve.wait_ge(vec_step, n)
                n = step.mark(v.reciprocal(ersum[:], esum[:]))
                dve.wait_ge(vec_step, n)
                for j in range(TILES):
                    v.tensor_scalar(gate_w[:, j, :], em[:, j, :], ersum[:, j:j + 1], None, ALU.mult).then_inc(gatew_ready, 1)
                dve.wait_ge(gwT_ready, g + 1)
                v.tensor_copy(gate_wT[:], M[0:EXPERTS, 1, 0:SEQ]).then_inc(gwT_moved, 1)
                dve.wait_ge(x2_ready, TILES * (g + 1))
                dve.wait_ge(b2_done, g + 1)
                v.tensor_tensor(acc[:], M[:, 0, 0:SEQ].rearrange("p (j d) -> p j d", j=TILES), x2[:],
                                ALU.add).then_inc(acc_started, 1)
                dve.wait_ge(acc_started, g + 1)
                for e in range(EXPERTS):
                    n = g * EXPERTS + e
                    dve.wait_ge(fc2_done, n + 1)
                    for j in range(TILES):
                        if e:
                            dve.wait_ge(combined, TILES * (n - 1) + j + 1)
                        v.scalar_tensor_tensor(acc[:, j, :], Y[:, j, :], gate_w[:, j, e:e + 1], acc[:, j, :],
                                               ALU.mult, ALU.add).then_inc(combined, 1)
                dve.wait_ge(combined, TILES * EXPERTS * (g + 1))
                if g:
                    dve.wait_ge(stored, 16 * g)
                layernorm(2, g, acc, yout, step.count, out_ready)

        @block.tensor
        def _(pe):
            t_ = nc.tensor
            pe.wait_ge(ident_ready, 1)
            pe.wait_ge(ones_ready, 1)
            pe.wait_ge(wabs_ready, 3)
            t_.matmul(M[:, 0, 0:6], ones[:], wabs[:], start=True, stop=True).then_inc(wtot_ready, 1)
            for k in range(4):
                pe.wait_ge(wclip_ready, k + 1)
                last = t_.transpose(T[:, k * D:(k + 1) * D], wmagic[:, k * D:(k + 1) * D], ident[:])
            last.then_inc(wT_ready, 1)
            pe.wait_ge(wclip_ready, 6)
            gate_m = wmagic[:, 4 * D:4 * D + GATE_BLOCKS * D]
            for k in range(4):
                last = t_.transpose(M[:, 1, k * P:(k + 1) * P], gate_m[:, k * D:(k + 1) * D], ident[:])
            last.then_inc(wT_ready, 1)
            pe.wait_ge(wT_moved, 1)
            t_.transpose(T[:, 0:P], gate_m[:, 4 * D:5 * D], ident[:])
            t_.transpose(T[:, P:P + GATE_TAIL], gate_m[0:GATE_TAIL, 5 * D:6 * D],
                         ident[0:GATE_TAIL, 0:GATE_TAIL]).then_inc(wT_ready, 1)
            pe.wait_ge(wT_moved, 2)
            down_m = wmagic[:, 4 * D + GATE_BLOCKS * D:WCOLS]
            for c, rows in DOWN:
                last = t_.transpose(M[0:rows, 1, c * D:(c + 1) * D], down_m[:, c * P:c * P + rows], ident[:])
            last.then_inc(wT_ready, 1)
            pe.wait_ge(wT_moved, 3)
            pe.wait_ge(small_loaded, 16 * 7)
            t_.transpose(T[:, 0:D], xw_raw[:], ident[:])
            t_.transpose(T[:, D:D + EXPERTS * CHUNKS], b1_rows[:],
                         ident[0:EXPERTS * CHUNKS, 0:EXPERTS * CHUNKS]).then_inc(wT_ready, 1)
            pe.wait_ge(wT_moved, 5)

            def transpose_tiles(bank, source):
                for j in range(TILES):
                    last = t_.transpose(bank[:, j * P:(j + 1) * P], source[:, j, :], ident[:])
                return last

            def fc1(g, e):
                n = g * EXPERTS + e
                if g == 0:
                    pe.wait_ge(w1_loaded[e], 16)
                for c in range(CHUNKS):
                    if n >= 2 and c % 2 == 0:
                        pe.wait_ge(gelu_done, CHUNKS * (n - 2) + c + 2)
                    last = t_.matmul(H[:, e % 2, c, :], w1_sb[:, e, c * P:(c + 1) * P], x2_T[:], start=True, stop=True)
                    if c % 2:
                        last.then_inc(fc1_done, 1)

            def fc2(g, e):
                n = g * EXPERTS + e
                if g == 0:
                    pe.wait_ge(w2_loaded[e], 16)
                if n:
                    pe.wait_ge(combined, TILES * n)
                pe.wait_ge(gelu_done, CHUNKS * (n + 1))
                for j in range(TILES):
                    for c in range(CHUNKS):
                        last = t_.matmul(Y[:, j, :], hid[:, e % 2, c, j * P:(j + 1) * P], w2_sb[:, e, c, :],
                                         start=(c == 0), stop=(c == CHUNKS - 1))
                last.then_inc(fc2_done, 1)

            for g in range(BATCH):
                pe.wait_ge(q_ready["in"], TILES * (g + 1))
                transpose_tiles(T, q["in"]).then_inc(qT_ready["in"], 1)
                pe.wait_ge(qT_moved["in"], g + 1)
                for j in range(TILES):
                    last = t_.matmul(M[:, j, 0:3 * D], qT["in"][:, j * P:(j + 1) * P], attn_T[:, 0:3 * D], start=True, stop=True)
                last.then_inc(ifg_done, 1)
                pe.wait_ge(ctx_loaded, 16 * (g + 1))
                pe.wait_ge(ifg_ready, g + 1)
                transpose_tiles(M[:, 1, :], ctx).then_inc(ctxT_ready, 1)
                pe.wait_ge(si_ready, g + 1)
                transpose_tiles(T, si2)
                transpose_tiles(T[:, SEQ:2 * SEQ], th[:, :, 1, :]).then_inc(if_T_ready, 1)
                pe.wait_ge(scan_done, g + 1)
                for j in range(TILES):
                    last = t_.transpose(M[:, 0, j * P:(j + 1) * P], o_T[:, j * P:(j + 1) * P], ident[:])
                last.then_inc(o_ready, 1)
                pe.wait_ge(q_ready["out"], TILES * (g + 1))
                transpose_tiles(T, q["out"]).then_inc(qT_ready["out"], 1)
                pe.wait_ge(qT_moved["out"], g + 1)
                pe.wait_ge(ctxT_moved, g + 1)
                for j in range(TILES):
                    last = t_.matmul(M[:, 1, j * D:(j + 1) * D], qT["out"][:, j * P:(j + 1) * P], attn_T[:, 3 * D:4 * D],
                                     start=True, stop=True)
                last.then_inc(wo_done, 1)
                pe.wait_ge(q_ready["mlp"], TILES * (g + 1))
                transpose_tiles(T, q["mlp"]).then_inc(qT_ready["mlp"], 1)
                pe.wait_ge(qT_moved["mlp"], g + 1)
                for j in range(TILES):
                    if j:
                        pe.wait_ge(z_ready, TILES * g + j)
                    t_.matmul(M[:, 0, 0:INNER], qT["mlp"][:, j * P:(j + 1) * P], gate_T[:, 0:INNER],
                              start=True, stop=True).then_inc(gate_done, 1)
                    t_.matmul(M[:, 1, 0:INNER], qT["mlp"][:, j * P:(j + 1) * P], gate_T[:, INNER:GATE_ROWS],
                              start=True, stop=True).then_inc(gate_done, 1)
                for j in range(TILES):
                    pe.wait_ge(q_ready["z"], TILES * g + j + 1)
                    if j:
                        pe.wait_ge(qT_moved["z"], len(DOWN) * (TILES * g + j))
                    for c, rows in DOWN:
                        last = t_.transpose(T[0:rows, c * P:(c + 1) * P], q["z"][:, j, c * P:c * P + rows], ident[:])
                    last.then_inc(qT_ready["z"], 1)
                for j in range(TILES):
                    pe.wait_ge(qT_moved["z"], len(DOWN) * (TILES * g + j + 1))
                    for c, rows in DOWN:
                        last = t_.matmul(M[:, 0, j * D:(j + 1) * D], qT_z[0:rows, j, c, :], down_T[0:rows, c, :],
                                         start=(c == 0), stop=(c == len(DOWN) - 1))
                last.then_inc(down_done, 1)
                pe.wait_ge(x1_ready, TILES * (g + 1))
                transpose_tiles(T, x1).then_inc(x1T_ready, 1)
                pe.wait_ge(x1T_moved, g + 1)
                for j in range(TILES):
                    t_.matmul(M[:, j, 0:SEQ], x1_T[:, j * P:(j + 1) * P], ctx_T[:], start=True, stop=True).then_inc(scores_done, 1)
                for j in range(TILES):
                    pe.wait_ge(prob_ready, TILES * g + j + 1)
                    for k in range(TILES):
                        last = t_.transpose(T[:, k * SEQ + j * P:k * SEQ + (j + 1) * P], prob[:, j, k * P:(k + 1) * P], ident[:])
                last.then_inc(probT_ready, 1)
                pe.wait_ge(probT_moved, g + 1)
                for k in range(TILES):
                    last = t_.matmul(M[:, 0, 0:SEQ], ctx[:, k, :], prob_T[:, k, :], start=(k == 0), stop=(k == TILES - 1))
                last.then_inc(att_done, 1)
                pe.wait_ge(attT_moved, g + 1)
                for j in range(TILES):
                    last = t_.matmul(M[:, 1, j * D:(j + 1) * D], att_T[:, j * P:(j + 1) * P], xw_T[:], start=True, stop=True)
                last.then_inc(proj_done, 1)
                pe.wait_ge(x2_ready, TILES * (g + 1))
                transpose_tiles(T, x2).then_inc(x2T_ready, 1)
                pe.wait_ge(x2T_moved, g + 1)
                for j in range(TILES):
                    last = t_.matmul(M[:, 0, j * EXPERTS:(j + 1) * EXPERTS], x2_T[:, j * P:(j + 1) * P], wr_sb[:],
                                     start=True, stop=True)
                last.then_inc(logits_done, 1)
                fc1(g, 0)
                pe.wait_ge(gatew_ready, TILES * (g + 1))
                for j in range(TILES):
                    last = t_.transpose(M[0:EXPERTS, 1, j * P:(j + 1) * P], gate_w[:, j, :], ident[:])
                last.then_inc(gwT_ready, 1)
                pe.wait_ge(gwT_moved, g + 1)
                for j in range(TILES):
                    last = t_.matmul(M[:, 0, j * D:(j + 1) * D], gate_wT[:, j * P:(j + 1) * P], b2_sb[:], start=True, stop=True)
                last.then_inc(b2_done, 1)
                for e in range(EXPERTS):
                    if e + 1 < EXPERTS:
                        fc1(g, e + 1)
                    fc2(g, e)


_NAMES = ["x", "ctx_1024", "_lenS2", "L0_attn_lower_bound", "L0_attn_attn_norm_w", "L0_attn_w_i", "L0_attn_w_f",
          "L0_attn_w_g", "L0_attn_g_norm_w", "L0_attn_w_o", "L0_attn_mlp_norm_w", "L0_attn_w_gate",
          "L0_attn_w_down", "L0_xattn_W", "L0_xattn_b", "L0_ffn_W1", "L0_ffn_b1", "L0_ffn_W2", "L0_ffn_b2",
          "L0_ffn_Wr", "L0_ffn_br"]


def kernel(**inputs):
    import numpy as np
    import concourse.bacc as bacc
    from concourse.bass_utils import run_bass_kernel_spmd

    nc = bacc.Bacc("TRN2", target_bir_lowering=False, num_devices=1)
    arrays, args = {}, []
    for name in _NAMES:
        a = np.ascontiguousarray(inputs[name])
        arrays[f"in_{name}"] = a
        args.append(nc.dram_tensor(f"in_{name}", a.shape, mybir.dt.from_np(a.dtype), kind="ExternalInput").ap())
    out = nc.dram_tensor("out", (BATCH, SEQ, D), mybir.dt.float32, kind="ExternalOutput")
    decoder_layer(nc, *args, out.ap())
    result = run_bass_kernel_spmd(nc, [arrays], core_ids=[0])
    return result.results[0]["out"]
```

```python
import concourse.bass as bass
from concourse import mybir
from contextlib import ExitStack

BATCH, SEQ, D = 4, 256, 128
P = 128
TILES = SEQ // P
INNER = 352
EXPERTS, HIDDEN = 8, 512
CHUNKS = HIDDEN // P
BITLINEAR = ("w_i", "w_f", "w_g", "w_o")
EPS = 1e-6
LN_EPS = 1e-5
CLIP = 1e-5
QMAX = 127.0
ROUND = 1.5 * 2.0 ** 23
SCALE = float(D) ** -0.5
NEG = -1e13


PAIR, PAIRS, HBANKS, YBANKS = 2, BATCH // 2, 2, 2
WLOAD = 2
PT = PAIR * TILES
TERNARY = ((0, 1, 2, 3), (4, 5))
X_UP = 2.0 ** 11
W_TARGET = 2.0 ** 13
FC2_LAG, GELU_LAG, HIGH_LAG, LOW_LAG = 7, 1, 2, 3
STAGES = ("ctx", "in_u", "in_var", "in_q", "in_deq", "if", "sigmoids", "g", "scan", "gain", "o", "out_var", "out_q",
          "res", "mlp_var", "mlp_q", "gate0", "gate1", "zsq0", "gate2", "zsq1", "gate3", "zsq2", "zsq3", "z_var",
          "z_q0", "z_q1", "z_q2", "z_q3", "down", "x1", "scores", "softmax", "turn", "attend", "ln2", "x2", "x2_lo",
          "router", "weigh", "turn_gates", "bias2")


def hi_on_act(k, e, c):
    return k == 1


def lo_on_pool(k, e, c):
    return k == 0 or c % 2 == 0


def hi_counts(n):
    made = [hi_on_act(m // CHUNKS // EXPERTS, m // CHUNKS % EXPERTS, m % CHUNKS) for m in range(n + 1)]
    return sum(made), len(made) - sum(made), made[-1]


def lo_counts(n):
    made = [lo_on_pool(m // CHUNKS // EXPERTS, m // CHUNKS % EXPERTS, m % CHUNKS) for m in range(n + 1)]
    return sum(made), len(made) - sum(made), made[-1]


ORDER = {
    "PE": """
        ctx:0 means:0 ctx:1 means:1 turn_w:0 in_q:0 in_deq:0 turn_w:1 if:0 g:0 turn_small in_q:1 in_deq:1 o:0 if:1
        g:1 o:1 out_q:0 res:0 out_q:1 sum_w res:1 mlp_q:0 gate0:0 gate1:0 gate2:0 mlp_q:1 gate3:0 gate0:1 gate1:1
        gate2:1 gate3:1 z_q0:0 z_q1:0 z_q2:0 z_q3:0 down:0 z_q0:1 z_q1:1 z_q2:1 z_q3:1 x1:0 down:1 scores:0 turn:0
        attend:0 x1:1 ln2:0 scores:1 turn:1 attend:1 x2:0 ln2:1 router:0 fc1:0:0:0 fc1:0:0:1 fc1:0:0:2 fc1:0:0:3
        turn_gates:0 fc1:0:1:0 fc1:0:1:1 bias2:0 fc1:0:1:2 fc2:0:0:0 fc1:0:1:3 fc1:0:2:0 fc2:0:0:1 fc2:0:0:2
        fc2:0:0:3 fc1:0:2:1 fc1:0:2:2 fc2:0:1:0 fc1:0:2:3 fc2:0:1:1 fc1:0:3:0 fc2:0:1:2 fc2:0:1:3 fc1:0:3:1
        fc1:0:3:2 fc2:0:2:0 fc1:0:3:3 fc2:0:2:1 fc1:0:4:0 fc2:0:2:2 fc2:0:2:3 fc1:0:4:1 fc1:0:4:2 fc2:0:3:0
        fc1:0:4:3 fc2:0:3:1 fc1:0:5:0 fc2:0:3:2 fc2:0:3:3 fc1:0:5:1 fc1:0:5:2 fc2:0:4:0 fc1:0:5:3 fc2:0:4:1
        fc1:0:6:0 fc2:0:4:2 fc2:0:4:3 fc1:0:6:1 fc1:0:6:2 fc2:0:5:0 fc1:0:6:3 fc2:0:5:1 fc1:0:7:0 fc2:0:5:2
        fc2:0:5:3 fc1:0:7:1 x2:1 fc1:0:7:2 fc1:0:7:3 fc2:0:6:0 fc2:0:6:1 fc2:0:6:2 fc1:1:0:0 fc1:1:0:1 fc2:0:6:3
        fc1:1:0:2 fc1:1:0:3 fc2:0:7:0 fc2:0:7:1 fc1:1:1:0 fc2:0:7:2 fc1:1:1:1 router:1 fc2:0:7:3 fc1:1:1:2 fc1:1:1:3
        fc2:1:0:0 fc2:1:0:1 fc1:1:2:0 fc2:1:0:2 fc1:1:2:1 fc2:1:0:3 turn_gates:1 fc1:1:2:2 fc1:1:2:3 fc2:1:1:0
        bias2:1 fc2:1:1:1 fc1:1:3:0 fc2:1:1:2 fc1:1:3:1 fc2:1:1:3 fc1:1:3:2 fc1:1:3:3 fc2:1:2:0 fc2:1:2:1 fc1:1:4:0
        fc2:1:2:2 fc1:1:4:1 fc2:1:2:3 fc1:1:4:2 fc1:1:4:3 fc2:1:3:0 fc2:1:3:1 fc1:1:5:0 fc2:1:3:2 fc1:1:5:1
        fc2:1:3:3 fc1:1:5:2 fc1:1:5:3 fc2:1:4:0 fc2:1:4:1 fc1:1:6:0 fc2:1:4:2 fc1:1:6:1 fc2:1:4:3 fc1:1:6:2
        fc1:1:6:3 fc2:1:5:0 fc1:1:7:0 fc2:1:5:1 fc1:1:7:1 fc2:1:5:2 fc2:1:5:3 fc1:1:7:2 fc1:1:7:3 fc2:1:6:0
        fc2:1:6:1 fc2:1:6:2 fc2:1:6:3 fc2:1:7:0 fc2:1:7:1 fc2:1:7:2 fc2:1:7:3""",
    "ACT": """
        ctx:0 in_u:0 ctx:1 round:0 round:1 in_u:1 in_q:0 in_deq:0 wsquare:0:0 wsquare:1:0 wsquare:0:1 wsquare:1:1
        wsquare:0:2 sigmoids:0 g:0 in_q:1 wsquare:1:2 wsquare:0:3 in_deq:1 o:0 wsquare:1:3 sigmoids:1 out_var:0 g:1
        wsquare:0:4 wsquare:1:4 o:1 wsquare:0:5 wsquare:1:5 wsquare:0:6 out_var:1 out_q:0 wsquare:1:6 wsquare:0:7
        wsquare:1:7 res:0 mlp_var:0 out_q:1 mlp_q:0 res:1 gate0:0 mlp_var:1 whigh:0:0 gate1:0 zsq0:0 whigh:1:0
        whigh:0:1 gate2:0 zsq1:0 whigh:1:1 whigh:0:2 whigh:1:2 mlp_q:1 gate3:0 zsq2:0 gate0:1 whigh:0:3 zsq3:0
        whigh:1:3 whigh:0:4 gate1:1 zsq0:1 whigh:1:4 whigh:0:5 gate2:1 zsq1:1 whigh:1:5 whigh:0:6 gate3:1 zsq2:1
        whigh:1:6 z_q0:0 whigh:0:7 z_q1:0 z_q2:0 zsq3:1 z_q3:0 whigh:1:7 z_q0:1 z_q1:1 z_q2:1 z_q3:1 x1:0 softmax:0
        turn:0 attend:0 x1:1 softmax:1 turn:1 attend:1 x2:0 router:0 gelu:0:0:0 gelu:0:0:1 gelu:0:0:2 gelu:0:0:3
        turn_gates:0 gelu:0:1:0 gelu:0:1:1 gelu:0:1:2 gelu:0:1:3 gelu:0:2:0 gelu:0:2:1 gelu:0:2:2 gelu:0:2:3
        gelu:0:3:0 gelu:0:3:1 gelu:0:3:2 gelu:0:3:3 gelu:0:4:0 gelu:0:4:1 gelu:0:4:2 gelu:0:4:3 gelu:0:5:0
        gelu:0:5:1 gelu:0:5:2 gelu:0:5:3 gelu:0:6:0 gelu:0:6:1 gelu:0:6:2 gelu:0:6:3 gelu:0:7:0 gelu:0:7:1 x2:1
        gelu:0:7:2 gelu:0:7:3 gelu:1:0:0 gelu:1:0:1 high:1:0:0 gelu:1:0:2 gelu:1:0:3 high:1:0:1 high:1:0:2
        gelu:1:1:0 high:1:0:3 gelu:1:1:1 high:1:1:0 gelu:1:1:2 router:1 gelu:1:1:3 high:1:1:1 high:1:1:2 gelu:1:2:0
        high:1:1:3 gelu:1:2:1 high:1:2:0 turn_gates:1 gelu:1:2:2 gelu:1:2:3 high:1:2:1 high:1:2:2 high:1:2:3
        gelu:1:3:0 gelu:1:3:1 high:1:3:0 gelu:1:3:2 gelu:1:3:3 high:1:3:1 high:1:3:2 gelu:1:4:0 high:1:3:3
        gelu:1:4:1 high:1:4:0 gelu:1:4:2 gelu:1:4:3 high:1:4:1 high:1:4:2 gelu:1:5:0 high:1:4:3 gelu:1:5:1
        high:1:5:0 gelu:1:5:2 gelu:1:5:3 high:1:5:1 high:1:5:2 gelu:1:6:0 high:1:5:3 gelu:1:6:1 high:1:6:0
        gelu:1:6:2 gelu:1:6:3 high:1:6:1 high:1:6:2 gelu:1:7:0 high:1:6:3 gelu:1:7:1 high:1:7:0 gelu:1:7:2
        high:1:7:1 gelu:1:7:3 high:1:7:2 high:1:7:3""",
    "DVE": """
        in_u:0 in_u:1 means:0 means:1 in_var:0 mean_w:0 mean_w:1 round:0 in_q:0 turn_w:0 in_deq:0 round:1 in_var:1
        turn_w:1 if:0 in_q:1 scan:0 gain:0 turn_small in_deq:1 if:1 o:0 scan:1 out_var:0 gain:1 out_q:0 o:1
        out_var:1 res:0 out_q:1 mlp_var:0 sum_w total_w mlp_q:0 res:1 scale_w gate0:0 mlp_var:1 wlow:0:0 gate1:0
        zsq0:0 mlp_q:1 gate2:0 zsq1:0 wlow:0:1 gate3:0 zsq2:0 zsq3:0 gate0:1 z_var:0 wlow:0:2 gate1:1 zsq0:1
        wlow:0:3 gate2:1 z_q0:0 z_q1:0 z_q2:0 z_q3:0 zsq1:1 gate3:1 zsq2:1 zsq3:1 wlow:0:4 z_var:1 wlow:0:5 wlow:0:6
        down:0 z_q0:1 z_q1:1 z_q2:1 z_q3:1 wlow:0:7 x1:0 down:1 scores:0 turn:0 x1:1 ln2:0 scores:1 x2:0 turn:1
        ln2:1 x2_lo:0 router:0 x2:1 weigh:0 high:0:0:0 high:0:0:1 high:0:0:2 high:0:0:3 high:0:1:0 high:0:1:1
        bias2:0 high:0:1:2 high:0:1:3 high:0:2:0 combine:0:0 high:0:2:1 high:0:2:2 high:0:2:3 combine:0:1 high:0:3:0
        high:0:3:1 high:0:3:2 high:0:3:3 combine:0:2 high:0:4:0 high:0:4:1 high:0:4:2 high:0:4:3 combine:0:3
        high:0:5:0 high:0:5:1 high:0:5:2 high:0:5:3 combine:0:4 high:0:6:0 high:0:6:1 high:0:6:2 high:0:6:3
        combine:0:5 high:0:7:0 high:0:7:1 high:0:7:2 x2_lo:1 high:0:7:3 combine:0:6 low:1:0:1 low:1:0:3 router:1
        combine:0:7 weigh:1 low:1:1:1 low:1:1:3 final:0 low:1:2:1 bias2:1 combine:1:0 low:1:2:3 final_apply:0
        combine:1:1 low:1:3:1 low:1:3:3 combine:1:2 low:1:4:1 low:1:4:3 combine:1:3 low:1:5:1 low:1:5:3 combine:1:4
        low:1:6:1 low:1:6:3 combine:1:5 low:1:7:1 low:1:7:3 combine:1:6 combine:1:7 final:1 final_apply:1""",
    "Pool": """
        masks:0:0 masks:0:1 masks:0:2 in_var:0 masks:0:3 masks:1:0 masks:1:1 in_var:1 masks:1:2 masks:1:3 gain:0
        out_var:0 gain:1 out_var:1 mlp_var:0 root_w mlp_var:1 wlow:1:0 wlow:1:1 wlow:1:2 z_var:0 wlow:1:3 wlow:1:4
        z_var:1 wlow:1:5 down:0 wlow:1:6 x1:0 wlow:1:7 down:1 x1:1 ln2:0 ln2:1 low:0:0:0 low:0:0:1 low:0:0:2
        low:0:0:3 low:0:1:0 low:0:1:1 low:0:1:2 low:0:1:3 low:0:2:0 low:0:2:1 low:0:2:2 low:0:2:3 low:0:3:0
        low:0:3:1 low:0:3:2 low:0:3:3 low:0:4:0 low:0:4:1 low:0:4:2 low:0:4:3 low:0:5:0 low:0:5:1 low:0:5:2
        low:0:5:3 low:0:6:0 low:0:6:1 low:0:6:2 low:0:6:3 low:0:7:0 low:0:7:1 low:0:7:2 low:0:7:3 low:1:0:0
        low:1:0:2 low:1:1:0 low:1:1:2 low:1:2:0 final:0 low:1:2:2 low:1:3:0 low:1:3:2 low:1:4:0 low:1:4:2 low:1:5:0
        low:1:5:2 low:1:6:0 low:1:6:2 low:1:7:0 low:1:7:2 final:1""",
}


def order_of(engine):
    for word in ORDER[engine].split():
        name, *numbers = word.split(":")
        numbers = [int(n) for n in numbers]
        yield ("ab", *numbers, name) if name in STAGES else (name, *numbers)


class Steps:

    def __init__(self, sem):
        self.sem, self.count = sem, 0

    def mark(self, instruction):
        instruction.then_inc(self.sem, 1)
        self.count += 1
        return self.count


def decoder_layer(nc, x, ctx_mem, pads, lower_bound, attn_norm_w, w_i, w_f, w_g, g_norm_w, w_o,
                  mlp_norm_w, w_gate, w_down, xattn_w, xattn_b, w1, b1, w2, b2, wr, br, out):
    fp32, bf16, fp16, int32 = mybir.dt.float32, mybir.dt.bfloat16, mybir.dt.float16, mybir.dt.int32
    ALU, ACT, AX = mybir.AluOpType, mybir.ActivationFunctionType, mybir.AxisListType.X
    AXY = mybir.AxisListType.XY

    GATE_ROWS = 2 * INNER
    GATE_BLOCKS = -(-GATE_ROWS // P)
    GATE_TAIL = GATE_ROWS - (GATE_BLOCKS - 1) * P
    DOWN = [(c, min(P, INNER - c * P)) for c in range(-(-INNER // P))]
    WCOLS = 4 * D + GATE_BLOCKS * D + INNER
    WEIGHT_COLS = [(k * D, (k + 1) * D) for k in range(4)] + [(4 * D, 4 * D + GATE_BLOCKS * D), (WCOLS - INNER, WCOLS)]

    stack = ExitStack()
    with stack:
        def sb(name, shape, dt=fp32):
            return stack.enter_context(nc.sbuf_tensor(name, shape, dt))

        def pb(name, shape, dt=fp32):
            return stack.enter_context(nc.psum_tensor(name, shape, dt))

        def sem(name):
            return stack.enter_context(nc.semaphore(name))

        ident = sb("ident", [P, P])
        ones = sb("ones", [P, P])
        half = sb("half", [P, PT])
        minus_half = sb("minus_half", [P, PT])
        qpos = sb("qpos", [P, TILES])
        kpos = sb("kpos", [P, SEQ])
        qpos_i = sb("qpos_i", [P, TILES], int32)
        kpos_i = sb("kpos_i", [P, SEQ], int32)
        round_up = sb("round_up", [P, 1])
        wraw = sb("wraw", [P, WCOLS])
        wmagic = wraw
        GATE_AT, DOWN_AT = 4 * D, 4 * D + GATE_BLOCKS * D
        attn_raw = wraw[:, 0:GATE_AT].rearrange("p (k d) -> p k d", k=4)
        gate_raw = wraw[:, GATE_AT:DOWN_AT].rearrange("p (k d) -> p k d", k=GATE_BLOCKS)
        down_raw = wraw[:, DOWN_AT:WCOLS]
        attn_T = sb("attn_T", [P, 4 * D], bf16)
        gate_T = sb("gate_T", [P, GATE_ROWS], bf16)
        down_T = sb("down_T", [P, len(DOWN), D], bf16)
        wabs = sb("wabs", [P, 6])
        wmean = sb("wmean", [P, 6])
        wscale = sb("wscale", [P, 6])
        half_mean = sb("half_mean", [P, 2])
        omf_bias = sb("omf_bias", [P, 1])
        omf_scale = sb("omf_scale", [P, 1])
        norm_w = sb("norm_w", [P, 3, D])
        gw_half = sb("gw_half", [P, D])
        xb_bias = sb("xb_bias", [P, D])
        br_bc = sb("br_bc", [P, EXPERTS])
        lb = sb("lb", [P, 1])
        f_gain = sb("f_gain", [P, 1])
        f_base = sb("f_base", [P, 1])
        xw_raw = sb("xw_raw", [P, D])
        xw_T = sb("xw_T", [P, D])
        wr_sb = sb("wr_sb", [P, EXPERTS])
        b2_sb = sb("b2_sb", [EXPERTS, D])
        b1_rows = sb("b1_rows", [EXPERTS * CHUNKS, P])
        b1_T = sb("b1_T", [P, EXPERTS * CHUNKS])
        w_sb = [sb(f"w{m}_sb", [P, EXPERTS, HIDDEN]) for m in (1, 2)]
        w_hi = [sb(f"w{m}_hi", [P, EXPERTS, HIDDEN], fp16) for m in (1, 2)]
        w_lo = [sb(f"w{m}_lo", [P, EXPERTS, HIDDEN], fp16) for m in (1, 2)]
        w_scaled = [sb(f"w_scaled{n}", [P, HIDDEN]) for n in range(2)]
        w_sumsq = sb("w_sumsq", [P, 2, EXPERTS])
        w_sum = sb("w_sum", [P, 2])
        w_total = sb("w_total", [P, 2])
        w_norm = sb("w_norm", [P, 2])
        w_power = sb("w_power", [P, 2])
        w_up = sb("w_up", [P, 2])
        w_down_scale = sb("w_down_scale", [P, 2])
        xt = sb("xt", [P, PAIRS, PT, D])
        ctx = sb("ctx", [P, PAIRS, PT, D])
        pad_i = sb("pad_i", [P, BATCH], int32)
        pad_f = sb("pad_f", [P, BATCH])

        def pairs(name, shape, dt=fp32):
            return [sb(f"{name}_{k}", shape, dt) for k in range(PAIRS)]

        qneg = pairs("qneg", [P, PT])
        negmask = pairs("negmask", [P, PT, SEQ])
        NORMS = ("in", "out", "mlp", "z")
        stat = [{t: {n: sb(f"{n}_{t}_{k}", [P, PT]) for n in
                     ("ssx", "ssu", "peak", "peakq", "tail", "var", "root", "step", "inv", "rroot")}
                 for t in NORMS} for k in range(PAIRS)]
        gss = pairs("gss", [P, PT])
        ginv = pairs("ginv", [P, PT])
        junk = pairs("junk", [P, 2, PT, D], bf16)
        u = pairs("u", [P, PT, D])
        q_d = pairs("q_d", [P, PT, D])
        qT_d = pairs("qT_d", [P, PT * P], bf16)
        qT = {"in": qT_d, "out": qT_d, "mlp": qT_d}
        qT_z = pairs("qT_z", [P, PT, len(DOWN), P], bf16)
        deq_in = pairs("deq_in", [P, PT])
        deq_g = pairs("deq_g", [P, PT])
        deq_gh = pairs("deq_gh", [P, PT])
        deq_gg = pairs("deq_gg", [P, PT])
        deq_bc = pairs("deq_bc", [P, PT * P])
        wide = pairs("wide", [P, 2 * PT * INNER])
        uf, ui, f_T, th_i, th_g = ([wide[k][:, n * PT * P:(n + 1) * PT * P] for k in range(PAIRS)] for n in range(5))
        th_g = [b.rearrange("p (j d) -> p j d", j=PT) for b in th_g]
        zt, q_z = ([wide[k][:, n * PT * INNER:(n + 1) * PT * INNER].rearrange("p (j n) -> p j n", j=PT)
                    for k in range(PAIRS)] for n in range(2))
        q = {"in": q_d, "out": q_d, "mlp": q_d, "z": q_z}
        th_f = f_T
        omf_T = uf
        i_T = th_i
        sg2 = gain = th_g
        o_T = deq_bc
        deq_o = pairs("deq_o", [P, PT])
        res = pairs("res", [P, PT, D])
        xres = [xt[:, k] for k in range(PAIRS)]
        deqh = pairs("deqh", [P, PT])
        deqg = pairs("deqg", [P, PT])
        deqgg = pairs("deqgg", [P, PT])
        za = z = zt
        deq_z = pairs("deq_z", [P, PT])
        pre = u
        bn = [pairs(f"bn{n}", [P, PT, 6]) for n in range(2)]
        mv = [pairs(f"mv{n}", [P, PT, 2]) for n in range(2)]
        lnv = [pairs(f"lnv{n}", [P, PT]) for n in range(2)]
        rstd = [pairs(f"rstd{n}", [P, PT]) for n in range(2)]
        x1 = q_d
        x1b = res
        x1_T = pairs("x1_T", [P, PT * P])
        ctx_T = pairs("ctx_T", [P, PT * P])
        sc = prob = negmask
        negmax = pairs("negmax", [P, PT])
        prob_sum = pairs("prob_sum", [P, PT])
        rsum = pairs("rsum", [P, PT])
        prob_T = [zt[k][:].rearrange("p j n -> p (j n)")[:, 0:PT * SEQ].rearrange("p (r t q) -> p r t q", r=PAIR, t=TILES)
                  for k in range(PAIRS)]
        att_T = deq_bc
        x2 = xres
        x2_T = x1_T
        lg = pairs("lg", [P, PT, EXPERTS])
        top = pairs("top", [P, PT, 8])
        lgt = pairs("lgt", [P, PT, EXPERTS])
        tg = pairs("tg", [P, PT, EXPERTS])
        den = pairs("den", [P, PT, EXPERTS])
        rden = pairs("rden", [P, PT, EXPERTS])
        eg = pairs("eg", [P, PT, EXPERTS])
        chosen = pairs("chosen", [P, PT, EXPERTS])
        em = pairs("em", [P, PT, EXPERTS])
        esum = pairs("esum", [P, PT])
        ersum = pairs("ersum", [P, PT])
        gate_w = pairs("gate_w", [P, PT, EXPERTS])
        gate_wT = [x1b[k][0:EXPERTS].rearrange("e j d -> e (j d)") for k in range(PAIRS)]
        x2_hi = sb("x2_hi", [P, PAIRS, PAIR, SEQ], fp16)
        x2_lo = sb("x2_lo", [P, PAIRS, PAIR, SEQ], fp16)
        gate_s = sb("gate_s", [P, PAIRS, PT, EXPERTS])
        acc = sb("acc", [P, PAIRS, PT, D])
        hid = sb("hid", [P, CHUNKS, PAIR * SEQ])
        h_hi = sb("h_hi", [P, 2, CHUNKS, PAIR * SEQ], fp16)
        h_lo = sb("h_lo", [P, 2, CHUNKS, PAIR * SEQ], fp16)
        fbn = sb("fbn", [P, PT, 6])
        fmv = sb("fmv", [P, PT, 2])
        flnv = sb("flnv", [P, PT])
        frstd = sb("frstd", [P, PT])
        fexp = sb("fexp", [P, PT])

        A = [pb(f"A{s}", [P, 512]) for s in range(PAIRS)]
        B = [pb(f"B{s}", [P, 512]) for s in range(PAIRS)]
        H = [pb(f"H{k}", [P, PAIR * SEQ]) for k in range(HBANKS)]
        Y = [pb(f"Y{k}", [P, PT, D]) for k in range(YBANKS)]

        Y0 = Y[0][:].rearrange("p j d -> p (j d)")

        x_loaded, ctx_loaded = [sem(f"x_loaded{k}") for k in range(PAIRS)], [sem(f"ctx_loaded{k}") for k in range(PAIRS)]
        pad_loaded = sem("pad_loaded")
        wattn_loaded, wgate_loaded, wdown_loaded = sem("wattn_loaded"), sem("wgate_loaded"), sem("wdown_loaded")
        lb_loaded, small_loaded = sem("lb_loaded"), sem("small_loaded")
        norm_loaded = [sem(f"norm_loaded{n}") for n in range(3)]
        w_loaded = [[sem(f"w{m}_loaded{n}") for n in range(EXPERTS // WLOAD)] for m in (1, 2)]
        stored = sem("stored")
        pad_zeroed, pool_step, ident_ready, ones_ready = (
            sem("pad_zeroed"), sem("pool_step"), sem("ident_ready"), sem("ones_ready"))
        wabs_ready, wtot_ready, wscale_ready = sem("wabs_ready"), sem("wtot_ready"), sem("wscale_ready")
        wmagic_ready, wclip_ready, wT_ready, wT_moved = (
            sem("wmagic_ready"), sem("wclip_ready"), sem("wT_ready"), sem("wT_moved"))
        wsq_ready, wsum_ready, wnorm_ready, wup_ready = sem("wsq_ready"), sem("wsum_ready"), sem("wnorm_ready"), sem("wup_ready")
        wsum_done, wtot_moved = sem("wsum_done"), sem("wtot_moved")
        w_hi_ready = [sem(f"w{m}_hi_ready") for m in (1, 2)]
        w_lo_ready = [sem(f"w{m}_lo_ready") for m in (1, 2)]
        vec_step, omf_set = sem("vec_step"), sem("omf_set")
        u_ready = {t: sem(f"u_ready_{t}") for t in NORMS}
        squares = {into: {t: sem(f"squares_{into}_{t}") for t in NORMS} for into in ("ssx", "ssu")}
        var_ready = {t: sem(f"var_ready_{t}") for t in NORMS}
        root_ready = {t: sem(f"root_ready_{t}") for t in NORMS}
        q_ready = {t: sem(f"q_ready_{t}") for t in NORMS}
        qT_ready = {t: sem(f"qT_ready_{t}") for t in NORMS}
        qT_moved = {t: sem(f"qT_moved_{t}") for t in NORMS}
        deq_ready, deq_bc_done, deq_bc_moved = sem("deq_ready"), sem("deq_bc_done"), sem("deq_bc_moved")
        f_done, i_done, g_done, uf_ready, ui_ready = sem("f_done"), sem("i_done"), sem("g_done"), sem("uf_ready"), sem("ui_ready")
        thf_ready, omf_ready, thi_ready = sem("thf_ready"), sem("omf_ready"), sem("thi_ready")
        thg_ready, sg_ready, gain_ready = sem("thg_ready"), sem("sg_ready"), sem("gain_ready")
        scan_done, o_ready, wo_done = sem("scan_done"), sem("o_ready"), sem("wo_done")
        res_ready, xres_ready, deqh_ready = sem("res_ready"), sem("xres_ready"), sem("deqh_ready")
        gate_done, value_done, zt_ready = sem("gate_done"), sem("value_done"), sem("zt_ready")
        za_ready, z_ready, down_done = sem("za_ready"), sem("z_ready"), sem("down_done")
        ln_var, ln_rstd = [sem(f"ln_var{n}") for n in range(3)], [sem(f"ln_rstd{n}") for n in range(3)]
        x1_ready, x1b_ready, x1T_ready, x1T_moved = sem("x1_ready"), sem("x1b_ready"), sem("x1T_ready"), sem("x1T_moved")
        ctxT_ready, ctxT_moved = sem("ctxT_ready"), sem("ctxT_moved")
        mask_ready, scores_done, sc_ready, prob_ready = sem("mask_ready"), sem("scores_done"), sem("sc_ready"), sem("prob_ready")
        probT_ready, att_done, attT_moved, proj_done = (
            sem("probT_ready"), sem("att_done"), sem("attT_moved"), sem("proj_done"))
        probT_moved = [sem("probT_moved_act"), sem("probT_moved_vec")]
        x2_ready, x2T_ready, x2T_moved = sem("x2_ready"), sem("x2T_ready"), sem("x2T_moved")
        gates_ready = sem("gates_ready")
        x2hi_ready, x2lo_ready = sem("x2hi_ready"), sem("x2lo_ready")
        logits_done, lg_ready, lgt_ready, tg_ready, gatew_ready = (
            sem("logits_done"), sem("lg_ready"), sem("lgt_ready"), sem("tg_ready"), sem("gatew_ready"))
        gwT_ready, gwT_moved, b2_done, acc_started = sem("gwT_ready"), sem("gwT_moved"), sem("b2_done"), sem("acc_started")
        fc1_done, gelu_done, h_hi_act, h_hi_vec, h_lo_pool, h_lo_vec, fc2_done, combined = (
            sem("fc1_done"), sem("gelu_done"), sem("h_hi_act"), sem("h_hi_vec"), sem("h_lo_pool"), sem("h_lo_vec"), sem("fc2_done"), sem("combined"))
        out_ready = sem("out_ready")

        block = stack.enter_context(nc.Block())

        def tiles_of(dram, g):
            return dram[g].rearrange("(j p) d -> p j d", p=P)

        def tiles(bank):
            return bank[:].rearrange("p (j d) -> p j d", j=PT)

        def rows_of(dram, k):
            return dram[PAIR * k:PAIR * (k + 1)].rearrange("r (j p) d -> p (r j) d", p=P)

        def every_tile(row):
            return row.unsqueeze(1).to_broadcast([P, PT, row.shape[1]])

        def every_column(col, n):
            return col.unsqueeze(2).to_broadcast([P, PT, n])

        def hi_wait(eng, n):
            on_act, on_vec, act_made = hi_counts(n)
            if act_made:
                eng.wait_ge(h_hi_act, on_act)
            else:
                eng.wait_ge(h_hi_vec, on_vec)

        def lo_wait(eng, n):
            on_pool, on_vec, pool_made = lo_counts(n)
            if pool_made:
                eng.wait_ge(h_lo_pool, on_pool)
            else:
                eng.wait_ge(h_lo_vec, on_vec)

        @block.sync
        def _(sp):
            sp.dma_start(xt[:, 0], rows_of(x, 0)).then_inc(x_loaded[0], 16)
            sp.dma_start(attn_raw[:, 0, :], w_i).then_inc(wattn_loaded, 16)
            sp.dma_start(attn_raw[:, 1, :], w_f).then_inc(wattn_loaded, 16)
            sp.dma_start(lb[:], lower_bound.rearrange("(p a) -> p a", a=1)).then_inc(lb_loaded, 16)
            sp.dma_start(pad_i[:], pads.partition_broadcast(P)).then_inc(pad_loaded, 16)
            sp.dma_start(norm_w[:, 1, :], g_norm_w.partition_broadcast(P)).then_inc(norm_loaded[1], 16)
            sp.dma_start(xt[:, 1], rows_of(x, 1)).then_inc(x_loaded[1], 16)
            sp.wait_ge(pad_zeroed, 1)
            sp.dma_start(gate_raw[:, 0:GATE_BLOCKS - 1, :],
                         w_gate[0:(GATE_BLOCKS - 1) * P, :].rearrange("(k p) d -> p k d", p=P)).then_inc(wgate_loaded, 16)
            sp.dma_start(gate_raw[0:GATE_TAIL, GATE_BLOCKS - 1, :],
                         w_gate[(GATE_BLOCKS - 1) * P:GATE_ROWS, :]).then_inc(wgate_loaded, 16)
            sp.dma_start(down_raw, w_down).then_inc(wdown_loaded, 16)
            sp.dma_start(norm_w[:, 2, :], mlp_norm_w.partition_broadcast(P)).then_inc(norm_loaded[2], 16)
            sp.dma_start(ctx[:, 1], rows_of(ctx_mem, 1)).then_inc(ctx_loaded[1], 16)
            for n in range(EXPERTS // WLOAD):
                es = slice(n * WLOAD, (n + 1) * WLOAD)
                sp.dma_start(w_sb[0][:, es, :], w1[es].rearrange("e p h -> p e h")).then_inc(w_loaded[0][n], 16)
                sp.dma_start(w_sb[1][:, es, :].rearrange("p e (c d) -> p e c d", c=CHUNKS),
                             w2[es].rearrange("e (c p) d -> p e c d", p=P)).then_inc(w_loaded[1][n], 16)
                if n == 0:
                    sp.dma_start(b1_rows[:], b1.rearrange("e (c p) -> (e c) p", p=P)).then_inc(small_loaded, 16)
                    sp.dma_start(xw_raw[:], xattn_w).then_inc(small_loaded, 16)
                    sp.dma_start(xb_bias[:], xattn_b.partition_broadcast(P)).then_inc(small_loaded, 16)
            sp.dma_start(br_bc[:], br.partition_broadcast(P)).then_inc(small_loaded, 16)
            sp.dma_start(wr_sb[:], wr).then_inc(small_loaded, 16)
            sp.dma_start(b2_sb[:], b2).then_inc(small_loaded, 16)
            for k in range(PAIRS):
                for r in range(PAIR):
                    sp.wait_ge(out_ready, PT * k + TILES * (r + 1))
                    sp.dma_start(tiles_of(out, PAIR * k + r), acc[:, k, r * TILES:(r + 1) * TILES, :]).then_inc(stored, 16)
            sp.wait_ge(stored, 16 * BATCH)

        @block.gpsimd
        def _(pool):
            step = Steps(pool_step)
            v = nc.gpsimd
            v.memset(gate_raw[GATE_TAIL:P, GATE_BLOCKS - 1, :], 0.0).then_inc(pad_zeroed, 1)
            pool.wait_ge(pad_zeroed, 1)
            v.memset(ones[:], 1.0).then_inc(ones_ready, 1)
            n = step.mark(v.memset(ident[:], 0.0))
            step.mark(v.memset(half[:], 0.5))
            step.mark(v.memset(fexp[:], -0.5))
            step.mark(v.memset(minus_half[:], -0.5))
            pool.wait_ge(pool_step, n)
            v.affine_select(out=ident[:], in_=ident[:], compare_op=ALU.not_equal, fill=1.0, base=0,
                            pattern=[[-1, P]], channel_multiplier=1).then_inc(ident_ready, 1)
            step.mark(v.iota(qpos_i[:], pattern=[[P, TILES]], base=0, channel_multiplier=1))
            n = step.mark(v.iota(kpos_i[:], pattern=[[1, SEQ]], base=0, channel_multiplier=0))
            pool.wait_ge(pool_step, n)
            step.mark(v.tensor_copy(qpos[:], qpos_i[:]))
            step.mark(v.tensor_copy(kpos[:], kpos_i[:]))

            pool.wait_ge(pad_loaded, 16)
            n = step.mark(v.tensor_copy(pad_f[:], pad_i[:]))
            pool.wait_ge(norm_loaded[1], 16)
            n = step.mark(v.tensor_scalar(gw_half[:], norm_w[:, 1, :], 0.5, None, ALU.mult))
            pool.wait_ge(pool_step, n)

            def masks(k, h):
                r, j = divmod(h, TILES)
                g = PAIR * k + r
                if j == 0:
                    n = step.mark(v.tensor_scalar(qneg[k][:, r * TILES:(r + 1) * TILES], qpos[:], pad_f[:, g:g + 1], NEG / SCALE,
                                                  ALU.is_ge, ALU.mult))
                    pool.wait_ge(pool_step, n)
                v.tensor_scalar(negmask[k][:, h, :], kpos[:], pad_f[:, g:g + 1], qneg[k][:, h:h + 1],
                                ALU.is_ge, ALU.mult).then_inc(mask_ready, 1)

            def root(t, k):
                pool.wait_ge(var_ready[t], k + 1)
                v.tensor_tensor(stat[k][t]["root"][:], stat[k][t]["var"][:], half[:], ALU.pow).then_inc(root_ready[t], 1)

            def inverse_root(n, k):
                pool.wait_ge(ln_var[n], k + 1)
                v.tensor_tensor(rstd[n][k][:], lnv[n][k][:], minus_half[:], ALU.pow).then_inc(ln_rstd[n], 1)

            def ab(k, stage):
                if stage == "in_var":
                    root("in", k)
                elif stage == "gain":
                    pool.wait_ge(sg_ready, k + 1)
                    v.tensor_tensor(gain[k][:], sg2[k][:], every_tile(gw_half[:]), ALU.mult).then_inc(gain_ready, 1)
                elif stage == "out_var":
                    root("out", k)
                elif stage == "mlp_var":
                    root("mlp", k)
                    pool.wait_ge(res_ready, PT * (k + 1))
                    v.tensor_tensor(xres[k], res[k][:], xt[:, k], ALU.add).then_inc(xres_ready, 1)
                elif stage == "z_var":
                    root("z", k)
                elif stage == "down":
                    inverse_root(0, k)
                elif stage == "x1":
                    pool.wait_ge(x1_ready, PT * (k + 1))
                    v.tensor_tensor(x1b[k][:], x1[k][:], every_tile(xb_bias[:]), ALU.add).then_inc(x1b_ready, 1)
                elif stage == "ln2":
                    inverse_root(1, k)

            def weights_norm():
                pool.wait_ge(wtot_moved, 1)
                v.tensor_tensor(w_norm[:], w_total[:], half[:, 0:2], ALU.pow).then_inc(wnorm_ready, 1)

            def split_low(m, e):
                if m == 1:
                    pool.wait_ge(wup_ready, 1)
                    scaled = w_scaled[e % 2]
                    if e >= 2:
                        pool.wait_ge(w_lo_ready[m], e - 1)
                    n = step.mark(v.tensor_scalar(scaled[:], w_sb[m][:, e, :], w_up[:, m:m + 1], None, ALU.mult))
                    pool.wait_ge(pool_step, n)
                    pool.wait_ge(w_hi_ready[m], e + 1)
                    v.tensor_tensor(w_lo[m][:, e, :], scaled[:], w_hi[m][:, e, :], ALU.subtract).then_inc(w_lo_ready[m], 1)

            def hidden_low(k, e, c):
                n = (k * EXPERTS + e) * CHUNKS + c
                if lo_on_pool(k, e, c):
                    hi_wait(pool, n)
                    if n >= 2 * CHUNKS:
                        pool.wait_ge(fc2_done, n // CHUNKS - 1)
                    v.tensor_tensor(h_lo[:, e % 2, c, :], hid[:, c, :], h_hi[:, e % 2, c, :],
                                    ALU.subtract).then_inc(h_lo_pool, 1)

            def final(k):
                pool.wait_ge(ln_var[2], k + 1)
                v.tensor_tensor(frstd[:], flnv[:], fexp[:], ALU.pow).then_inc(ln_rstd[2], 1)

            for what in order_of("Pool"):
                if what[0] == "ab":
                    ab(*what[1:])
                elif what[0] == "masks":
                    masks(*what[1:])
                elif what[0] == "root_w":
                    weights_norm()
                elif what[0] == "wlow":
                    split_low(*what[1:])
                elif what[0] == "low":
                    hidden_low(*what[1:])
                elif what[0] == "final":
                    final(*what[1:])

        @block.scalar
        def _(act):
            a = nc.scalar
            act.dma_start(norm_w[:, 0, :], attn_norm_w.partition_broadcast(P)).then_inc(norm_loaded[0], 16)
            act.dma_start(attn_raw[:, 2, :], w_g).then_inc(wattn_loaded, 16)
            act.dma_start(attn_raw[:, 3, :], w_o).then_inc(wattn_loaded, 16)
            act.dma_start(ctx[:, 0], rows_of(ctx_mem, 0)).then_inc(ctx_loaded[0], 16)

            def ternary_round(part):
                act.wait_ge(wscale_ready, part + 1)
                for k in TERNARY[part]:
                    lo, hi = WEIGHT_COLS[k]
                    a.activation(wmagic[:, lo:hi], wraw[:, lo:hi], ACT.Identity, bias=round_up[:],
                                 scale=wscale[:, k:k + 1]).then_inc(wmagic_ready, 1)

            def weights_square(m, e):
                act.wait_ge(w_loaded[m][e // WLOAD], 16)
                a.activation(w_lo[m][:, e, :], w_sb[m][:, e, :], ACT.Square,
                             accum_out=w_sumsq[:, m, e:e + 1]).then_inc(wsq_ready, 1)

            def split_high(m, e):
                act.wait_ge(wup_ready, 1)
                a.activation(w_hi[m][:, e, :], w_sb[m][:, e, :], ACT.Copy, scale=w_up[:, m:m + 1]).then_inc(w_hi_ready[m], 1)

            def square_sums(t, k, source, into):
                for j in range(PT):
                    a.activation(junk[k][:, ("ssx", "ssu").index(into), j, :], source[:, j, :], ACT.Square,
                                 accum_out=stat[k][t][into][:, j:j + 1]).then_inc(squares[into][t], 1)

            def strip_round(t, k, bank):
                act.wait_ge(qT_ready[t], k + 1)
                a.activation(qT[t][k][:], bank[:], ACT.Copy, bias=-ROUND).then_inc(qT_moved[t], 1)

            def ab(k, stage):
                if stage == "ctx":
                    act.wait_ge(ctxT_ready, k + 1)
                    a.activation(ctx_T[k][:], B[k][:], ACT.Copy).then_inc(ctxT_moved, 1)
                elif stage == "in_u":
                    act.wait_ge(x_loaded[k], 16)
                    square_sums("in", k, xt[:, k], "ssx")
                    act.wait_ge(u_ready["in"], k + 1)
                    square_sums("in", k, u[k], "ssu")
                elif stage == "in_q":
                    strip_round("in", k, A[k])
                elif stage == "in_deq":
                    act.wait_ge(deq_bc_done, k + 1)
                    a.activation(deq_bc[k][:], B[k][:], ACT.Copy).then_inc(deq_bc_moved, 1)
                elif stage == "sigmoids":
                    act.wait_ge(uf_ready, k + 1)
                    a.activation(th_f[k][:], uf[k][:], ACT.Tanh, scale=half_mean[:, 1:2]).then_inc(thf_ready, 1)
                    act.wait_ge(ui_ready, k + 1)
                    a.activation(th_i[k][:], ui[k][:], ACT.Tanh, scale=half_mean[:, 0:1]).then_inc(thi_ready, 1)
                    act.wait_ge(thf_ready, k + 1)
                    act.wait_ge(omf_set, 1)
                    a.activation(omf_T[k][:], th_f[k][:], ACT.Identity, bias=omf_bias[:], scale=omf_scale[:]).then_inc(omf_ready, 1)
                elif stage == "g":
                    act.wait_ge(g_done, k + 1)
                    for j in range(PT):
                        a.activation(th_g[k][:, j, :], B[k][:, j * D:(j + 1) * D], ACT.Tanh,
                                     scale=deq_gh[k][:, j:j + 1]).then_inc(thg_ready, 1)
                elif stage == "o":
                    act.wait_ge(o_ready, k + 1)
                    square_sums("out", k, tiles(A[k]), "ssx")
                elif stage == "out_var":
                    act.wait_ge(u_ready["out"], k + 1)
                    square_sums("out", k, u[k], "ssu")
                elif stage == "out_q":
                    strip_round("out", k, B[k])
                elif stage == "res":
                    act.wait_ge(res_ready, PT * (k + 1))
                    square_sums("mlp", k, res[k], "ssx")
                elif stage == "mlp_var":
                    act.wait_ge(u_ready["mlp"], k + 1)
                    square_sums("mlp", k, u[k], "ssu")
                elif stage == "mlp_q":
                    strip_round("mlp", k, B[k])
                elif stage.startswith("gate"):
                    j = int(stage[-1])
                    n = PT * k + j
                    if j == 0:
                        act.wait_ge(deqh_ready, k + 1)
                    act.wait_ge(gate_done, n + 1)
                    a.activation(zt[k][:, j, :], A[k][:, 0:INNER], ACT.Tanh, scale=deqh[k][:, j:j + 1]).then_inc(zt_ready, 1)
                elif stage.startswith("zsq"):
                    j = int(stage[-1])
                    act.wait_ge(z_ready, PT * k + j + 1)
                    a.activation(q_z[k][:, j, :], z[k][:, j, :], ACT.Square,
                                 accum_out=stat[k]["z"]["ssu"][:, j:j + 1]).then_inc(squares["ssu"]["z"], 1)
                elif stage.startswith("z_q"):
                    j = int(stage[-1])
                    act.wait_ge(qT_ready["z"], PT * k + j + 1)
                    a.activation(qT_z[k][:, j, :, :], (A, B)[j % 2][k][:, 0:len(DOWN) * P].rearrange("p (c q) -> p c q", c=len(DOWN)),
                                 ACT.Copy, bias=-ROUND).then_inc(qT_moved["z"], 1)
                elif stage == "x1":
                    act.wait_ge(x1T_ready, k + 1)
                    a.activation(x1_T[k][:], B[k][:], ACT.Copy).then_inc(x1T_moved, 1)
                elif stage == "softmax":
                    for j in range(PT):
                        act.wait_ge(sc_ready, PT * k + j + 1)
                        a.activation(prob[k][:, j, :], sc[k][:, j, :], ACT.Exp, bias=negmax[k][:, j:j + 1], scale=-1.0,
                                     accum_out=prob_sum[k][:, j:j + 1]).then_inc(prob_ready, 1)
                elif stage == "turn":
                    act.wait_ge(probT_ready, PAIR * k + 1)
                    a.activation(prob_T[k][:, 0], A[k][:].rearrange("p (t q) -> p t q", t=TILES), ACT.Copy).then_inc(probT_moved[0], 1)
                elif stage == "attend":
                    for r in range(PAIR):
                        act.wait_ge(att_done, PAIR * k + r + 1)
                        a.activation(att_T[k][:, r * SEQ:(r + 1) * SEQ], (A, B)[r][k][:, 0:SEQ], ACT.Copy).then_inc(attT_moved, 1)
                elif stage == "x2":
                    act.wait_ge(x2T_ready, k + 1)
                    a.activation(x2_T[k][:], B[k][:], ACT.Copy).then_inc(x2T_moved, 1)
                    act.wait_ge(x2T_moved, k + 1)
                    a.activation(x2_hi[:, k], x2_T[k][:].rearrange("p (r t) -> p r t", r=PAIR), ACT.Copy, scale=X_UP).then_inc(x2hi_ready, 1)
                elif stage == "router":
                    act.wait_ge(lgt_ready, k + 1)
                    a.activation(tg[k][:], lgt[k][:], ACT.Tanh, scale=0.5).then_inc(tg_ready, 1)
                elif stage == "turn_gates":
                    act.wait_ge(gwT_ready, k + 1)
                    a.activation(gate_wT[k][:], B[k][0:EXPERTS, :], ACT.Copy).then_inc(gwT_moved, 1)

            def hidden(k, e, c):
                n = (k * EXPERTS + e) * CHUNKS + c
                act.wait_ge(fc1_done, n + 1)
                if n >= CHUNKS:
                    lo_wait(act, n - CHUNKS)
                    hi_wait(act, n - CHUNKS)
                a.activation(hid[:, c, :], H[n % HBANKS][:], ACT.Gelu, scale=w_down_scale[:, 0:1],
                             bias=b1_T[:, e * CHUNKS + c:e * CHUNKS + c + 1]).then_inc(gelu_done, 1)

            def hidden_high(k, e, c):
                n = (k * EXPERTS + e) * CHUNKS + c
                if hi_on_act(k, e, c):
                    act.wait_ge(gelu_done, n + 1)
                    if n >= 2 * CHUNKS:
                        act.wait_ge(fc2_done, n // CHUNKS - 1)
                    a.activation(h_hi[:, e % 2, c, :], hid[:, c, :], ACT.Copy).then_inc(h_hi_act, 1)

            for what in order_of("ACT"):
                if what[0] == "ab":
                    ab(*what[1:])
                elif what[0] == "round":
                    ternary_round(*what[1:])
                elif what[0] == "wsquare":
                    weights_square(*what[1:])
                elif what[0] == "whigh":
                    split_high(*what[1:])
                elif what[0] == "gelu":
                    hidden(*what[1:])
                elif what[0] == "high":
                    hidden_high(*what[1:])

        @block.vector
        def _(dve):
            step = Steps(vec_step)
            v = nc.vector
            step.mark(v.memset(round_up[:], ROUND))
            made = {}

            def ternary_means(part):
                if part == 0:
                    dve.wait_ge(wattn_loaded, 64)
                    v.tensor_reduce(wabs[:, 0:4], attn_raw, AX, ALU.add, apply_absolute_value=True).then_inc(wabs_ready, 1)
                else:
                    dve.wait_ge(wgate_loaded, 32)
                    v.tensor_reduce(wabs[:, 4:5], gate_raw, AXY, ALU.add, apply_absolute_value=True).then_inc(wabs_ready, 1)
                    dve.wait_ge(wdown_loaded, 16)
                    v.tensor_reduce(wabs[:, 5:6], down_raw, AX, ALU.add, apply_absolute_value=True).then_inc(wabs_ready, 1)

            def ternary_scales(part):
                cols, size = (((0, 4), D * D), ((4, 6), D * INNER))[part]
                dve.wait_ge(wtot_ready, part + 1)
                if part == 0:
                    n = step.mark(v.tensor_scalar(wmean[:, 0:4], Y[1][:, 0, 0:4], 1.0 / size, CLIP, ALU.mult, ALU.max))
                else:
                    step.mark(v.tensor_scalar(wmean[:, 4:5], Y[1][:, 0, 4:5], 0.5 / size, CLIP, ALU.mult, ALU.max))
                    n = step.mark(v.tensor_scalar(wmean[:, 5:6], Y[1][:, 0, 5:6], 1.0 / size, CLIP, ALU.mult, ALU.max))
                dve.wait_ge(vec_step, n)
                v.reciprocal(wscale[:, cols[0]:cols[1]], wmean[:, cols[0]:cols[1]]).then_inc(wscale_ready, 1)
                if part == 0:
                    dve.wait_ge(lb_loaded, 16)
                    step.mark(v.tensor_scalar(half_mean[:], wmean[:, 0:2], 0.5, None, ALU.mult))
                    n = step.mark(v.tensor_scalar(f_gain[:], lb[:], -0.5, 0.5, ALU.mult, ALU.add))
                    dve.wait_ge(vec_step, n)
                    step.mark(v.tensor_scalar(f_base[:], lb[:], f_gain[:], None, ALU.add))
                    n = step.mark(v.tensor_scalar(omf_bias[:], half_mean[:, 0:1], f_gain[:], None, ALU.mult))
                    dve.wait_ge(vec_step, n)
                    v.tensor_scalar(omf_scale[:], omf_bias[:], -1.0, None, ALU.mult).then_inc(omf_set, 1)

            def ternary_clip(part):
                for k in TERNARY[part]:
                    lo, hi = WEIGHT_COLS[k]
                    dve.wait_ge(wmagic_ready, k + 1)
                    v.tensor_scalar(wmagic[:, lo:hi], wmagic[:, lo:hi], ROUND + 1.0, ROUND - 1.0,
                                    ALU.min, ALU.max).then_inc(wclip_ready, 1)

            def ternary_move(part):
                if part == 0:
                    dve.wait_ge(wT_ready, 1)
                    v.tensor_scalar(attn_T[:], H[0][:], -ROUND, None, ALU.add).then_inc(wT_moved, 1)
                    return
                dve.wait_ge(wT_ready, 2)
                v.tensor_scalar(gate_T[:, 0:512], H[1][:], -ROUND, None, ALU.add).then_inc(wT_moved, 1)
                dve.wait_ge(wT_ready, 3)
                v.tensor_scalar(gate_T[:, 512:GATE_ROWS], Y0[:, 0:GATE_ROWS - 512], -ROUND, None, ALU.add).then_inc(wT_moved, 1)
                dve.wait_ge(wT_ready, 4)
                for c, rows in DOWN:
                    last = v.tensor_scalar(down_T[0:rows, c, :], H[0][0:rows, c * D:(c + 1) * D], -ROUND, None, ALU.add)
                last.then_inc(wT_moved, 1)

            def move_small():
                dve.wait_ge(wT_ready, 5)
                v.tensor_copy(xw_T[:], H[1][:, 0:D])
                v.tensor_copy(b1_T[:], H[1][:, D:D + EXPERTS * CHUNKS]).then_inc(wT_moved, 1)

            def weights_power():
                dve.wait_ge(wsq_ready, 2 * EXPERTS)
                v.tensor_reduce(w_sum[:], w_sumsq[:], AX, ALU.add).then_inc(wsum_ready, 1)

            def weights_total():
                dve.wait_ge(wsum_done, 1)
                v.tensor_copy(w_total[:], Y[1][:, 0, 0:2]).then_inc(wtot_moved, 1)

            def weights_scale():
                dve.wait_ge(wnorm_ready, 1)
                n = step.mark(v.tensor_scalar(w_norm[:], w_norm[:], 1e-30, None, ALU.max))
                dve.wait_ge(vec_step, n)
                n = step.mark(v.tensor_scalar(w_power[:].bitcast(int32), w_norm[:].bitcast(int32), 0x7F800000, None,
                                              ALU.bitwise_and))
                dve.wait_ge(vec_step, n)
                n = step.mark(v.reciprocal(w_up[:], w_power[:]))
                step.mark(v.tensor_scalar(w_down_scale[:, 0:1], w_power[:, 0:1], 1.0 / (W_TARGET * X_UP), None, ALU.mult))
                step.mark(v.tensor_scalar(w_down_scale[:, 1:2], w_power[:, 1:2], 1.0 / W_TARGET, None, ALU.mult))
                dve.wait_ge(vec_step, n)
                v.tensor_scalar(w_up[:], w_up[:], W_TARGET, None, ALU.mult).then_inc(wup_ready, 1)

            def split_low(m, e):
                if m == 0:
                    dve.wait_ge(wup_ready, 1)
                    dve.wait_ge(w_hi_ready[m], e + 1)
                    v.scalar_tensor_tensor(w_lo[m][:, e, :], w_sb[m][:, e, :], w_up[:, m:m + 1], w_hi[m][:, e, :],
                                           ALU.mult, ALU.subtract).then_inc(w_lo_ready[m], 1)

            def peak(t, k, source):
                made["peak", t, k] = step.mark(v.tensor_reduce(stat[k][t]["peak"][:], source, AX, ALU.max,
                                                               apply_absolute_value=True))

            def variance(t, k, scale=None):
                s = stat[k][t]
                peak_step = made["peak", t, k]
                dve.wait_ge(vec_step, peak_step)
                if scale is None:
                    step.mark(v.tensor_scalar(s["peakq"][:], s["peak"][:], 1.0 / QMAX, None, ALU.mult))
                else:
                    step.mark(v.scalar_tensor_tensor(s["peakq"][:], s["peak"][:], 1.0 / QMAX, scale[:], ALU.mult, ALU.mult))
                if t == "z":
                    dve.wait_ge(squares["ssu"]["z"], PT * (k + 1))
                    v.tensor_scalar(s["var"][:], s["ssu"][:], 1.0 / INNER, EPS, ALU.mult, ALU.add).then_inc(var_ready[t], 1)
                    return
                dve.wait_ge(squares["ssx"][t], PT * (k + 1))
                n = step.mark(v.tensor_scalar(s["tail"][:], s["ssx"][:], EPS / D, EPS * EPS, ALU.mult, ALU.add))
                dve.wait_ge(squares["ssu"][t], PT * (k + 1))
                total = s["ssu"]
                if scale is not None:
                    total = gss[k]
                    n = step.mark(v.tensor_tensor(total[:], s["ssu"][:], deq_gg[k][:], ALU.mult))
                dve.wait_ge(vec_step, n)
                v.scalar_tensor_tensor(s["var"][:], total[:], 1.0 / D, s["tail"][:], ALU.mult,
                                       ALU.add).then_inc(var_ready[t], 1)

            def quantise(t, k, source, scale=None, tiles_now=range(PT)):
                s = stat[k][t]
                if tiles_now[0] == 0:
                    dve.wait_ge(root_ready[t], k + 1)
                    n = step.mark(v.scalar_tensor_tensor(s["step"][:], s["root"][:], CLIP / QMAX, s["peakq"][:], ALU.mult, ALU.max))
                    made["rroot", t, k] = step.mark(v.reciprocal(s["rroot"][:], s["root"][:]))
                    dve.wait_ge(vec_step, n)
                    n = step.mark(v.reciprocal(s["inv"][:], s["step"][:]))
                    if scale is not None:
                        dve.wait_ge(vec_step, n)
                        n = step.mark(v.tensor_tensor(ginv[k][:], s["inv"][:], scale[:], ALU.mult))
                    dve.wait_ge(vec_step, n)
                inv = s["inv"] if scale is None else ginv[k]
                for j in tiles_now:
                    v.tensor_scalar(q[t][k][:, j, :], source[:, j, :], inv[:, j:j + 1], ROUND, ALU.mult,
                                    ALU.add).then_inc(q_ready[t], 1)

            def dequantiser(t, k, w, into):
                s = stat[k][t]
                dve.wait_ge(vec_step, made["rroot", t, k])
                scalar = wmean[:, w:w + 1] if w is not None else 1.0
                return v.scalar_tensor_tensor(into[:], s["step"][:], scalar, s["rroot"][:], ALU.mult, ALU.mult)

            def layernorm_stats(m, k, source, n):
                dve.wait_ge(vec_step, n)
                for j in range(PT):
                    n = step.mark(v.bn_stats(bn[m][k][:, j, :], source[:, j, :]))
                dve.wait_ge(vec_step, n)
                for j in range(PT):
                    n = step.mark(v.bn_aggr(mv[m][k][:, j, :], bn[m][k][:, j, :]))
                dve.wait_ge(vec_step, n)
                v.tensor_scalar(lnv[m][k][:], mv[m][k][:, :, 1], LN_EPS, None, ALU.add).then_inc(ln_var[m], 1)

            def layernorm(m, k, source, into, ready):
                dve.wait_ge(ln_rstd[m], k + 1)
                for j in range(PT):
                    v.tensor_scalar(into[:, j, :], source[:, j, :], mv[m][k][:, j, 0:1], rstd[m][k][:, j:j + 1],
                                    ALU.subtract, ALU.mult).then_inc(ready, 1)

            def ab(k, stage):
                if stage == "in_u":
                    dve.wait_ge(x_loaded[k], 16)
                    dve.wait_ge(norm_loaded[0], 16)
                    v.tensor_tensor(u[k][:], xt[:, k], every_tile(norm_w[:, 0, :]), ALU.mult).then_inc(u_ready["in"], 1)
                    dve.wait_ge(u_ready["in"], k + 1)
                    peak("in", k, u[k][:])
                elif stage == "in_var":
                    variance("in", k)
                elif stage == "in_q":
                    quantise("in", k, u[k])
                    dequantiser("in", k, None, deq_in[k]).then_inc(deq_ready, 1)
                elif stage == "in_deq":
                    if k == 0:
                        dve.wait_ge(wscale_ready, 1)
                    n = step.mark(dequantiser("in", k, 2, deq_g[k]))
                    dve.wait_ge(vec_step, n)
                    v.tensor_scalar(deq_gh[k][:], deq_g[k][:], 0.5, None, ALU.mult).then_inc(deq_ready, 1)
                    made["deq_gg", k] = step.mark(v.tensor_tensor(deq_gg[k][:], deq_g[k][:], deq_g[k][:], ALU.mult))
                elif stage == "if":
                    dve.wait_ge(deq_bc_moved, k + 1)
                    dve.wait_ge(f_done, k + 1)
                    v.tensor_tensor(uf[k][:], B[k][:], deq_bc[k][:], ALU.mult).then_inc(uf_ready, 1)
                    dve.wait_ge(i_done, k + 1)
                    v.tensor_tensor(ui[k][:], A[k][:], deq_bc[k][:], ALU.mult).then_inc(ui_ready, 1)
                elif stage == "scan":
                    dve.wait_ge(thi_ready, k + 1)
                    n = step.mark(v.scalar_tensor_tensor(th_i[k][:], th_i[k][:], 1.0, ui[k][:], ALU.add, ALU.mult))
                    dve.wait_ge(omf_ready, k + 1)
                    m = step.mark(v.tensor_scalar(f_T[k][:], th_f[k][:], f_gain[:], f_base[:], ALU.mult, ALU.add))
                    dve.wait_ge(vec_step, n)
                    n = step.mark(v.tensor_tensor(i_T[k][:], th_i[k][:], omf_T[k][:], ALU.mult))
                    dve.wait_ge(vec_step, max(m, n))
                    for r in range(PAIR):
                        row = slice(r * SEQ, (r + 1) * SEQ)
                        v.tensor_tensor_scan(o_T[k][:, row], f_T[k][:, row], i_T[k][:, row], 0.0, ALU.mult, ALU.add).then_inc(scan_done, 1)
                elif stage == "gain":
                    dve.wait_ge(thg_ready, PT * (k + 1))
                    v.scalar_tensor_tensor(sg2[k][:], th_g[k][:], 1.0, tiles(B[k]), ALU.add, ALU.mult).then_inc(sg_ready, 1)
                elif stage == "o":
                    dve.wait_ge(squares["ssx"]["out"], PT * (k + 1))
                    dve.wait_ge(gain_ready, k + 1)
                    v.tensor_tensor(u[k][:], tiles(A[k]), gain[k][:], ALU.mult).then_inc(u_ready["out"], 1)
                    dve.wait_ge(u_ready["out"], k + 1)
                    peak("out", k, u[k][:])
                elif stage == "out_var":
                    dve.wait_ge(vec_step, made["deq_gg", k])
                    variance("out", k, deq_g[k])
                elif stage == "out_q":
                    quantise("out", k, u[k], deq_g[k])
                    made["deq_o", k] = step.mark(dequantiser("out", k, 3, deq_o[k]))
                elif stage == "res":
                    dve.wait_ge(wo_done, k + 1)
                    dve.wait_ge(vec_step, made["deq_o", k])
                    for j in range(PT):
                        v.scalar_tensor_tensor(res[k][:, j, :], A[k][:, j * D:(j + 1) * D], deq_o[k][:, j:j + 1],
                                               xt[:, k, j, :], ALU.mult, ALU.add).then_inc(res_ready, 1)
                    dve.wait_ge(res_ready, PT * (k + 1))
                    dve.wait_ge(norm_loaded[2], 16)
                    v.tensor_tensor(u[k][:], res[k][:], every_tile(norm_w[:, 2, :]), ALU.mult).then_inc(u_ready["mlp"], 1)
                    dve.wait_ge(u_ready["mlp"], k + 1)
                    peak("mlp", k, u[k][:])
                elif stage == "mlp_var":
                    variance("mlp", k)
                elif stage == "mlp_q":
                    if k == 0:
                        dve.wait_ge(wscale_ready, 2)
                    quantise("mlp", k, u[k])
                    n = step.mark(dequantiser("mlp", k, 4, deqg[k]))
                    dve.wait_ge(vec_step, n)
                    v.tensor_scalar(deqh[k][:], deqg[k][:], 0.5, None, ALU.mult).then_inc(deqh_ready, 1)
                    made["deqgg", k] = step.mark(v.scalar_tensor_tensor(deqgg[k][:], deqg[k][:], 0.5, deqg[k][:], ALU.mult, ALU.mult))
                elif stage.startswith("gate"):
                    j = int(stage[-1])
                    n = PT * k + j
                    dve.wait_ge(zt_ready, n + 1)
                    v.scalar_tensor_tensor(za[k][:, j, :], zt[k][:, j, :], 1.0, A[k][:, 0:INNER], ALU.add, ALU.mult).then_inc(za_ready, 1)
                    dve.wait_ge(vec_step, made["deqgg", k])
                    dve.wait_ge(za_ready, n + 1)
                    dve.wait_ge(value_done, n + 1)
                    v.scalar_tensor_tensor(z[k][:, j, :], B[k][:, 0:INNER], deqgg[k][:, j:j + 1], za[k][:, j, :], ALU.mult,
                                           ALU.mult).then_inc(z_ready, 1)
                elif stage.startswith("zsq"):
                    j = int(stage[-1])
                    dve.wait_ge(z_ready, PT * k + j + 1)
                    made["peak", "z", k] = step.mark(v.tensor_reduce(stat[k]["z"]["peak"][:, j:j + 1], z[k][:, j, :], AX, ALU.max,
                                                                     apply_absolute_value=True))
                elif stage == "z_var":
                    variance("z", k)
                elif stage.startswith("z_q"):
                    j = int(stage[-1])
                    quantise("z", k, z[k], tiles_now=[j])
                    if j == PT - 1:
                        made["deq_z", k] = step.mark(dequantiser("z", k, 5, deq_z[k]))
                elif stage == "down":
                    dve.wait_ge(xres_ready, k + 1)
                    dve.wait_ge(down_done, k + 1)
                    dve.wait_ge(vec_step, made["deq_z", k])
                    for j in range(PT):
                        n = step.mark(v.scalar_tensor_tensor(pre[k][:, j, :], A[k][:, j * D:(j + 1) * D],
                                                             deq_z[k][:, j:j + 1], xres[k][:, j, :], ALU.mult, ALU.add))
                    layernorm_stats(0, k, pre[k], n)
                elif stage == "x1":
                    layernorm(0, k, pre[k], x1[k], x1_ready)
                elif stage == "scores":
                    for j in range(PT):
                        dve.wait_ge(mask_ready, PT * k + j + 1)
                        r, h = divmod(j, TILES)
                        dve.wait_ge(scores_done, PT * k + (r + 1) * TILES)
                        v.tensor_tensor_reduce(out=sc[k][:, j, :], in0=(A, B)[r][k][:, h * SEQ:(h + 1) * SEQ],
                                               in1=negmask[k][:, j, :], scale=-SCALE, scalar=3.0e38, op0=ALU.add, op1=ALU.min,
                                               accum_out=negmax[k][:, j:j + 1]).then_inc(sc_ready, 1)
                elif stage == "turn":
                    dve.wait_ge(probT_ready, PAIR * k + 2)
                    v.tensor_copy(prob_T[k][:, 1], B[k][:].rearrange("p (t q) -> p t q", t=TILES)).then_inc(probT_moved[1], 1)
                    made["rsum", k] = step.mark(v.reciprocal(rsum[k][:], prob_sum[k][:]))
                elif stage == "ln2":
                    dve.wait_ge(x1b_ready, k + 1)
                    dve.wait_ge(proj_done, k + 1)
                    dve.wait_ge(vec_step, made["rsum", k])
                    for j in range(PT):
                        n = step.mark(v.scalar_tensor_tensor(pre[k][:, j, :], A[k][:, j * D:(j + 1) * D],
                                                             rsum[k][:, j:j + 1], x1b[k][:, j, :], ALU.mult, ALU.add))
                    layernorm_stats(1, k, pre[k], n)
                elif stage == "x2":
                    layernorm(1, k, pre[k], x2[k], x2_ready)
                elif stage == "x2_lo":
                    dve.wait_ge(x2hi_ready, k + 1)
                    v.scalar_tensor_tensor(x2_lo[:, k], x2_T[k][:].rearrange("p (r t) -> p r t", r=PAIR), X_UP, x2_hi[:, k], ALU.mult,
                                           ALU.subtract).then_inc(x2lo_ready, 1)
                elif stage == "router":
                    dve.wait_ge(logits_done, k + 1)
                    v.tensor_tensor(lg[k][:], A[k][:, 0:PT * EXPERTS].rearrange("p (j e) -> p j e", j=PT),
                                    every_tile(br_bc[:]), ALU.add).then_inc(lg_ready, 1)
                    dve.wait_ge(lg_ready, k + 1)
                    for j in range(PT):
                        n = step.mark(v.max(top[k][:, j, :], lg[k][:, j, :]))
                    dve.wait_ge(vec_step, n)
                    v.tensor_tensor(lgt[k][:], lg[k][:], every_column(top[k][:, :, 0], EXPERTS), ALU.subtract).then_inc(lgt_ready, 1)
                    made["chosen", k] = step.mark(v.tensor_tensor(chosen[k][:], lg[k][:], every_column(top[k][:, :, 1], EXPERTS), ALU.is_ge))
                elif stage == "weigh":
                    dve.wait_ge(tg_ready, k + 1)
                    n = step.mark(v.tensor_scalar(den[k][:], tg[k][:], -1.0, 1.0, ALU.mult, ALU.add))
                    dve.wait_ge(vec_step, n)
                    n = step.mark(v.reciprocal(rden[k][:], den[k][:]))
                    dve.wait_ge(vec_step, n)
                    n = step.mark(v.scalar_tensor_tensor(eg[k][:], tg[k][:], 1.0, rden[k][:], ALU.add, ALU.mult))
                    dve.wait_ge(vec_step, n)
                    n = step.mark(v.tensor_tensor(em[k][:], eg[k][:], chosen[k][:], ALU.mult))
                    dve.wait_ge(vec_step, n)
                    n = step.mark(v.tensor_reduce(esum[k][:], em[k][:], AX, ALU.add))
                    dve.wait_ge(vec_step, n)
                    n = step.mark(v.reciprocal(ersum[k][:], esum[k][:]))
                    dve.wait_ge(vec_step, n)
                    v.tensor_tensor(gate_w[k][:], em[k][:], every_column(ersum[k][:], EXPERTS), ALU.mult).then_inc(gatew_ready, 1)
                    dve.wait_ge(gatew_ready, k + 1)
                    dve.wait_ge(wup_ready, 1)
                    v.tensor_scalar(gate_s[:, k], gate_w[k][:], w_down_scale[:, 1:2], None, ALU.mult).then_inc(gates_ready, 1)
                elif stage == "bias2":
                    dve.wait_ge(b2_done, k + 1)
                    v.tensor_tensor(acc[:, k], tiles(A[k]), x2[k][:], ALU.add).then_inc(acc_started, 1)

            def hidden_high(k, e, c):
                n = (k * EXPERTS + e) * CHUNKS + c
                if not hi_on_act(k, e, c):
                    dve.wait_ge(gelu_done, n + 1)
                    if n >= 2 * CHUNKS:
                        dve.wait_ge(fc2_done, n // CHUNKS - 1)
                    v.tensor_copy(h_hi[:, e % 2, c, :], hid[:, c, :]).then_inc(h_hi_vec, 1)

            def hidden_low(k, e, c):
                n = (k * EXPERTS + e) * CHUNKS + c
                if not lo_on_pool(k, e, c):
                    hi_wait(dve, n)
                    if n >= 2 * CHUNKS:
                        dve.wait_ge(fc2_done, n // CHUNKS - 1)
                    v.tensor_tensor(h_lo[:, e % 2, c, :], hid[:, c, :], h_hi[:, e % 2, c, :],
                                    ALU.subtract).then_inc(h_lo_vec, 1)

            def combine(k, e):
                n = k * EXPERTS + e
                if e == 0:
                    dve.wait_ge(acc_started, k + 1)
                    dve.wait_ge(gates_ready, k + 1)
                dve.wait_ge(fc2_done, n + 1)
                for j in range(PT):
                    if e:
                        dve.wait_ge(combined, PT * (n - 1) + j + 1)
                    v.scalar_tensor_tensor(acc[:, k, j, :], Y[n % YBANKS][:, j, :], gate_s[:, k, j, e:e + 1], acc[:, k, j, :],
                                           ALU.mult, ALU.add).then_inc(combined, 1)

            def final(k):
                dve.wait_ge(combined, PT * EXPERTS * (k + 1))
                for j in range(PT):
                    n = step.mark(v.bn_stats(fbn[:, j, :], acc[:, k, j, :]))
                dve.wait_ge(vec_step, n)
                for j in range(PT):
                    n = step.mark(v.bn_aggr(fmv[:, j, :], fbn[:, j, :]))
                dve.wait_ge(vec_step, n)
                v.tensor_scalar(flnv[:], fmv[:, :, 1], LN_EPS, None, ALU.add).then_inc(ln_var[2], 1)

            def final_apply(k):
                dve.wait_ge(ln_rstd[2], k + 1)
                for j in range(PT):
                    v.tensor_scalar(acc[:, k, j, :], acc[:, k, j, :], fmv[:, j, 0:1], frstd[:, j:j + 1],
                                    ALU.subtract, ALU.mult).then_inc(out_ready, 1)

            for what in order_of("DVE"):
                if what[0] == "ab":
                    ab(*what[1:])
                elif what[0] == "means":
                    ternary_means(*what[1:])
                elif what[0] == "mean_w":
                    ternary_scales(*what[1:])
                elif what[0] == "round":
                    ternary_clip(*what[1:])
                elif what[0] == "turn_w":
                    ternary_move(*what[1:])
                elif what[0] == "turn_small":
                    move_small()
                elif what[0] == "sum_w":
                    weights_power()
                elif what[0] == "total_w":
                    weights_total()
                elif what[0] == "scale_w":
                    weights_scale()
                elif what[0] == "wlow":
                    split_low(*what[1:])
                elif what[0] == "high":
                    hidden_high(*what[1:])
                elif what[0] == "low":
                    hidden_low(*what[1:])
                elif what[0] == "combine":
                    combine(*what[1:])
                elif what[0] == "final":
                    final(*what[1:])
                elif what[0] == "final_apply":
                    final_apply(*what[1:])

        @block.tensor
        def _(pe):
            t_ = nc.tensor
            pe.wait_ge(ident_ready, 1)
            pe.wait_ge(ones_ready, 1)

            def ternary_sums(part):
                pe.wait_ge(wabs_ready, (1, 3)[part])
                cols = ((0, 4), (4, 6))[part]
                if part:
                    pe.wait_ge(wscale_ready, 1)
                t_.matmul(Y[1][:, 0, cols[0]:cols[1]], ones[:], wabs[:, cols[0]:cols[1]], start=True, stop=True).then_inc(wtot_ready, 1)

            def ternary_turn(part):
                if part == 0:
                    for k in range(4):
                        pe.wait_ge(wclip_ready, k + 1)
                        last = t_.transpose(H[0][:, k * D:(k + 1) * D], wmagic[:, k * D:(k + 1) * D], ident[:])
                    last.then_inc(wT_ready, 1)
                    return
                pe.wait_ge(wclip_ready, 6)
                pe.wait_ge(wT_moved, 1)
                for k in range(4):
                    last = t_.transpose(H[1][:, k * P:(k + 1) * P], wmagic[:, GATE_AT + k * D:GATE_AT + (k + 1) * D], ident[:])
                last.then_inc(wT_ready, 1)
                t_.transpose(Y0[:, 0:P], wmagic[:, GATE_AT + 4 * D:GATE_AT + 5 * D], ident[:])
                t_.transpose(Y0[:, P:P + GATE_TAIL], wmagic[0:GATE_TAIL, GATE_AT + 5 * D:GATE_AT + 6 * D],
                             ident[0:GATE_TAIL, 0:GATE_TAIL]).then_inc(wT_ready, 1)
                for c, rows in DOWN:
                    last = t_.transpose(H[0][0:rows, c * D:(c + 1) * D], wmagic[:, DOWN_AT + c * P:DOWN_AT + c * P + rows], ident[:])
                last.then_inc(wT_ready, 1)

            def turn_small():
                pe.wait_ge(small_loaded, 16 * 6)
                pe.wait_ge(wT_moved, 2)
                t_.transpose(H[1][:, 0:D], xw_raw[:], ident[:])
                t_.transpose(H[1][:, D:D + EXPERTS * CHUNKS], b1_rows[:],
                             ident[0:EXPERTS * CHUNKS, 0:EXPERTS * CHUNKS]).then_inc(wT_ready, 1)

            def transpose_tiles(bank, source):
                for j in range(PT):
                    last = t_.transpose(bank[:, j * P:(j + 1) * P], source[:, j, :], ident[:])
                return last

            def ab(k, stage):
                if stage == "ctx":
                    pe.wait_ge(ctx_loaded[k], 16)
                    transpose_tiles(B[k], ctx[:, k]).then_inc(ctxT_ready, 1)
                elif stage == "in_q":
                    pe.wait_ge(q_ready["in"], PT * (k + 1))
                    transpose_tiles(A[k], q["in"][k]).then_inc(qT_ready["in"], 1)
                elif stage == "in_deq":
                    pe.wait_ge(ctxT_moved, k + 1)
                    pe.wait_ge(deq_ready, 2 * k + 1)
                    for j in range(PT):
                        last = t_.matmul(B[k][:, j * P:(j + 1) * P], deq_in[k][:, j:j + 1].to_broadcast([P, P]), ident[:],
                                         start=True, stop=True)
                    last.then_inc(deq_bc_done, 1)
                elif stage == "if":
                    if k == 0:
                        pe.wait_ge(wT_moved, 1)
                    pe.wait_ge(qT_moved["in"], k + 1)
                    pe.wait_ge(deq_bc_moved, k + 1)
                    t_.matmul(B[k][:], attn_T[:, D:2 * D], qT["in"][k][:], start=True, stop=True).then_inc(f_done, 1)
                    t_.matmul(A[k][:], attn_T[:, 0:D], qT["in"][k][:], start=True, stop=True).then_inc(i_done, 1)
                elif stage == "g":
                    pe.wait_ge(uf_ready, k + 1)
                    pe.wait_ge(deq_ready, 2 * k + 2)
                    for j in range(PT):
                        last = t_.matmul(B[k][:, j * D:(j + 1) * D], qT["in"][k][:, j * P:(j + 1) * P],
                                         attn_T[:, 2 * D:3 * D], start=True, stop=True)
                    last.then_inc(g_done, 1)
                elif stage == "o":
                    pe.wait_ge(ui_ready, k + 1)
                    for j in range(PT):
                        if j % TILES == 0:
                            pe.wait_ge(scan_done, PAIR * k + j // TILES + 1)
                        last = t_.transpose(A[k][:, j * P:(j + 1) * P], o_T[k][:, j * P:(j + 1) * P], ident[:])
                    last.then_inc(o_ready, 1)
                elif stage == "out_q":
                    pe.wait_ge(sg_ready, k + 1)
                    pe.wait_ge(q_ready["out"], PT * (k + 1))
                    transpose_tiles(B[k], q["out"][k]).then_inc(qT_ready["out"], 1)
                elif stage == "res":
                    pe.wait_ge(qT_moved["out"], k + 1)
                    for j in range(PT):
                        last = t_.matmul(A[k][:, j * D:(j + 1) * D], qT["out"][k][:, j * P:(j + 1) * P], attn_T[:, 3 * D:4 * D],
                                         start=True, stop=True)
                    last.then_inc(wo_done, 1)
                elif stage == "mlp_q":
                    pe.wait_ge(q_ready["mlp"], PT * (k + 1))
                    transpose_tiles(B[k], q["mlp"][k]).then_inc(qT_ready["mlp"], 1)
                elif stage.startswith("gate"):
                    j = int(stage[-1])
                    n = PT * k + j
                    if j == 0:
                        pe.wait_ge(qT_moved["mlp"], k + 1)
                        if k == 0:
                            pe.wait_ge(wT_moved, 5)
                    else:
                        pe.wait_ge(za_ready, n)
                    t_.matmul(A[k][:, 0:INNER], qT["mlp"][k][:, j * P:(j + 1) * P], gate_T[:, 0:INNER],
                              start=True, stop=True).then_inc(gate_done, 1)
                    if j:
                        pe.wait_ge(z_ready, n)
                    t_.matmul(B[k][:, 0:INNER], qT["mlp"][k][:, j * P:(j + 1) * P], gate_T[:, INNER:GATE_ROWS],
                              start=True, stop=True).then_inc(value_done, 1)
                elif stage.startswith("z_q"):
                    j = int(stage[-1])
                    pe.wait_ge(q_ready["z"], PT * k + j + 1)
                    if j >= 2:
                        pe.wait_ge(qT_moved["z"], PT * k + j - 1)
                    for c, rows in DOWN:
                        last = t_.transpose((A, B)[j % 2][k][0:rows, c * P:(c + 1) * P], q["z"][k][:, j, c * P:c * P + rows], ident[:])
                    last.then_inc(qT_ready["z"], 1)
                elif stage == "down":
                    pe.wait_ge(qT_moved["z"], PT * (k + 1))
                    for j in range(PT):
                        for c, rows in DOWN:
                            last = t_.matmul(A[k][:, j * D:(j + 1) * D], qT_z[k][0:rows, j, c, :], down_T[0:rows, c, :],
                                             start=(c == 0), stop=(c == len(DOWN) - 1))
                    last.then_inc(down_done, 1)
                elif stage == "x1":
                    pe.wait_ge(x1_ready, PT * (k + 1))
                    transpose_tiles(B[k], x1[k]).then_inc(x1T_ready, 1)
                elif stage == "scores":
                    pe.wait_ge(x1T_moved, k + 1)
                    for j in range(PT):
                        r, h = divmod(j, TILES)
                        t_.matmul((A, B)[r][k][:, h * SEQ:(h + 1) * SEQ], x1_T[k][:, j * P:(j + 1) * P],
                                  ctx_T[k][:, r * SEQ:(r + 1) * SEQ], start=True, stop=True).then_inc(scores_done, 1)
                elif stage == "turn":
                    for j in range(PT):
                        r, h = divmod(j, TILES)
                        pe.wait_ge(prob_ready, PT * k + j + 1)
                        if h == 0:
                            pe.wait_ge(sc_ready, PT * k + (r + 1) * TILES)
                        for t in range(TILES):
                            last = t_.transpose((A, B)[r][k][:, t * SEQ + h * P:t * SEQ + (h + 1) * P],
                                                prob[k][:, j, t * P:(t + 1) * P], ident[:])
                        if h == TILES - 1:
                            last.then_inc(probT_ready, 1)
                elif stage == "attend":
                    for r in range(PAIR):
                        pe.wait_ge(probT_moved[r], k + 1)
                        for t in range(TILES):
                            last = t_.matmul((A, B)[r][k][:, 0:SEQ], ctx[:, k, r * TILES + t, :], prob_T[k][:, r, t, :],
                                             start=(t == 0), stop=(t == TILES - 1))
                        last.then_inc(att_done, 1)
                elif stage == "ln2":
                    pe.wait_ge(attT_moved, PAIR * (k + 1))
                    for j in range(PT):
                        last = t_.matmul(A[k][:, j * D:(j + 1) * D], att_T[k][:, j * P:(j + 1) * P], xw_T[:], start=True, stop=True)
                    last.then_inc(proj_done, 1)
                elif stage == "x2":
                    pe.wait_ge(x2_ready, PT * (k + 1))
                    transpose_tiles(B[k], x2[k]).then_inc(x2T_ready, 1)
                elif stage == "router":
                    pe.wait_ge(x2T_moved, k + 1)
                    for j in range(PT):
                        last = t_.matmul(A[k][:, j * EXPERTS:(j + 1) * EXPERTS], x2_T[k][:, j * P:(j + 1) * P], wr_sb[:],
                                         start=True, stop=True)
                    last.then_inc(logits_done, 1)
                elif stage == "turn_gates":
                    pe.wait_ge(gatew_ready, k + 1)
                    for j in range(PT):
                        last = t_.transpose(B[k][0:EXPERTS, j * P:(j + 1) * P], gate_w[k][:, j, :], ident[:])
                    last.then_inc(gwT_ready, 1)
                elif stage == "bias2":
                    pe.wait_ge(gwT_moved, k + 1)
                    for j in range(PT):
                        last = t_.matmul(A[k][:, j * D:(j + 1) * D], gate_wT[k][:, j * P:(j + 1) * P], b2_sb[:], start=True, stop=True)
                    last.then_inc(b2_done, 1)

            def weights_sum():
                pe.wait_ge(wsum_ready, 1)
                pe.wait_ge(wscale_ready, 2)
                t_.matmul(Y[1][:, 0, 0:2], ones[:], w_sum[:], start=True, stop=True).then_inc(wsum_done, 1)

            def fc1(k, e, c):
                n = (k * EXPERTS + e) * CHUNKS + c
                if c == 0:
                    if k == 0:
                        pe.wait_ge(w_lo_ready[0], e + 1)
                    if e == 0:
                        pe.wait_ge(x2lo_ready, k + 1)
                hi = x2_hi[:, k].rearrange("p r t -> p (r t)")
                lo = x2_lo[:, k].rearrange("p r t -> p (r t)")
                if n >= HBANKS:
                    pe.wait_ge(gelu_done, n - HBANKS + 1)
                cols = slice(c * P, (c + 1) * P)
                bank = H[n % HBANKS]
                t_.matmul(bank[:], w_hi[0][:, e, cols], hi, start=True, stop=False)
                t_.matmul(bank[:], w_hi[0][:, e, cols], lo, start=False, stop=False)
                t_.matmul(bank[:], w_lo[0][:, e, cols], hi, start=False, stop=True).then_inc(fc1_done, 1)

            def fc2(k, e, j):
                n = k * EXPERTS + e
                if j == 0:
                    if k == 0:
                        pe.wait_ge(w_lo_ready[1], e + 1)
                    if n == 1:
                        pe.wait_ge(wtot_moved, 1)
                    if n >= YBANKS:
                        pe.wait_ge(combined, PT * (n - YBANKS + 1))
                    for c in range(CHUNKS):
                        lo_wait(pe, n * CHUNKS + c)
                cols = slice(j * P, (j + 1) * P)
                bank = Y[n % YBANKS]
                for c in range(CHUNKS):
                    rows = slice(c * D, (c + 1) * D)
                    t_.matmul(bank[:, j, :], h_hi[:, e % 2, c, cols], w_hi[1][:, e, rows], start=(c == 0), stop=False)
                    t_.matmul(bank[:, j, :], h_hi[:, e % 2, c, cols], w_lo[1][:, e, rows], start=False, stop=False)
                    last = t_.matmul(bank[:, j, :], h_lo[:, e % 2, c, cols], w_hi[1][:, e, rows], start=False,
                                     stop=(c == CHUNKS - 1))
                if j == PT - 1:
                    last.then_inc(fc2_done, 1)

            for what in order_of("PE"):
                if what[0] == "ab":
                    ab(*what[1:])
                elif what[0] == "means":
                    ternary_sums(*what[1:])
                elif what[0] == "turn_w":
                    ternary_turn(*what[1:])
                elif what[0] == "turn_small":
                    turn_small()
                elif what[0] == "sum_w":
                    weights_sum()
                elif what[0] == "fc1":
                    fc1(*what[1:])
                elif what[0] == "fc2":
                    fc2(*what[1:])


_NAMES = ["x", "ctx_1024", "_lenS2", "L0_attn_lower_bound", "L0_attn_attn_norm_w", "L0_attn_w_i", "L0_attn_w_f",
          "L0_attn_w_g", "L0_attn_g_norm_w", "L0_attn_w_o", "L0_attn_mlp_norm_w", "L0_attn_w_gate",
          "L0_attn_w_down", "L0_xattn_W", "L0_xattn_b", "L0_ffn_W1", "L0_ffn_b1", "L0_ffn_W2", "L0_ffn_b2",
          "L0_ffn_Wr", "L0_ffn_br"]


def kernel(**inputs):
    import numpy as np
    import concourse.bacc as bacc
    from concourse.bass_utils import run_bass_kernel_spmd

    nc = bacc.Bacc("TRN2", target_bir_lowering=False, num_devices=1)
    arrays, args = {}, []
    for name in _NAMES:
        a = np.ascontiguousarray(inputs[name])
        arrays[f"in_{name}"] = a
        args.append(nc.dram_tensor(f"in_{name}", a.shape, mybir.dt.from_np(a.dtype), kind="ExternalInput").ap())
    out = nc.dram_tensor("out", (BATCH, SEQ, D), mybir.dt.float32, kind="ExternalOutput")
    decoder_layer(nc, *args, out.ap())
    result = run_bass_kernel_spmd(nc, [arrays], core_ids=[0])
    return result.results[0]["out"]
```

```python
import concourse.bass as bass
from concourse import mybir
from contextlib import ExitStack

BATCH, SEQ, D = 4, 256, 128
P = 128
TILES = SEQ // P
INNER = 352
EXPERTS, HIDDEN = 8, 512
CHUNKS = HIDDEN // P
BITLINEAR = ("w_i", "w_f", "w_g", "w_o")
EPS = 1e-6
LN_EPS = 1e-5
CLIP = 1e-5
QMAX = 127.0
ROUND = 1.5 * 2.0 ** 23
SCALE = float(D) ** -0.5
NEG = -1e13


PAIR, PAIRS, HBANKS, YBANKS = 2, BATCH // 2, 2, 2
WLOAD = 2
LOADS = EXPERTS // WLOAD
NORM_GROUPS = 2
PT = PAIR * TILES
TERNARY = ((0, 1, 2, 3), (4, 5))
X_UP = 2.0 ** 11
W_TARGET = 2.0 ** 13
FC2_LAG, GELU_LAG, HIGH_LAG, LOW_LAG = 7, 1, 2, 3
STAGES = ("ctx", "in_u", "in_peak", "in_var", "in_q", "in_deq", "if", "sigmoids", "g", "swish", "scan", "gain", "o",
          "out_peak", "out_var", "out_q", "res", "mlp_peak", "mlp_var", "mlp_q", "gate0", "gate1", "zsq0", "gate2", "zsq1",
          "gate3", "zsq2", "zsq3", "z_var", "z_inv", "quant_z", "z_q0", "z_q1", "z_q2", "z_q3", "down", "x1", "scores", "softmax", "turn",
          "attend", "ln2", "x2", "x2_lo", "router", "weigh", "turn_gates", "bias2")


def product_on_pool(k):
    return k == 1


def hi_on_act(k, e, c):
    return k == 1


def lo_on_pool(k, e, c):
    if k == 0:
        return c % 2 == 0 if e == 0 else c < 3
    return c % 2 == 0 and e < EXPERTS - 1


def hi_counts(n):
    made = [hi_on_act(m // CHUNKS // EXPERTS, m // CHUNKS % EXPERTS, m % CHUNKS) for m in range(n + 1)]
    return sum(made), len(made) - sum(made), made[-1]


def lo_counts(n):
    made = [lo_on_pool(m // CHUNKS // EXPERTS, m // CHUNKS % EXPERTS, m % CHUNKS) for m in range(n + 1)]
    return sum(made), len(made) - sum(made), made[-1]


ORDER = {
    "PE": """
        means:0 ctx:0 turn_w:0 means:1 ctx:1 in_q:0 in_deq:0 turn_w:1 in_q:1 in_deq:1 if:0 g:0 if:1 g:1 turn_small
        sum_w:0 o:0 o:1 out_q:0 out_q:1 res:0 res:1 sum_w:1 mlp_q:0 gate0:0 mlp_q:1 gate1:0 gate2:0 gate3:0 gate0:1
        gate1:1 gate2:1 z_q0:0 z_q1:0 gate3:1 z_q2:0 z_q3:0 down:0 z_q0:1 z_q1:1 x1:0 z_q2:1 z_q3:1 scores:0 down:1
        turn:0 attend:0 ln2:0 x1:1 scores:1 turn:1 x2:0 attend:1 router:0 fc1:0:0:0 fc1:0:0:1 ln2:1 turn_gates:0
        fc1:0:0:2 fc1:0:0:3 bias2:0 fc1:0:1:0 fc1:0:1:1 x2:1 fc1:0:1:2 fc1:0:1:3 router:1 fc2:0:0:0 fc2:0:0:1
        fc1:0:2:0 fc2:0:0:2 fc1:0:2:1 fc2:0:0:3 fc1:0:2:2 fc1:0:2:3 fc2:0:1:0 fc2:0:1:1 fc1:0:3:0 fc2:0:1:2
        fc1:0:3:1 fc2:0:1:3 fc1:0:3:2 fc1:0:3:3 fc2:0:2:0 fc2:0:2:1 fc1:0:4:0 fc2:0:2:2 fc1:0:4:1 fc2:0:2:3
        fc1:0:4:2 fc1:0:4:3 fc2:0:3:0 fc2:0:3:1 fc1:0:5:0 fc2:0:3:2 fc1:0:5:1 fc2:0:3:3 fc1:0:5:2 fc1:0:5:3
        fc2:0:4:0 fc2:0:4:1 fc1:0:6:0 fc2:0:4:2 fc1:0:6:1 fc2:0:4:3 fc1:0:6:2 fc1:0:6:3 fc2:0:5:0 fc2:0:5:1
        fc1:0:7:0 fc2:0:5:2 fc1:0:7:1 fc2:0:5:3 turn_gates:1 fc1:0:7:2 fc1:0:7:3 bias2:1 fc2:0:6:0 fc1:1:0:0
        fc2:0:6:1 fc1:1:0:1 fc2:0:6:2 fc2:0:6:3 fc1:1:0:2 fc1:1:0:3 fc2:0:7:0 fc1:1:1:0 fc2:0:7:1 fc1:1:1:1
        fc2:0:7:2 fc2:0:7:3 fc1:1:1:2 fc1:1:1:3 fc2:1:0:0 fc1:1:2:0 fc2:1:0:1 fc1:1:2:1 fc2:1:0:2 fc2:1:0:3
        fc1:1:2:2 fc1:1:2:3 fc2:1:1:0 fc1:1:3:0 fc2:1:1:1 fc1:1:3:1 fc2:1:1:2 fc2:1:1:3 fc1:1:3:2 fc1:1:3:3
        fc2:1:2:0 fc1:1:4:0 fc2:1:2:1 fc1:1:4:1 fc2:1:2:2 fc2:1:2:3 fc1:1:4:2 fc1:1:4:3 fc2:1:3:0 fc1:1:5:0
        fc2:1:3:1 fc1:1:5:1 fc2:1:3:2 fc2:1:3:3 fc1:1:5:2 fc1:1:5:3 fc2:1:4:0 fc1:1:6:0 fc2:1:4:1 fc1:1:6:1
        fc2:1:4:2 fc2:1:4:3 fc1:1:6:2 fc1:1:6:3 fc2:1:5:0 fc1:1:7:0 fc2:1:5:1 fc1:1:7:1 fc2:1:5:2 fc2:1:5:3
        fc1:1:7:2 fc1:1:7:3 fc2:1:6:0 fc2:1:6:1 fc2:1:6:2 fc2:1:6:3 fc2:1:7:0 fc2:1:7:1 fc2:1:7:2 fc2:1:7:3""",
    "ACT": """
        round:0 ctx:0 in_u:0 ctx:1 in_u:1 round:1 in_q:0 wsquare:0:0 in_deq:0 wsquare:1:0 wsquare:0:1 in_q:1
        in_deq:1 wsquare:1:1 sigmoids:0 sigmoids:1 g:0 g:1 wsquare:0:2 wsquare:1:2 o:0 o:1 out_var:0 out_var:1
        wscale:0 whigh:0:0 whigh:1:0 out_q:0 whigh:0:1 out_q:1 wsquare:0:3 wscale:1 res:0 res:1 mlp_var:0 mlp_var:1
        wsquare:1:3 whigh:1:1 mlp_q:0 gate0:0 mlp_q:1 gate1:0 zsq0:0 whigh:0:2 gate2:0 zsq1:0 wscale:2 whigh:1:2
        gate3:0 zsq2:0 gate0:1 whigh:0:3 zsq3:0 wscale:3 gate1:1 zsq0:1 whigh:1:3 quant_z:0 gate2:1 zsq1:1 z_q0:0
        z_q1:0 gate3:1 zsq2:1 z_q2:0 zsq3:1 z_q3:0 quant_z:1 z_q0:1 z_q1:1 x1:0 z_q2:1 z_q3:1 softmax:0 turn:0
        attend:0 x1:1 softmax:1 turn:1 x2:0 attend:1 router:0 gelu:0:0:0 gelu:0:0:1 turn_gates:0 gelu:0:0:2
        gelu:0:0:3 gelu:0:1:0 gelu:0:1:1 x2:1 gelu:0:1:2 gelu:0:1:3 gelu:0:2:0 router:1 gelu:0:2:1 gelu:0:2:2
        gelu:0:2:3 gelu:0:3:0 gelu:0:3:1 gelu:0:3:2 gelu:0:3:3 gelu:0:4:0 gelu:0:4:1 gelu:0:4:2 gelu:0:4:3
        gelu:0:5:0 gelu:0:5:1 gelu:0:5:2 gelu:0:5:3 gelu:0:6:0 gelu:0:6:1 gelu:0:6:2 gelu:0:6:3 gelu:0:7:0
        gelu:0:7:1 turn_gates:1 gelu:0:7:2 gelu:0:7:3 gelu:1:0:0 gelu:1:0:1 high:1:0:0 gelu:1:0:2 gelu:1:0:3
        high:1:0:1 high:1:0:2 gelu:1:1:0 gelu:1:1:1 high:1:0:3 high:1:1:0 gelu:1:1:2 gelu:1:1:3 high:1:1:1
        high:1:1:2 gelu:1:2:0 high:1:1:3 gelu:1:2:1 high:1:2:0 gelu:1:2:2 gelu:1:2:3 high:1:2:1 high:1:2:2
        gelu:1:3:0 gelu:1:3:1 high:1:2:3 high:1:3:0 gelu:1:3:2 gelu:1:3:3 high:1:3:1 high:1:3:2 gelu:1:4:0
        gelu:1:4:1 high:1:3:3 high:1:4:0 gelu:1:4:2 gelu:1:4:3 high:1:4:1 high:1:4:2 gelu:1:5:0 gelu:1:5:1
        high:1:4:3 high:1:5:0 gelu:1:5:2 gelu:1:5:3 high:1:5:1 high:1:5:2 gelu:1:6:0 high:1:5:3 gelu:1:6:1
        high:1:6:0 gelu:1:6:2 gelu:1:6:3 high:1:6:1 high:1:6:2 gelu:1:7:0 high:1:6:3 gelu:1:7:1 high:1:7:0
        gelu:1:7:2 high:1:7:1 gelu:1:7:3 high:1:7:2 high:1:7:3""",
    "DVE": """
        in_u:0 means:0 mean_w:0 round:0 means:1 in_peak:0 in_peak:1 in_var:0 turn_w:0 mean_w:1 in_q:0 in_var:1
        in_deq:0 round:1 in_q:1 in_deq:1 turn_w:1 if:0 if:1 swish:0 turn_small swish:1 total_w:0 scan:0 scan:1
        gain:0 gain:1 scale_w:0 o:0 out_peak:0 o:1 out_var:0 out_peak:1 out_var:1 out_q:0 out_q:1 wlow:0:0 res:0
        res:1 wlow:0:1 mlp_peak:0 mlp_peak:1 mlp_var:0 mlp_var:1 mlp_q:0 total_w:1 mlp_q:1 gate0:0 scale_w:1 gate1:0
        zsq0:0 wlow:0:2 gate2:0 zsq1:0 gate3:0 zsq2:0 zsq3:0 gate0:1 z_var:0 wlow:0:3 z_inv:0 gate1:1 quant_z:0
        zsq0:1 gate2:1 zsq1:1 gate3:1 zsq2:1 zsq3:1 z_var:1 down:0 z_inv:1 quant_z:1 x1:0 scores:0 down:1 turn:0
        x1:1 ln2:0 scores:1 x2:0 turn:1 x2_lo:0 router:0 weigh:0 ln2:1 high:0:0:0 bias2:0 scale_gates:0:0 high:0:0:1
        x2:1 low:0:0:1 high:0:0:2 high:0:0:3 high:0:1:0 low:0:0:3 high:0:1:1 scale_gates:0:1 x2_lo:1 high:0:1:2
        router:1 high:0:1:3 low:0:1:3 weigh:1 high:0:2:0 high:0:2:1 high:0:2:2 high:0:2:3 combine:0:0 low:0:2:3
        scale_gates:1:0 scale_gates:1:1 high:0:3:0 high:0:3:1 high:0:3:2 high:0:3:3 combine:0:1 low:0:3:3 high:0:4:0
        high:0:4:1 high:0:4:2 high:0:4:3 combine:0:2 low:0:4:3 high:0:5:0 high:0:5:1 high:0:5:2 high:0:5:3
        combine:0:3 low:0:5:3 high:0:6:0 high:0:6:1 high:0:6:2 high:0:6:3 combine:0:4 low:0:6:3 high:0:7:0
        high:0:7:1 combine:0:5 high:0:7:2 high:0:7:3 bias2:1 low:0:7:3 combine:0:6 low:1:0:1 low:1:0:3 combine:0:7
        final:0 low:1:1:1 low:1:1:3 combine:1:0 final_apply:0 low:1:2:1 low:1:2:3 combine:1:1 low:1:3:1 low:1:3:3
        combine:1:2 low:1:4:1 low:1:4:3 combine:1:3 low:1:5:1 low:1:5:3 combine:1:4 low:1:6:1 low:1:6:3 low:1:7:0
        combine:1:5 low:1:7:1 low:1:7:2 low:1:7:3 combine:1:6 combine:1:7 final:1 final_apply:1""",
    "Pool": """
        in_u:1 masks:0:0 masks:0:1 in_var:0 masks:0:2 in_var:1 masks:0:3 masks:1:0 masks:1:1 masks:1:2 masks:1:3
        swish:1 root_w:0 gain:0 gain:1 out_var:0 out_var:1 wlow:1:0 res:1 mlp_var:0 mlp_var:1 root_w:1 wlow:1:1
        wlow:1:2 z_var:0 wlow:1:3 z_var:1 down:0 x1:0 down:1 x1:1 ln2:0 ln2:1 low:0:0:0 low:0:0:2 low:0:1:0
        low:0:1:1 low:0:1:2 low:0:2:0 low:0:2:1 low:0:2:2 low:0:3:0 low:0:3:1 low:0:3:2 low:0:4:0 low:0:4:1
        low:0:4:2 low:0:5:0 low:0:5:1 low:0:5:2 low:0:6:0 low:0:6:1 low:0:6:2 low:0:7:0 low:0:7:1 low:0:7:2
        low:1:0:0 low:1:0:2 low:1:1:0 low:1:1:2 final:0 low:1:2:0 low:1:2:2 low:1:3:0 low:1:3:2 low:1:4:0 low:1:4:2
        low:1:5:0 low:1:5:2 low:1:6:0 low:1:6:2 final:1""",
}


def order_of(engine):
    for word in ORDER[engine].split():
        name, *numbers = word.split(":")
        numbers = [int(n) for n in numbers]
        yield ("ab", *numbers, name) if name in STAGES else (name, *numbers)


class Steps:

    def __init__(self, sem):
        self.sem, self.count = sem, 0

    def mark(self, instruction):
        instruction.then_inc(self.sem, 1)
        self.count += 1
        return self.count


def decoder_layer(nc, x, ctx_mem, pads, lower_bound, attn_norm_w, w_i, w_f, w_g, g_norm_w, w_o,
                  mlp_norm_w, w_gate, w_down, xattn_w, xattn_b, w1, b1, w2, b2, wr, br, out):
    fp32, bf16, fp16, int32 = mybir.dt.float32, mybir.dt.bfloat16, mybir.dt.float16, mybir.dt.int32
    ALU, ACT, AX = mybir.AluOpType, mybir.ActivationFunctionType, mybir.AxisListType.X
    AXY = mybir.AxisListType.XY

    GATE_ROWS = 2 * INNER
    GATE_BLOCKS = -(-GATE_ROWS // P)
    GATE_TAIL = GATE_ROWS - (GATE_BLOCKS - 1) * P
    DOWN = [(c, min(P, INNER - c * P)) for c in range(-(-INNER // P))]
    WCOLS = 4 * D + GATE_BLOCKS * D + INNER
    WEIGHT_COLS = [(k * D, (k + 1) * D) for k in range(4)] + [(4 * D, 4 * D + GATE_BLOCKS * D), (WCOLS - INNER, WCOLS)]

    stack = ExitStack()
    with stack:
        def sb(name, shape, dt=fp32):
            return stack.enter_context(nc.sbuf_tensor(name, shape, dt))

        def pb(name, shape, dt=fp32):
            return stack.enter_context(nc.psum_tensor(name, shape, dt))

        def sem(name):
            return stack.enter_context(nc.semaphore(name))

        ident = sb("ident", [P, P])
        ones = sb("ones", [P, P])
        half = sb("half", [P, PT])
        minus_half = sb("minus_half", [P, PT])
        qpos = sb("qpos", [P, TILES])
        kpos = sb("kpos", [P, SEQ])
        qpos_i = sb("qpos_i", [P, TILES], int32)
        kpos_i = sb("kpos_i", [P, SEQ], int32)
        round_up = sb("round_up", [P, 1])
        wraw = sb("wraw", [P, WCOLS])
        wmagic = wraw
        GATE_AT, DOWN_AT = 4 * D, 4 * D + GATE_BLOCKS * D
        attn_raw = wraw[:, 0:GATE_AT].rearrange("p (k d) -> p k d", k=4)
        gate_raw = wraw[:, GATE_AT:DOWN_AT].rearrange("p (k d) -> p k d", k=GATE_BLOCKS)
        down_raw = wraw[:, DOWN_AT:WCOLS]
        attn_T = sb("attn_T", [P, 4 * D], bf16)
        gate_T = sb("gate_T", [P, GATE_ROWS], bf16)
        down_T = sb("down_T", [P, len(DOWN), D], bf16)
        wabs = sb("wabs", [P, 6])
        wmean = sb("wmean", [P, 6])
        wscale = sb("wscale", [P, 6])
        half_mean = sb("half_mean", [P, 2])
        omf_bias = sb("omf_bias", [P, 1])
        omf_scale = sb("omf_scale", [P, 1])
        norm_w = sb("norm_w", [P, 3, D])
        gw_half = sb("gw_half", [P, D])
        xb_bias = sb("xb_bias", [P, D])
        br_bc = sb("br_bc", [P, EXPERTS])
        lb = sb("lb", [P, 1])
        f_gain = sb("f_gain", [P, 1])
        f_base = sb("f_base", [P, 1])
        xw_raw = sb("xw_raw", [P, D])
        xw_T = sb("xw_T", [P, D])
        wr_sb = sb("wr_sb", [P, EXPERTS])
        b2_sb = sb("b2_sb", [EXPERTS, D])
        b1_rows = sb("b1_rows", [EXPERTS * CHUNKS, P])
        b1_T = sb("b1_T", [P, EXPERTS * CHUNKS])
        w_sb = [sb(f"w{m}_sb", [P, EXPERTS, HIDDEN]) for m in (1, 2)]
        w_hi = [sb(f"w{m}_hi", [P, EXPERTS, HIDDEN], fp16) for m in (1, 2)]
        w_lo = [sb(f"w{m}_lo", [P, EXPERTS, HIDDEN], fp16) for m in (1, 2)]
        w_scaled = sb("w_scaled", [P, WLOAD, HIDDEN])
        NORM_SHAPE = [P, NORM_GROUPS, 2, LOADS // NORM_GROUPS]
        w_sumsq, w_total, w_norm, w_power, w_up, w_in_scale = (
            sb(name, NORM_SHAPE) for name in ("w_sumsq", "w_total", "w_norm", "w_power", "w_up", "w_in_scale"))
        w_out_scale = sb("w_out_scale", [P, EXPERTS])
        xt = sb("xt", [P, PAIRS, PT, D])
        ctx = sb("ctx", [P, PAIRS, PT, D])
        pad_i = sb("pad_i", [P, BATCH], int32)
        pad_f = sb("pad_f", [P, BATCH])

        def pairs(name, shape, dt=fp32):
            return [sb(f"{name}_{k}", shape, dt) for k in range(PAIRS)]

        qneg = pairs("qneg", [P, PT])
        negmask = pairs("negmask", [P, PT, SEQ])
        NORMS = ("in", "out", "mlp", "z")
        stat = [{t: {n: sb(f"{n}_{t}_{k}", [P, PT]) for n in
                     ("ssx", "ssu", "peak", "peakq", "tail", "var", "root", "step", "inv", "rroot")}
                 for t in NORMS} for k in range(PAIRS)]
        gss = pairs("gss", [P, PT])
        ginv = pairs("ginv", [P, PT])
        junk = pairs("junk", [P, 2, PT, D], bf16)
        u = pairs("u", [P, PT, D])
        q_d = pairs("q_d", [P, PT, D])
        qT_d = pairs("qT_d", [P, PT * P], bf16)
        qT = {"in": qT_d, "out": qT_d, "mlp": qT_d}
        qT_z = pairs("qT_z", [P, PT, len(DOWN), P], bf16)
        deq_in = pairs("deq_in", [P, PT])
        deq_g = pairs("deq_g", [P, PT])
        deq_gh = pairs("deq_gh", [P, PT])
        deq_gg = pairs("deq_gg", [P, PT])
        deq_bc = pairs("deq_bc", [P, PT * P])
        wide = pairs("wide", [P, 2 * PT * INNER])
        uf, ui, f_T, th_i, th_g = ([wide[k][:, n * PT * P:(n + 1) * PT * P] for k in range(PAIRS)] for n in range(5))
        th_g = [b.rearrange("p (j d) -> p j d", j=PT) for b in th_g]
        zt, q_z = ([wide[k][:, n * PT * INNER:(n + 1) * PT * INNER].rearrange("p (j n) -> p j n", j=PT)
                    for k in range(PAIRS)] for n in range(2))
        q = {"in": q_d, "out": q_d, "mlp": q_d, "z": q_z}
        th_f = f_T
        omf_T = uf
        i_T = th_i
        sg2 = gain = th_g
        o_T = deq_bc
        deq_o = pairs("deq_o", [P, PT])
        res = pairs("res", [P, PT, D])
        xres = [xt[:, k] for k in range(PAIRS)]
        deqh = pairs("deqh", [P, PT])
        deqg = pairs("deqg", [P, PT])
        deqgg = pairs("deqgg", [P, PT])
        za = z = zt
        deq_z = pairs("deq_z", [P, PT])
        pre = u
        bn = [pairs(f"bn{n}", [P, PT, 6]) for n in range(2)]
        mv = [pairs(f"mv{n}", [P, PT, 2]) for n in range(2)]
        lnv = [pairs(f"lnv{n}", [P, PT]) for n in range(2)]
        rstd = [pairs(f"rstd{n}", [P, PT]) for n in range(2)]
        x1 = q_d
        x1b = res
        x1_T = pairs("x1_T", [P, PT * P])
        ctx_T = pairs("ctx_T", [P, PT * P])
        sc = prob = negmask
        negmax = pairs("negmax", [P, PT])
        prob_sum = pairs("prob_sum", [P, PT])
        rsum = pairs("rsum", [P, PT])
        prob_T = [zt[k][:].rearrange("p j n -> p (j n)")[:, 0:PT * SEQ].rearrange("p (r t q) -> p r t q", r=PAIR, t=TILES)
                  for k in range(PAIRS)]
        att_T = deq_bc
        x2 = xres
        x2_T = x1_T
        lg = pairs("lg", [P, PT, EXPERTS])
        top = pairs("top", [P, PT, 8])
        lgt = pairs("lgt", [P, PT, EXPERTS])
        tg = pairs("tg", [P, PT, EXPERTS])
        den = pairs("den", [P, PT, EXPERTS])
        rden = pairs("rden", [P, PT, EXPERTS])
        eg = pairs("eg", [P, PT, EXPERTS])
        chosen = pairs("chosen", [P, PT, EXPERTS])
        em = pairs("em", [P, PT, EXPERTS])
        esum = pairs("esum", [P, PT])
        ersum = pairs("ersum", [P, PT])
        gate_w = pairs("gate_w", [P, PT, EXPERTS])
        gate_wT = [x1b[k][0:EXPERTS].rearrange("e j d -> e (j d)") for k in range(PAIRS)]
        x2_hi = sb("x2_hi", [P, PAIRS, PAIR, SEQ], fp16)
        x2_lo = sb("x2_lo", [P, PAIRS, PAIR, SEQ], fp16)
        gate_s = sb("gate_s", [P, PAIRS, PT, EXPERTS])
        acc = sb("acc", [P, PAIRS, PT, D])
        hid = sb("hid", [P, CHUNKS, PAIR * SEQ])
        h_hi = sb("h_hi", [P, 2, CHUNKS, PAIR * SEQ], fp16)
        h_lo = sb("h_lo", [P, 2, CHUNKS, PAIR * SEQ], fp16)
        fbn = sb("fbn", [P, PT, 6])
        fmv = sb("fmv", [P, PT, 2])
        flnv = sb("flnv", [P, PT])
        frstd = sb("frstd", [P, PT])
        fexp = sb("fexp", [P, PT])

        A = [pb(f"A{s}", [P, 512]) for s in range(PAIRS)]
        B = [pb(f"B{s}", [P, 512]) for s in range(PAIRS)]
        H = [pb(f"H{k}", [P, PAIR * SEQ]) for k in range(HBANKS)]
        Y = [pb(f"Y{k}", [P, PT, D]) for k in range(YBANKS)]

        Y0 = Y[0][:].rearrange("p j d -> p (j d)")

        x_loaded, ctx_loaded = [sem(f"x_loaded{k}") for k in range(PAIRS)], [sem(f"ctx_loaded{k}") for k in range(PAIRS)]
        pad_loaded = sem("pad_loaded")
        wattn_loaded, wgate_loaded, wdown_loaded = sem("wattn_loaded"), sem("wgate_loaded"), sem("wdown_loaded")
        lb_loaded, small_loaded = sem("lb_loaded"), sem("small_loaded")
        norm_loaded = [sem(f"norm_loaded{n}") for n in range(3)]
        w_loaded = [[sem(f"w{m}_loaded{n}") for n in range(EXPERTS // WLOAD)] for m in (1, 2)]
        stored = sem("stored")
        pad_zeroed, pool_step, ident_ready, ones_ready = (
            sem("pad_zeroed"), sem("pool_step"), sem("ident_ready"), sem("ones_ready"))
        wabs_ready, wtot_ready, wscale_ready = sem("wabs_ready"), sem("wtot_ready"), sem("wscale_ready")
        wmagic_ready, wclip_ready, wT_ready, wT_moved = (
            sem("wmagic_ready"), sem("wclip_ready"), sem("wT_ready"), sem("wT_moved"))
        wsq_ready, wnorm_ready, wup_ready = sem("wsq_ready"), sem("wnorm_ready"), sem("wup_ready")
        wsum_done, wtot_moved = sem("wsum_done"), sem("wtot_moved")
        w_scaled_ready = sem("w_scaled_ready")
        w_hi_ready = [sem(f"w{m}_hi_ready") for m in (1, 2)]
        w_lo_ready = [sem(f"w{m}_lo_ready") for m in (1, 2)]
        vec_step, omf_set = sem("vec_step"), sem("omf_set")
        u_ready = {t: sem(f"u_ready_{t}") for t in NORMS}
        squares = {into: {t: sem(f"squares_{into}_{t}") for t in NORMS} for into in ("ssx", "ssu")}
        var_ready = {t: sem(f"var_ready_{t}") for t in NORMS}
        root_ready = {t: sem(f"root_ready_{t}") for t in NORMS}
        q_ready = {t: sem(f"q_ready_{t}") for t in NORMS}
        qT_ready = {t: sem(f"qT_ready_{t}") for t in NORMS}
        qT_moved = {t: sem(f"qT_moved_{t}") for t in NORMS}
        deq_ready, deq_bc_done, deq_bc_moved = sem("deq_ready"), sem("deq_bc_done"), sem("deq_bc_moved")
        f_done, i_done, g_done, uf_ready, ui_ready = sem("f_done"), sem("i_done"), sem("g_done"), sem("uf_ready"), sem("ui_ready")
        thf_ready, omf_ready, thi_ready = sem("thf_ready"), sem("omf_ready"), sem("thi_ready")
        thg_ready, sg_ready, gain_ready = sem("thg_ready"), sem("sg_ready"), sem("gain_ready")
        si_ready, iT_ready = sem("si_ready"), sem("iT_ready")
        scan_done, o_ready, wo_done = sem("scan_done"), sem("o_ready"), sem("wo_done")
        res_ready, xres_ready, deqh_ready = sem("res_ready"), sem("xres_ready"), sem("deqh_ready")
        gate_done, value_done, zt_ready = sem("gate_done"), sem("value_done"), sem("zt_ready")
        inv_ready, qz_vec, qz_act = sem("inv_ready"), sem("qz_vec"), sem("qz_act")
        za_ready, z_ready, down_done = sem("za_ready"), sem("z_ready"), sem("down_done")
        ln_var, ln_rstd = [sem(f"ln_var{n}") for n in range(3)], [sem(f"ln_rstd{n}") for n in range(3)]
        x1_ready, x1b_ready, x1T_ready, x1T_moved = sem("x1_ready"), sem("x1b_ready"), sem("x1T_ready"), sem("x1T_moved")
        ctxT_ready, ctxT_moved = sem("ctxT_ready"), sem("ctxT_moved")
        mask_ready, scores_done, sc_ready, prob_ready = sem("mask_ready"), sem("scores_done"), sem("sc_ready"), sem("prob_ready")
        probT_ready, att_done, attT_moved, proj_done = (
            sem("probT_ready"), sem("att_done"), sem("attT_moved"), sem("proj_done"))
        probT_moved = sem("probT_moved")
        x2_ready, x2T_ready, x2T_moved = sem("x2_ready"), sem("x2T_ready"), sem("x2T_moved")
        gates_ready = sem("gates_ready")
        x2hi_ready, x2lo_ready = sem("x2hi_ready"), sem("x2lo_ready")
        logits_done, lg_ready, lgt_ready, tg_ready, gatew_ready = (
            sem("logits_done"), sem("lg_ready"), sem("lgt_ready"), sem("tg_ready"), sem("gatew_ready"))
        gwT_ready, gwT_moved, b2_done, acc_started = sem("gwT_ready"), sem("gwT_moved"), sem("b2_done"), sem("acc_started")
        fc1_done, gelu_done, h_hi_act, h_hi_vec, h_lo_pool, h_lo_vec, fc2_done, combined = (
            sem("fc1_done"), sem("gelu_done"), sem("h_hi_act"), sem("h_hi_vec"), sem("h_lo_pool"), sem("h_lo_vec"), sem("fc2_done"), sem("combined"))
        out_ready = sem("out_ready")

        block = stack.enter_context(nc.Block())

        def tiles_of(dram, g):
            return dram[g].rearrange("(j p) d -> p j d", p=P)

        def flat(block):
            return block.rearrange("p a b -> p (a b)")

        def tiles(bank):
            return bank[:].rearrange("p (j d) -> p j d", j=PT)

        def rows_of(dram, k):
            return dram[PAIR * k:PAIR * (k + 1)].rearrange("r (j p) d -> p (r j) d", p=P)

        def every_tile(row):
            return row.unsqueeze(1).to_broadcast([P, PT, row.shape[1]])

        def every_column(col, n):
            return col.unsqueeze(2).to_broadcast([P, PT, n])

        def hi_wait(eng, n):
            on_act, on_vec, act_made = hi_counts(n)
            if act_made:
                eng.wait_ge(h_hi_act, on_act)
            else:
                eng.wait_ge(h_hi_vec, on_vec)

        def lo_wait(eng, n):
            on_pool, on_vec, pool_made = lo_counts(n)
            if pool_made:
                eng.wait_ge(h_lo_pool, on_pool)
            else:
                eng.wait_ge(h_lo_vec, on_vec)

        @block.sync
        def _(sp):
            sp.dma_start(xt[:, 0], rows_of(x, 0)).then_inc(x_loaded[0], 16)
            sp.dma_start(attn_raw[:, 0, :], w_i).then_inc(wattn_loaded, 16)
            sp.dma_start(attn_raw[:, 1, :], w_f).then_inc(wattn_loaded, 16)
            sp.dma_start(lb[:], lower_bound.rearrange("(p a) -> p a", a=1)).then_inc(lb_loaded, 16)
            sp.dma_start(pad_i[:], pads.partition_broadcast(P)).then_inc(pad_loaded, 16)
            sp.dma_start(norm_w[:, 1, :], g_norm_w.partition_broadcast(P)).then_inc(norm_loaded[1], 16)
            sp.dma_start(xt[:, 1], rows_of(x, 1)).then_inc(x_loaded[1], 16)
            sp.wait_ge(pad_zeroed, 1)
            sp.dma_start(gate_raw[:, 0:GATE_BLOCKS - 1, :],
                         w_gate[0:(GATE_BLOCKS - 1) * P, :].rearrange("(k p) d -> p k d", p=P)).then_inc(wgate_loaded, 16)
            sp.dma_start(gate_raw[0:GATE_TAIL, GATE_BLOCKS - 1, :],
                         w_gate[(GATE_BLOCKS - 1) * P:GATE_ROWS, :]).then_inc(wgate_loaded, 16)
            sp.dma_start(down_raw, w_down).then_inc(wdown_loaded, 16)
            sp.dma_start(norm_w[:, 2, :], mlp_norm_w.partition_broadcast(P)).then_inc(norm_loaded[2], 16)
            sp.dma_start(ctx[:, 1], rows_of(ctx_mem, 1)).then_inc(ctx_loaded[1], 16)
            for n in range(EXPERTS // WLOAD):
                es = slice(n * WLOAD, (n + 1) * WLOAD)
                sp.dma_start(w_sb[0][:, es, :], w1[es].rearrange("e p h -> p e h")).then_inc(w_loaded[0][n], 16)
                sp.dma_start(w_sb[1][:, es, :].rearrange("p e (c d) -> p e c d", c=CHUNKS),
                             w2[es].rearrange("e (c p) d -> p e c d", p=P)).then_inc(w_loaded[1][n], 16)
                if n == 0:
                    sp.dma_start(b1_rows[:], b1.rearrange("e (c p) -> (e c) p", p=P)).then_inc(small_loaded, 16)
                    sp.dma_start(xw_raw[:], xattn_w).then_inc(small_loaded, 16)
                    sp.dma_start(xb_bias[:], xattn_b.partition_broadcast(P)).then_inc(small_loaded, 16)
            sp.dma_start(br_bc[:], br.partition_broadcast(P)).then_inc(small_loaded, 16)
            sp.dma_start(wr_sb[:], wr).then_inc(small_loaded, 16)
            sp.dma_start(b2_sb[:], b2).then_inc(small_loaded, 16)
            for k in range(PAIRS):
                for r in range(PAIR):
                    sp.wait_ge(out_ready, PT * k + TILES * (r + 1))
                    sp.dma_start(tiles_of(out, PAIR * k + r), acc[:, k, r * TILES:(r + 1) * TILES, :]).then_inc(stored, 16)
            sp.wait_ge(stored, 16 * BATCH)

        @block.gpsimd
        def _(pool):
            step = Steps(pool_step)
            v = nc.gpsimd
            v.memset(gate_raw[GATE_TAIL:P, GATE_BLOCKS - 1, :], 0.0).then_inc(pad_zeroed, 1)
            pool.wait_ge(pad_zeroed, 1)
            v.memset(ones[:], 1.0).then_inc(ones_ready, 1)
            n = step.mark(v.memset(ident[:], 0.0))
            step.mark(v.memset(half[:], 0.5))
            step.mark(v.memset(fexp[:], -0.5))
            step.mark(v.memset(minus_half[:], -0.5))
            pool.wait_ge(pool_step, n)
            v.affine_select(out=ident[:], in_=ident[:], compare_op=ALU.not_equal, fill=1.0, base=0,
                            pattern=[[-1, P]], channel_multiplier=1).then_inc(ident_ready, 1)
            step.mark(v.iota(qpos_i[:], pattern=[[P, TILES]], base=0, channel_multiplier=1))
            n = step.mark(v.iota(kpos_i[:], pattern=[[1, SEQ]], base=0, channel_multiplier=0))
            pool.wait_ge(pool_step, n)
            step.mark(v.tensor_copy(qpos[:], qpos_i[:]))
            step.mark(v.tensor_copy(kpos[:], kpos_i[:]))

            pool.wait_ge(pad_loaded, 16)
            n = step.mark(v.tensor_copy(pad_f[:], pad_i[:]))
            pool.wait_ge(norm_loaded[1], 16)
            n = step.mark(v.tensor_scalar(gw_half[:], norm_w[:, 1, :], 0.5, None, ALU.mult))
            pool.wait_ge(pool_step, n)

            def masks(k, h):
                r, j = divmod(h, TILES)
                g = PAIR * k + r
                if j == 0:
                    n = step.mark(v.tensor_scalar(qneg[k][:, r * TILES:(r + 1) * TILES], qpos[:], pad_f[:, g:g + 1], NEG / SCALE,
                                                  ALU.is_ge, ALU.mult))
                    pool.wait_ge(pool_step, n)
                v.tensor_scalar(negmask[k][:, h, :], kpos[:], pad_f[:, g:g + 1], qneg[k][:, h:h + 1],
                                ALU.is_ge, ALU.mult).then_inc(mask_ready, 1)

            def root(t, k):
                pool.wait_ge(var_ready[t], k + 1)
                v.tensor_tensor(stat[k][t]["root"][:], stat[k][t]["var"][:], half[:], ALU.pow).then_inc(root_ready[t], 1)

            def inverse_root(n, k):
                pool.wait_ge(ln_var[n], k + 1)
                v.tensor_tensor(rstd[n][k][:], lnv[n][k][:], minus_half[:], ALU.pow).then_inc(ln_rstd[n], 1)

            def ab(k, stage):
                if stage == "in_u":
                    if product_on_pool(k):
                        pool.wait_ge(x_loaded[k], 16)
                        pool.wait_ge(norm_loaded[0], 16)
                        v.tensor_tensor(u[k][:], xt[:, k], every_tile(norm_w[:, 0, :]), ALU.mult).then_inc(u_ready["in"], 1)
                elif stage == "in_var":
                    root("in", k)
                elif stage == "swish":
                    if product_on_pool(k):
                        pool.wait_ge(si_ready, k + 1)
                        pool.wait_ge(omf_ready, k + 1)
                        v.tensor_tensor(i_T[k][:], th_i[k][:], omf_T[k][:], ALU.mult).then_inc(iT_ready, 1)
                elif stage == "res":
                    if product_on_pool(k):
                        pool.wait_ge(res_ready, PT * (k + 1))
                        pool.wait_ge(norm_loaded[2], 16)
                        v.tensor_tensor(u[k][:], res[k][:], every_tile(norm_w[:, 2, :]), ALU.mult).then_inc(u_ready["mlp"], 1)
                elif stage == "gain":
                    pool.wait_ge(sg_ready, k + 1)
                    v.tensor_tensor(gain[k][:], sg2[k][:], every_tile(gw_half[:]), ALU.mult).then_inc(gain_ready, 1)
                elif stage == "out_var":
                    root("out", k)
                elif stage == "mlp_var":
                    root("mlp", k)
                    pool.wait_ge(res_ready, PT * (k + 1))
                    v.tensor_tensor(xres[k], res[k][:], xt[:, k], ALU.add).then_inc(xres_ready, 1)
                elif stage == "z_var":
                    root("z", k)
                elif stage == "down":
                    inverse_root(0, k)
                elif stage == "x1":
                    pool.wait_ge(x1_ready, PT * (k + 1))
                    v.tensor_tensor(x1b[k][:], x1[k][:], every_tile(xb_bias[:]), ALU.add).then_inc(x1b_ready, 1)
                elif stage == "ln2":
                    inverse_root(1, k)

            def weights_norm(g):
                pool.wait_ge(wtot_moved, g + 1)
                v.tensor_tensor(flat(w_norm[:, g]), flat(w_total[:, g]), half[:], ALU.pow).then_inc(wnorm_ready, 1)

            def split_low(m, n):
                if m == 1:
                    es = slice(n * WLOAD, (n + 1) * WLOAD)
                    pool.wait_ge(w_scaled_ready, n + 1)
                    pool.wait_ge(w_hi_ready[m], n + 1)
                    v.tensor_tensor(w_lo[m][:, es, :], w_scaled[:], w_hi[m][:, es, :], ALU.subtract).then_inc(w_lo_ready[m], 1)

            def hidden_low(k, e, c):
                n = (k * EXPERTS + e) * CHUNKS + c
                if lo_on_pool(k, e, c):
                    hi_wait(pool, n)
                    if n >= 2 * CHUNKS:
                        pool.wait_ge(fc2_done, n // CHUNKS - 1)
                    v.tensor_tensor(h_lo[:, e % 2, c, :], hid[:, c, :], h_hi[:, e % 2, c, :],
                                    ALU.subtract).then_inc(h_lo_pool, 1)

            def final(k):
                pool.wait_ge(ln_var[2], k + 1)
                v.tensor_tensor(frstd[:], flnv[:], fexp[:], ALU.pow).then_inc(ln_rstd[2], 1)

            for what in order_of("Pool"):
                if what[0] == "ab":
                    ab(*what[1:])
                elif what[0] == "masks":
                    masks(*what[1:])
                elif what[0] == "root_w":
                    weights_norm(*what[1:])
                elif what[0] == "wlow":
                    split_low(*what[1:])
                elif what[0] == "low":
                    hidden_low(*what[1:])
                elif what[0] == "final":
                    final(*what[1:])

        @block.scalar
        def _(act):
            a = nc.scalar
            act.dma_start(norm_w[:, 0, :], attn_norm_w.partition_broadcast(P)).then_inc(norm_loaded[0], 16)
            act.dma_start(attn_raw[:, 2, :], w_g).then_inc(wattn_loaded, 16)
            act.dma_start(attn_raw[:, 3, :], w_o).then_inc(wattn_loaded, 16)
            act.dma_start(ctx[:, 0], rows_of(ctx_mem, 0)).then_inc(ctx_loaded[0], 16)

            def ternary_round(part):
                act.wait_ge(wscale_ready, part + 1)
                for k in TERNARY[part]:
                    lo, hi = WEIGHT_COLS[k]
                    a.activation(wmagic[:, lo:hi], wraw[:, lo:hi], ACT.Identity, bias=round_up[:],
                                 scale=wscale[:, k:k + 1]).then_inc(wmagic_ready, 1)

            def weights_square(m, n):
                g, l = divmod(n, LOADS // NORM_GROUPS)
                es = slice(n * WLOAD, (n + 1) * WLOAD)
                act.wait_ge(w_loaded[m][n], 16)
                a.activation(w_lo[m][:, es, :], w_sb[m][:, es, :], ACT.Square,
                             accum_out=w_sumsq[:, g, m, l:l + 1]).then_inc(wsq_ready, 1)

            def split_high(m, n):
                g, l = divmod(n, LOADS // NORM_GROUPS)
                es = slice(n * WLOAD, (n + 1) * WLOAD)
                act.wait_ge(wup_ready, g + 1)
                a.activation(w_hi[m][:, es, :], w_sb[m][:, es, :], ACT.Copy, scale=w_up[:, g, m, l:l + 1]).then_inc(w_hi_ready[m], 1)

            def scale_load(n):
                g, l = divmod(n, LOADS // NORM_GROUPS)
                act.wait_ge(wup_ready, g + 1)
                if n:
                    act.wait_ge(w_lo_ready[1], n)
                a.activation(w_scaled[:], w_sb[1][:, n * WLOAD:(n + 1) * WLOAD, :], ACT.Copy,
                             scale=w_up[:, g, 1, l:l + 1]).then_inc(w_scaled_ready, 1)

            def square_sums(t, k, source, into):
                for j in range(PT):
                    a.activation(junk[k][:, ("ssx", "ssu").index(into), j, :], source[:, j, :], ACT.Square,
                                 accum_out=stat[k][t][into][:, j:j + 1]).then_inc(squares[into][t], 1)

            def strip_round(t, k, bank):
                act.wait_ge(qT_ready[t], k + 1)
                a.activation(qT[t][k][:], bank[:], ACT.Copy, bias=-ROUND).then_inc(qT_moved[t], 1)

            def ab(k, stage):
                if stage == "ctx":
                    act.wait_ge(ctxT_ready, k + 1)
                    a.activation(ctx_T[k][:], B[k][:], ACT.Copy).then_inc(ctxT_moved, 1)
                elif stage == "in_u":
                    act.wait_ge(x_loaded[k], 16)
                    square_sums("in", k, xt[:, k], "ssx")
                    act.wait_ge(u_ready["in"], k + 1)
                    square_sums("in", k, u[k], "ssu")
                elif stage == "in_q":
                    strip_round("in", k, A[k])
                elif stage == "in_deq":
                    act.wait_ge(deq_bc_done, k + 1)
                    a.activation(deq_bc[k][:], B[k][:], ACT.Copy).then_inc(deq_bc_moved, 1)
                elif stage == "sigmoids":
                    act.wait_ge(uf_ready, k + 1)
                    a.activation(th_f[k][:], uf[k][:], ACT.Tanh, scale=half_mean[:, 1:2]).then_inc(thf_ready, 1)
                    act.wait_ge(ui_ready, k + 1)
                    a.activation(th_i[k][:], ui[k][:], ACT.Tanh, scale=half_mean[:, 0:1]).then_inc(thi_ready, 1)
                    act.wait_ge(thf_ready, k + 1)
                    act.wait_ge(omf_set, 1)
                    a.activation(omf_T[k][:], th_f[k][:], ACT.Identity, bias=omf_bias[:], scale=omf_scale[:]).then_inc(omf_ready, 1)
                elif stage == "g":
                    act.wait_ge(g_done, k + 1)
                    for j in range(PT):
                        a.activation(th_g[k][:, j, :], B[k][:, j * D:(j + 1) * D], ACT.Tanh,
                                     scale=deq_gh[k][:, j:j + 1]).then_inc(thg_ready, 1)
                elif stage == "o":
                    act.wait_ge(o_ready, k + 1)
                    square_sums("out", k, tiles(A[k]), "ssx")
                elif stage == "out_var":
                    act.wait_ge(u_ready["out"], k + 1)
                    square_sums("out", k, u[k], "ssu")
                elif stage == "out_q":
                    strip_round("out", k, B[k])
                elif stage == "res":
                    act.wait_ge(res_ready, PT * (k + 1))
                    square_sums("mlp", k, res[k], "ssx")
                elif stage == "mlp_var":
                    act.wait_ge(u_ready["mlp"], k + 1)
                    square_sums("mlp", k, u[k], "ssu")
                elif stage == "mlp_q":
                    strip_round("mlp", k, B[k])
                elif stage.startswith("gate"):
                    j = int(stage[-1])
                    n = PT * k + j
                    if j == 0:
                        act.wait_ge(deqh_ready, k + 1)
                    act.wait_ge(gate_done, n + 1)
                    a.activation(zt[k][:, j, :], A[k][:, 0:INNER], ACT.Tanh, scale=deqh[k][:, j:j + 1]).then_inc(zt_ready, 1)
                elif stage.startswith("zsq"):
                    j = int(stage[-1])
                    act.wait_ge(z_ready, PT * k + j + 1)
                    a.activation(q_z[k][:, j, :], z[k][:, j, :], ACT.Square,
                                 accum_out=stat[k]["z"]["ssu"][:, j:j + 1]).then_inc(squares["ssu"]["z"], 1)
                elif stage == "quant_z":
                    for j in range(1, PT, 2):
                        act.wait_ge(inv_ready, k + 1)
                        a.activation(q_z[k][:, j, :], z[k][:, j, :], ACT.Identity, bias=round_up[:],
                                     scale=stat[k]["z"]["inv"][:, j:j + 1]).then_inc(qz_act, 1)
                elif stage.startswith("z_q"):
                    j = int(stage[-1])
                    act.wait_ge(qT_ready["z"], PT * k + j + 1)
                    a.activation(qT_z[k][:, j, :, :], (A, B)[j % 2][k][:, 0:len(DOWN) * P].rearrange("p (c q) -> p c q", c=len(DOWN)),
                                 ACT.Copy, bias=-ROUND).then_inc(qT_moved["z"], 1)
                elif stage == "x1":
                    act.wait_ge(x1T_ready, k + 1)
                    a.activation(x1_T[k][:], B[k][:], ACT.Copy).then_inc(x1T_moved, 1)
                elif stage == "softmax":
                    for j in range(PT):
                        act.wait_ge(sc_ready, PT * k + j + 1)
                        a.activation(prob[k][:, j, :], sc[k][:, j, :], ACT.Exp, bias=negmax[k][:, j:j + 1], scale=-1.0,
                                     accum_out=prob_sum[k][:, j:j + 1]).then_inc(prob_ready, 1)
                elif stage == "turn":
                    for r in range(PAIR):
                        act.wait_ge(probT_ready, PAIR * k + r + 1)
                        a.activation(prob_T[k][:, r], (A, B)[r][k][:].rearrange("p (t q) -> p t q", t=TILES), ACT.Copy).then_inc(probT_moved, 1)
                elif stage == "attend":
                    for r in range(PAIR):
                        act.wait_ge(att_done, PAIR * k + r + 1)
                        a.activation(att_T[k][:, r * SEQ:(r + 1) * SEQ], (A, B)[r][k][:, 0:SEQ], ACT.Copy).then_inc(attT_moved, 1)
                elif stage == "x2":
                    act.wait_ge(x2T_ready, k + 1)
                    a.activation(x2_T[k][:], B[k][:], ACT.Copy).then_inc(x2T_moved, 1)
                    act.wait_ge(x2T_moved, k + 1)
                    a.activation(x2_hi[:, k], x2_T[k][:].rearrange("p (r t) -> p r t", r=PAIR), ACT.Copy, scale=X_UP).then_inc(x2hi_ready, 1)
                elif stage == "router":
                    act.wait_ge(lgt_ready, k + 1)
                    a.activation(tg[k][:], lgt[k][:], ACT.Tanh, scale=0.5).then_inc(tg_ready, 1)
                elif stage == "turn_gates":
                    act.wait_ge(gwT_ready, k + 1)
                    a.activation(gate_wT[k][:], B[k][0:EXPERTS, :], ACT.Copy).then_inc(gwT_moved, 1)

            def hidden(k, e, c):
                n = (k * EXPERTS + e) * CHUNKS + c
                act.wait_ge(fc1_done, n + 1)
                if n >= CHUNKS:
                    lo_wait(act, n - CHUNKS)
                    hi_wait(act, n - CHUNKS)
                g, l = divmod(e // WLOAD, LOADS // NORM_GROUPS)
                a.activation(hid[:, c, :], H[n % HBANKS][:], ACT.Gelu, scale=w_in_scale[:, g, 0, l:l + 1],
                             bias=b1_T[:, e * CHUNKS + c:e * CHUNKS + c + 1]).then_inc(gelu_done, 1)

            def hidden_high(k, e, c):
                n = (k * EXPERTS + e) * CHUNKS + c
                if hi_on_act(k, e, c):
                    act.wait_ge(gelu_done, n + 1)
                    if n >= 2 * CHUNKS:
                        act.wait_ge(fc2_done, n // CHUNKS - 1)
                    a.activation(h_hi[:, e % 2, c, :], hid[:, c, :], ACT.Copy).then_inc(h_hi_act, 1)

            for what in order_of("ACT"):
                if what[0] == "ab":
                    ab(*what[1:])
                elif what[0] == "round":
                    ternary_round(*what[1:])
                elif what[0] == "wsquare":
                    weights_square(*what[1:])
                elif what[0] == "wscale":
                    scale_load(*what[1:])
                elif what[0] == "whigh":
                    split_high(*what[1:])
                elif what[0] == "gelu":
                    hidden(*what[1:])
                elif what[0] == "high":
                    hidden_high(*what[1:])

        @block.vector
        def _(dve):
            step = Steps(vec_step)
            v = nc.vector
            step.mark(v.memset(round_up[:], ROUND))
            made = {}

            def ternary_means(part):
                if part == 0:
                    dve.wait_ge(wattn_loaded, 64)
                    v.tensor_reduce(wabs[:, 0:4], attn_raw, AX, ALU.add, apply_absolute_value=True).then_inc(wabs_ready, 1)
                else:
                    dve.wait_ge(wgate_loaded, 32)
                    v.tensor_reduce(wabs[:, 4:5], gate_raw, AXY, ALU.add, apply_absolute_value=True).then_inc(wabs_ready, 1)
                    dve.wait_ge(wdown_loaded, 16)
                    v.tensor_reduce(wabs[:, 5:6], down_raw, AX, ALU.add, apply_absolute_value=True).then_inc(wabs_ready, 1)

            def ternary_scales(part):
                cols, size = (((0, 4), D * D), ((4, 6), D * INNER))[part]
                dve.wait_ge(wtot_ready, part + 1)
                if part == 0:
                    n = step.mark(v.tensor_scalar(wmean[:, 0:4], Y[1][:, 0, 0:4], 1.0 / size, CLIP, ALU.mult, ALU.max))
                else:
                    step.mark(v.tensor_scalar(wmean[:, 4:5], Y[1][:, 0, 4:5], 0.5 / size, CLIP, ALU.mult, ALU.max))
                    n = step.mark(v.tensor_scalar(wmean[:, 5:6], Y[1][:, 0, 5:6], 1.0 / size, CLIP, ALU.mult, ALU.max))
                dve.wait_ge(vec_step, n)
                v.reciprocal(wscale[:, cols[0]:cols[1]], wmean[:, cols[0]:cols[1]]).then_inc(wscale_ready, 1)
                if part == 0:
                    dve.wait_ge(lb_loaded, 16)
                    step.mark(v.tensor_scalar(half_mean[:], wmean[:, 0:2], 0.5, None, ALU.mult))
                    n = step.mark(v.tensor_scalar(f_gain[:], lb[:], -0.5, 0.5, ALU.mult, ALU.add))
                    dve.wait_ge(vec_step, n)
                    step.mark(v.tensor_scalar(f_base[:], lb[:], f_gain[:], None, ALU.add))
                    n = step.mark(v.tensor_scalar(omf_bias[:], half_mean[:, 0:1], f_gain[:], None, ALU.mult))
                    dve.wait_ge(vec_step, n)
                    v.tensor_scalar(omf_scale[:], omf_bias[:], -1.0, None, ALU.mult).then_inc(omf_set, 1)

            def ternary_clip(part):
                for k in TERNARY[part]:
                    lo, hi = WEIGHT_COLS[k]
                    dve.wait_ge(wmagic_ready, k + 1)
                    v.tensor_scalar(wmagic[:, lo:hi], wmagic[:, lo:hi], ROUND + 1.0, ROUND - 1.0,
                                    ALU.min, ALU.max).then_inc(wclip_ready, 1)

            def ternary_move(part):
                if part == 0:
                    dve.wait_ge(wT_ready, 1)
                    v.tensor_scalar(attn_T[:], H[0][:], -ROUND, None, ALU.add).then_inc(wT_moved, 1)
                    return
                dve.wait_ge(wT_ready, 2)
                v.tensor_scalar(gate_T[:, 0:512], H[1][:], -ROUND, None, ALU.add).then_inc(wT_moved, 1)
                dve.wait_ge(wT_ready, 3)
                v.tensor_scalar(gate_T[:, 512:GATE_ROWS], Y0[:, 0:GATE_ROWS - 512], -ROUND, None, ALU.add).then_inc(wT_moved, 1)
                dve.wait_ge(wT_ready, 4)
                for c, rows in DOWN:
                    last = v.tensor_scalar(down_T[0:rows, c, :], H[0][0:rows, c * D:(c + 1) * D], -ROUND, None, ALU.add)
                last.then_inc(wT_moved, 1)

            def move_small():
                dve.wait_ge(wT_ready, 5)
                v.tensor_copy(xw_T[:], H[1][:, 0:D])
                v.tensor_copy(b1_T[:], H[1][:, D:D + EXPERTS * CHUNKS]).then_inc(wT_moved, 1)

            def weights_total(g):
                dve.wait_ge(wsum_done, g + 1)
                v.tensor_scalar(flat(w_total[:, g]), Y[1][:, g, 0:PT], 1e-36, None, ALU.max).then_inc(wtot_moved, 1)

            def weights_scale(g):
                dve.wait_ge(wnorm_ready, g + 1)
                n = step.mark(v.tensor_scalar(flat(w_power[:, g]).bitcast(int32), flat(w_norm[:, g]).bitcast(int32), 0x7F800000, None,
                                              ALU.bitwise_and))
                dve.wait_ge(vec_step, n)
                n = step.mark(v.reciprocal(flat(w_up[:, g]), flat(w_power[:, g])))
                step.mark(v.tensor_scalar(flat(w_in_scale[:, g]), flat(w_power[:, g]), 1.0 / (W_TARGET * X_UP), None, ALU.mult))
                experts = EXPERTS // NORM_GROUPS
                made["out_scale", g] = step.mark(v.tensor_scalar(
                    w_out_scale[:, g * experts:(g + 1) * experts].rearrange("p (l e) -> p l e", e=WLOAD),
                    w_power[:, g, 1, :].unsqueeze(2).to_broadcast([P, LOADS // NORM_GROUPS, WLOAD]), 1.0 / W_TARGET, None, ALU.mult))
                dve.wait_ge(vec_step, n)
                v.tensor_scalar(flat(w_up[:, g]), flat(w_up[:, g]), W_TARGET, None, ALU.mult).then_inc(wup_ready, 1)

            def scale_gates(k, g):
                es = slice(g * EXPERTS // NORM_GROUPS, (g + 1) * EXPERTS // NORM_GROUPS)
                dve.wait_ge(gatew_ready, k + 1)
                dve.wait_ge(vec_step, made["out_scale", g])
                v.tensor_tensor(gate_s[:, k, :, es], gate_w[k][:, :, es], every_tile(w_out_scale[:, es]), ALU.mult).then_inc(gates_ready, 1)

            def split_low(m, n):
                if m == 0:
                    g, l = divmod(n, LOADS // NORM_GROUPS)
                    es = slice(n * WLOAD, (n + 1) * WLOAD)
                    dve.wait_ge(wup_ready, g + 1)
                    dve.wait_ge(w_hi_ready[m], n + 1)
                    v.scalar_tensor_tensor(w_lo[m][:, es, :], w_sb[m][:, es, :], w_up[:, g, m, l:l + 1], w_hi[m][:, es, :],
                                           ALU.mult, ALU.subtract).then_inc(w_lo_ready[m], 1)

            def peak(t, k, source):
                made["peak", t, k] = step.mark(v.tensor_reduce(stat[k][t]["peak"][:], source, AX, ALU.max,
                                                               apply_absolute_value=True))

            def variance(t, k, scale=None):
                s = stat[k][t]
                peak_step = made["peak", t, k]
                dve.wait_ge(vec_step, peak_step)
                if scale is None:
                    step.mark(v.tensor_scalar(s["peakq"][:], s["peak"][:], 1.0 / QMAX, None, ALU.mult))
                else:
                    step.mark(v.scalar_tensor_tensor(s["peakq"][:], s["peak"][:], 1.0 / QMAX, scale[:], ALU.mult, ALU.mult))
                if t == "z":
                    dve.wait_ge(squares["ssu"]["z"], PT * (k + 1))
                    v.tensor_scalar(s["var"][:], s["ssu"][:], 1.0 / INNER, EPS, ALU.mult, ALU.add).then_inc(var_ready[t], 1)
                    return
                dve.wait_ge(squares["ssx"][t], PT * (k + 1))
                n = step.mark(v.tensor_scalar(s["tail"][:], s["ssx"][:], EPS / D, EPS * EPS, ALU.mult, ALU.add))
                dve.wait_ge(squares["ssu"][t], PT * (k + 1))
                total = s["ssu"]
                if scale is not None:
                    total = gss[k]
                    n = step.mark(v.tensor_tensor(total[:], s["ssu"][:], deq_gg[k][:], ALU.mult))
                dve.wait_ge(vec_step, n)
                v.scalar_tensor_tensor(s["var"][:], total[:], 1.0 / D, s["tail"][:], ALU.mult,
                                       ALU.add).then_inc(var_ready[t], 1)

            def scales(t, k):
                s = stat[k][t]
                dve.wait_ge(root_ready[t], k + 1)
                n = step.mark(v.scalar_tensor_tensor(s["step"][:], s["root"][:], CLIP / QMAX, s["peakq"][:], ALU.mult, ALU.max))
                made["rroot", t, k] = step.mark(v.reciprocal(s["rroot"][:], s["root"][:]))
                dve.wait_ge(vec_step, n)
                return v.reciprocal(s["inv"][:], s["step"][:])

            def quantise(t, k, source, scale=None):
                s = stat[k][t]
                inv, n = s["inv"], step.mark(scales(t, k))
                if scale is not None:
                    inv = ginv[k]
                    dve.wait_ge(vec_step, n)
                    n = step.mark(v.tensor_tensor(inv[:], s["inv"][:], scale[:], ALU.mult))
                dve.wait_ge(vec_step, n)
                for j in range(PT):
                    v.tensor_scalar(q[t][k][:, j, :], source[:, j, :], inv[:, j:j + 1], ROUND, ALU.mult,
                                    ALU.add).then_inc(q_ready[t], 1)

            def dequantiser(t, k, w, into):
                s = stat[k][t]
                dve.wait_ge(vec_step, made["rroot", t, k])
                scalar = wmean[:, w:w + 1] if w is not None else 1.0
                return v.scalar_tensor_tensor(into[:], s["step"][:], scalar, s["rroot"][:], ALU.mult, ALU.mult)

            def layernorm_stats(m, k, source, n):
                dve.wait_ge(vec_step, n)
                for j in range(PT):
                    n = step.mark(v.bn_stats(bn[m][k][:, j, :], source[:, j, :]))
                dve.wait_ge(vec_step, n)
                for j in range(PT):
                    n = step.mark(v.bn_aggr(mv[m][k][:, j, :], bn[m][k][:, j, :]))
                dve.wait_ge(vec_step, n)
                v.tensor_scalar(lnv[m][k][:], mv[m][k][:, :, 1], LN_EPS, None, ALU.add).then_inc(ln_var[m], 1)

            def layernorm(m, k, source, into, ready):
                dve.wait_ge(ln_rstd[m], k + 1)
                for j in range(PT):
                    v.tensor_scalar(into[:, j, :], source[:, j, :], mv[m][k][:, j, 0:1], rstd[m][k][:, j:j + 1],
                                    ALU.subtract, ALU.mult).then_inc(ready, 1)

            def ab(k, stage):
                if stage == "in_u":
                    if not product_on_pool(k):
                        dve.wait_ge(x_loaded[k], 16)
                        dve.wait_ge(norm_loaded[0], 16)
                        v.tensor_tensor(u[k][:], xt[:, k], every_tile(norm_w[:, 0, :]), ALU.mult).then_inc(u_ready["in"], 1)
                elif stage == "in_peak":
                    dve.wait_ge(u_ready["in"], k + 1)
                    peak("in", k, u[k][:])
                elif stage == "in_var":
                    variance("in", k)
                elif stage == "in_q":
                    quantise("in", k, u[k])
                    dequantiser("in", k, None, deq_in[k]).then_inc(deq_ready, 1)
                elif stage == "in_deq":
                    if k == 0:
                        dve.wait_ge(wscale_ready, 1)
                    n = step.mark(dequantiser("in", k, 2, deq_g[k]))
                    dve.wait_ge(vec_step, n)
                    v.tensor_scalar(deq_gh[k][:], deq_g[k][:], 0.5, None, ALU.mult).then_inc(deq_ready, 1)
                    made["deq_gg", k] = step.mark(v.tensor_tensor(deq_gg[k][:], deq_g[k][:], deq_g[k][:], ALU.mult))
                elif stage == "if":
                    dve.wait_ge(deq_bc_moved, k + 1)
                    dve.wait_ge(f_done, k + 1)
                    v.tensor_tensor(uf[k][:], B[k][:], deq_bc[k][:], ALU.mult).then_inc(uf_ready, 1)
                    dve.wait_ge(i_done, k + 1)
                    v.tensor_tensor(ui[k][:], A[k][:], deq_bc[k][:], ALU.mult).then_inc(ui_ready, 1)
                elif stage == "swish":
                    dve.wait_ge(thi_ready, k + 1)
                    v.scalar_tensor_tensor(th_i[k][:], th_i[k][:], 1.0, ui[k][:], ALU.add, ALU.mult).then_inc(si_ready, 1)
                    dve.wait_ge(omf_ready, k + 1)
                    made["f", k] = step.mark(v.tensor_scalar(f_T[k][:], th_f[k][:], f_gain[:], f_base[:], ALU.mult, ALU.add))
                    if not product_on_pool(k):
                        dve.wait_ge(si_ready, k + 1)
                        v.tensor_tensor(i_T[k][:], th_i[k][:], omf_T[k][:], ALU.mult).then_inc(iT_ready, 1)
                elif stage == "scan":
                    dve.wait_ge(vec_step, made["f", k])
                    dve.wait_ge(iT_ready, k + 1)
                    for r in range(PAIR):
                        row = slice(r * SEQ, (r + 1) * SEQ)
                        v.tensor_tensor_scan(o_T[k][:, row], f_T[k][:, row], i_T[k][:, row], 0.0, ALU.mult, ALU.add).then_inc(scan_done, 1)
                elif stage == "gain":
                    dve.wait_ge(thg_ready, PT * (k + 1))
                    v.scalar_tensor_tensor(sg2[k][:], th_g[k][:], 1.0, tiles(B[k]), ALU.add, ALU.mult).then_inc(sg_ready, 1)
                elif stage == "o":
                    dve.wait_ge(squares["ssx"]["out"], PT * (k + 1))
                    dve.wait_ge(gain_ready, k + 1)
                    v.tensor_tensor(u[k][:], tiles(A[k]), gain[k][:], ALU.mult).then_inc(u_ready["out"], 1)
                elif stage == "out_peak":
                    dve.wait_ge(u_ready["out"], k + 1)
                    peak("out", k, u[k][:])
                elif stage == "out_var":
                    dve.wait_ge(vec_step, made["deq_gg", k])
                    variance("out", k, deq_g[k])
                elif stage == "out_q":
                    quantise("out", k, u[k], deq_g[k])
                    made["deq_o", k] = step.mark(dequantiser("out", k, 3, deq_o[k]))
                elif stage == "res":
                    dve.wait_ge(wo_done, k + 1)
                    dve.wait_ge(vec_step, made["deq_o", k])
                    for j in range(PT):
                        v.scalar_tensor_tensor(res[k][:, j, :], A[k][:, j * D:(j + 1) * D], deq_o[k][:, j:j + 1],
                                               xt[:, k, j, :], ALU.mult, ALU.add).then_inc(res_ready, 1)
                    if not product_on_pool(k):
                        dve.wait_ge(res_ready, PT * (k + 1))
                        dve.wait_ge(norm_loaded[2], 16)
                        v.tensor_tensor(u[k][:], res[k][:], every_tile(norm_w[:, 2, :]), ALU.mult).then_inc(u_ready["mlp"], 1)
                elif stage == "mlp_peak":
                    dve.wait_ge(u_ready["mlp"], k + 1)
                    peak("mlp", k, u[k][:])
                elif stage == "mlp_var":
                    variance("mlp", k)
                elif stage == "mlp_q":
                    if k == 0:
                        dve.wait_ge(wscale_ready, 2)
                    quantise("mlp", k, u[k])
                    n = step.mark(dequantiser("mlp", k, 4, deqg[k]))
                    dve.wait_ge(vec_step, n)
                    v.tensor_scalar(deqh[k][:], deqg[k][:], 0.5, None, ALU.mult).then_inc(deqh_ready, 1)
                    made["deqgg", k] = step.mark(v.scalar_tensor_tensor(deqgg[k][:], deqg[k][:], 0.5, deqg[k][:], ALU.mult, ALU.mult))
                elif stage.startswith("gate"):
                    j = int(stage[-1])
                    n = PT * k + j
                    dve.wait_ge(zt_ready, n + 1)
                    v.scalar_tensor_tensor(za[k][:, j, :], zt[k][:, j, :], 1.0, A[k][:, 0:INNER], ALU.add, ALU.mult).then_inc(za_ready, 1)
                    dve.wait_ge(vec_step, made["deqgg", k])
                    dve.wait_ge(za_ready, n + 1)
                    dve.wait_ge(value_done, n + 1)
                    v.scalar_tensor_tensor(z[k][:, j, :], B[k][:, 0:INNER], deqgg[k][:, j:j + 1], za[k][:, j, :], ALU.mult,
                                           ALU.mult).then_inc(z_ready, 1)
                elif stage.startswith("zsq"):
                    j = int(stage[-1])
                    dve.wait_ge(z_ready, PT * k + j + 1)
                    made["peak", "z", k] = step.mark(v.tensor_reduce(stat[k]["z"]["peak"][:, j:j + 1], z[k][:, j, :], AX, ALU.max,
                                                                     apply_absolute_value=True))
                elif stage == "z_var":
                    variance("z", k)
                elif stage == "z_inv":
                    scales("z", k).then_inc(inv_ready, 1)
                elif stage == "quant_z":
                    dve.wait_ge(inv_ready, k + 1)
                    for j in range(0, PT, 2):
                        v.tensor_scalar(q_z[k][:, j, :], z[k][:, j, :], stat[k]["z"]["inv"][:, j:j + 1], ROUND, ALU.mult,
                                        ALU.add).then_inc(qz_vec, 1)
                    made["deq_z", k] = step.mark(dequantiser("z", k, 5, deq_z[k]))
                elif stage == "down":
                    dve.wait_ge(xres_ready, k + 1)
                    dve.wait_ge(down_done, k + 1)
                    dve.wait_ge(vec_step, made["deq_z", k])
                    for j in range(PT):
                        n = step.mark(v.scalar_tensor_tensor(pre[k][:, j, :], A[k][:, j * D:(j + 1) * D],
                                                             deq_z[k][:, j:j + 1], xres[k][:, j, :], ALU.mult, ALU.add))
                    layernorm_stats(0, k, pre[k], n)
                elif stage == "x1":
                    layernorm(0, k, pre[k], x1[k], x1_ready)
                elif stage == "scores":
                    for j in range(PT):
                        dve.wait_ge(mask_ready, PT * k + j + 1)
                        r, h = divmod(j, TILES)
                        dve.wait_ge(scores_done, PT * k + (r + 1) * TILES)
                        v.tensor_tensor_reduce(out=sc[k][:, j, :], in0=(A, B)[r][k][:, h * SEQ:(h + 1) * SEQ],
                                               in1=negmask[k][:, j, :], scale=-SCALE, scalar=3.0e38, op0=ALU.add, op1=ALU.min,
                                               accum_out=negmax[k][:, j:j + 1]).then_inc(sc_ready, 1)
                elif stage == "turn":
                    dve.wait_ge(prob_ready, PT * (k + 1))
                    made["rsum", k] = step.mark(v.reciprocal(rsum[k][:], prob_sum[k][:]))
                elif stage == "ln2":
                    dve.wait_ge(x1b_ready, k + 1)
                    dve.wait_ge(proj_done, k + 1)
                    dve.wait_ge(vec_step, made["rsum", k])
                    for j in range(PT):
                        n = step.mark(v.scalar_tensor_tensor(pre[k][:, j, :], A[k][:, j * D:(j + 1) * D],
                                                             rsum[k][:, j:j + 1], x1b[k][:, j, :], ALU.mult, ALU.add))
                    layernorm_stats(1, k, pre[k], n)
                elif stage == "x2":
                    layernorm(1, k, pre[k], x2[k], x2_ready)
                elif stage == "x2_lo":
                    dve.wait_ge(x2hi_ready, k + 1)
                    v.scalar_tensor_tensor(x2_lo[:, k], x2_T[k][:].rearrange("p (r t) -> p r t", r=PAIR), X_UP, x2_hi[:, k], ALU.mult,
                                           ALU.subtract).then_inc(x2lo_ready, 1)
                elif stage == "router":
                    dve.wait_ge(logits_done, k + 1)
                    v.tensor_tensor(lg[k][:], A[k][:, 0:PT * EXPERTS].rearrange("p (j e) -> p j e", j=PT),
                                    every_tile(br_bc[:]), ALU.add).then_inc(lg_ready, 1)
                    dve.wait_ge(lg_ready, k + 1)
                    for j in range(PT):
                        n = step.mark(v.max(top[k][:, j, :], lg[k][:, j, :]))
                    dve.wait_ge(vec_step, n)
                    v.tensor_tensor(lgt[k][:], lg[k][:], every_column(top[k][:, :, 0], EXPERTS), ALU.subtract).then_inc(lgt_ready, 1)
                    made["chosen", k] = step.mark(v.tensor_tensor(chosen[k][:], lg[k][:], every_column(top[k][:, :, 1], EXPERTS), ALU.is_ge))
                elif stage == "weigh":
                    dve.wait_ge(tg_ready, k + 1)
                    n = step.mark(v.tensor_scalar(den[k][:], tg[k][:], -1.0, 1.0, ALU.mult, ALU.add))
                    dve.wait_ge(vec_step, n)
                    n = step.mark(v.reciprocal(rden[k][:], den[k][:]))
                    dve.wait_ge(vec_step, n)
                    n = step.mark(v.scalar_tensor_tensor(eg[k][:], tg[k][:], 1.0, rden[k][:], ALU.add, ALU.mult))
                    dve.wait_ge(vec_step, n)
                    n = step.mark(v.tensor_tensor(em[k][:], eg[k][:], chosen[k][:], ALU.mult))
                    dve.wait_ge(vec_step, n)
                    n = step.mark(v.tensor_reduce(esum[k][:], em[k][:], AX, ALU.add))
                    dve.wait_ge(vec_step, n)
                    n = step.mark(v.reciprocal(ersum[k][:], esum[k][:]))
                    dve.wait_ge(vec_step, n)
                    v.tensor_tensor(gate_w[k][:], em[k][:], every_column(ersum[k][:], EXPERTS), ALU.mult).then_inc(gatew_ready, 1)
                elif stage == "bias2":
                    dve.wait_ge(b2_done, k + 1)
                    v.tensor_tensor(acc[:, k], tiles(A[k]), x2[k][:], ALU.add).then_inc(acc_started, 1)

            def hidden_high(k, e, c):
                n = (k * EXPERTS + e) * CHUNKS + c
                if not hi_on_act(k, e, c):
                    dve.wait_ge(gelu_done, n + 1)
                    if n >= 2 * CHUNKS:
                        dve.wait_ge(fc2_done, n // CHUNKS - 1)
                    v.tensor_copy(h_hi[:, e % 2, c, :], hid[:, c, :]).then_inc(h_hi_vec, 1)

            def hidden_low(k, e, c):
                n = (k * EXPERTS + e) * CHUNKS + c
                if not lo_on_pool(k, e, c):
                    hi_wait(dve, n)
                    if n >= 2 * CHUNKS:
                        dve.wait_ge(fc2_done, n // CHUNKS - 1)
                    v.tensor_tensor(h_lo[:, e % 2, c, :], hid[:, c, :], h_hi[:, e % 2, c, :],
                                    ALU.subtract).then_inc(h_lo_vec, 1)

            def combine(k, e):
                n = k * EXPERTS + e
                if e == 0:
                    dve.wait_ge(acc_started, k + 1)
                dve.wait_ge(gates_ready, NORM_GROUPS * k + e * NORM_GROUPS // EXPERTS + 1)
                dve.wait_ge(fc2_done, n + 1)
                for j in range(PT):
                    if e:
                        dve.wait_ge(combined, PT * (n - 1) + j + 1)
                    v.scalar_tensor_tensor(acc[:, k, j, :], Y[n % YBANKS][:, j, :], gate_s[:, k, j, e:e + 1], acc[:, k, j, :],
                                           ALU.mult, ALU.add).then_inc(combined, 1)

            def final(k):
                dve.wait_ge(combined, PT * EXPERTS * (k + 1))
                for j in range(PT):
                    n = step.mark(v.bn_stats(fbn[:, j, :], acc[:, k, j, :]))
                dve.wait_ge(vec_step, n)
                for j in range(PT):
                    n = step.mark(v.bn_aggr(fmv[:, j, :], fbn[:, j, :]))
                dve.wait_ge(vec_step, n)
                v.tensor_scalar(flnv[:], fmv[:, :, 1], LN_EPS, None, ALU.add).then_inc(ln_var[2], 1)

            def final_apply(k):
                dve.wait_ge(ln_rstd[2], k + 1)
                for j in range(PT):
                    v.tensor_scalar(acc[:, k, j, :], acc[:, k, j, :], fmv[:, j, 0:1], frstd[:, j:j + 1],
                                    ALU.subtract, ALU.mult).then_inc(out_ready, 1)

            for what in order_of("DVE"):
                if what[0] == "ab":
                    ab(*what[1:])
                elif what[0] == "means":
                    ternary_means(*what[1:])
                elif what[0] == "mean_w":
                    ternary_scales(*what[1:])
                elif what[0] == "round":
                    ternary_clip(*what[1:])
                elif what[0] == "turn_w":
                    ternary_move(*what[1:])
                elif what[0] == "turn_small":
                    move_small()
                elif what[0] == "total_w":
                    weights_total(*what[1:])
                elif what[0] == "scale_w":
                    weights_scale(*what[1:])
                elif what[0] == "scale_gates":
                    scale_gates(*what[1:])
                elif what[0] == "wlow":
                    split_low(*what[1:])
                elif what[0] == "high":
                    hidden_high(*what[1:])
                elif what[0] == "low":
                    hidden_low(*what[1:])
                elif what[0] == "combine":
                    combine(*what[1:])
                elif what[0] == "final":
                    final(*what[1:])
                elif what[0] == "final_apply":
                    final_apply(*what[1:])

        @block.tensor
        def _(pe):
            t_ = nc.tensor
            pe.wait_ge(ident_ready, 1)
            pe.wait_ge(ones_ready, 1)

            def ternary_sums(part):
                pe.wait_ge(wabs_ready, (1, 3)[part])
                cols = ((0, 4), (4, 6))[part]
                if part:
                    pe.wait_ge(wscale_ready, 1)
                t_.matmul(Y[1][:, 0, cols[0]:cols[1]], ones[:], wabs[:, cols[0]:cols[1]], start=True, stop=True).then_inc(wtot_ready, 1)

            def ternary_turn(part):
                if part == 0:
                    for k in range(4):
                        pe.wait_ge(wclip_ready, k + 1)
                        last = t_.transpose(H[0][:, k * D:(k + 1) * D], wmagic[:, k * D:(k + 1) * D], ident[:])
                    last.then_inc(wT_ready, 1)
                    return
                pe.wait_ge(wclip_ready, 6)
                pe.wait_ge(wT_moved, 1)
                for k in range(4):
                    last = t_.transpose(H[1][:, k * P:(k + 1) * P], wmagic[:, GATE_AT + k * D:GATE_AT + (k + 1) * D], ident[:])
                last.then_inc(wT_ready, 1)
                t_.transpose(Y0[:, 0:P], wmagic[:, GATE_AT + 4 * D:GATE_AT + 5 * D], ident[:])
                t_.transpose(Y0[:, P:P + GATE_TAIL], wmagic[0:GATE_TAIL, GATE_AT + 5 * D:GATE_AT + 6 * D],
                             ident[0:GATE_TAIL, 0:GATE_TAIL]).then_inc(wT_ready, 1)
                for c, rows in DOWN:
                    last = t_.transpose(H[0][0:rows, c * D:(c + 1) * D], wmagic[:, DOWN_AT + c * P:DOWN_AT + c * P + rows], ident[:])
                last.then_inc(wT_ready, 1)

            def turn_small():
                pe.wait_ge(small_loaded, 16 * 6)
                pe.wait_ge(wT_moved, 2)
                t_.transpose(H[1][:, 0:D], xw_raw[:], ident[:])
                t_.transpose(H[1][:, D:D + EXPERTS * CHUNKS], b1_rows[:],
                             ident[0:EXPERTS * CHUNKS, 0:EXPERTS * CHUNKS]).then_inc(wT_ready, 1)

            def transpose_tiles(bank, source):
                for j in range(PT):
                    last = t_.transpose(bank[:, j * P:(j + 1) * P], source[:, j, :], ident[:])
                return last

            def ab(k, stage):
                if stage == "ctx":
                    pe.wait_ge(ctx_loaded[k], 16)
                    transpose_tiles(B[k], ctx[:, k]).then_inc(ctxT_ready, 1)
                elif stage == "in_q":
                    pe.wait_ge(q_ready["in"], PT * (k + 1))
                    transpose_tiles(A[k], q["in"][k]).then_inc(qT_ready["in"], 1)
                elif stage == "in_deq":
                    pe.wait_ge(ctxT_moved, k + 1)
                    pe.wait_ge(deq_ready, 2 * k + 1)
                    for j in range(PT):
                        last = t_.matmul(B[k][:, j * P:(j + 1) * P], deq_in[k][:, j:j + 1].to_broadcast([P, P]), ident[:],
                                         start=True, stop=True)
                    last.then_inc(deq_bc_done, 1)
                elif stage == "if":
                    if k == 0:
                        pe.wait_ge(wT_moved, 1)
                    pe.wait_ge(qT_moved["in"], k + 1)
                    pe.wait_ge(deq_bc_moved, k + 1)
                    t_.matmul(B[k][:], attn_T[:, D:2 * D], qT["in"][k][:], start=True, stop=True).then_inc(f_done, 1)
                    t_.matmul(A[k][:], attn_T[:, 0:D], qT["in"][k][:], start=True, stop=True).then_inc(i_done, 1)
                elif stage == "g":
                    pe.wait_ge(uf_ready, k + 1)
                    pe.wait_ge(deq_ready, 2 * k + 2)
                    for j in range(PT):
                        last = t_.matmul(B[k][:, j * D:(j + 1) * D], qT["in"][k][:, j * P:(j + 1) * P],
                                         attn_T[:, 2 * D:3 * D], start=True, stop=True)
                    last.then_inc(g_done, 1)
                elif stage == "o":
                    pe.wait_ge(ui_ready, k + 1)
                    for j in range(PT):
                        if j % TILES == 0:
                            pe.wait_ge(scan_done, PAIR * k + j // TILES + 1)
                        last = t_.transpose(A[k][:, j * P:(j + 1) * P], o_T[k][:, j * P:(j + 1) * P], ident[:])
                    last.then_inc(o_ready, 1)
                elif stage == "out_q":
                    pe.wait_ge(sg_ready, k + 1)
                    pe.wait_ge(q_ready["out"], PT * (k + 1))
                    transpose_tiles(B[k], q["out"][k]).then_inc(qT_ready["out"], 1)
                elif stage == "res":
                    pe.wait_ge(qT_moved["out"], k + 1)
                    for j in range(PT):
                        last = t_.matmul(A[k][:, j * D:(j + 1) * D], qT["out"][k][:, j * P:(j + 1) * P], attn_T[:, 3 * D:4 * D],
                                         start=True, stop=True)
                    last.then_inc(wo_done, 1)
                elif stage == "mlp_q":
                    pe.wait_ge(q_ready["mlp"], PT * (k + 1))
                    transpose_tiles(B[k], q["mlp"][k]).then_inc(qT_ready["mlp"], 1)
                elif stage.startswith("gate"):
                    j = int(stage[-1])
                    n = PT * k + j
                    if j == 0:
                        pe.wait_ge(qT_moved["mlp"], k + 1)
                        if k == 0:
                            pe.wait_ge(wT_moved, 5)
                    else:
                        pe.wait_ge(za_ready, n)
                    t_.matmul(A[k][:, 0:INNER], qT["mlp"][k][:, j * P:(j + 1) * P], gate_T[:, 0:INNER],
                              start=True, stop=True).then_inc(gate_done, 1)
                    if j:
                        pe.wait_ge(z_ready, n)
                    t_.matmul(B[k][:, 0:INNER], qT["mlp"][k][:, j * P:(j + 1) * P], gate_T[:, INNER:GATE_ROWS],
                              start=True, stop=True).then_inc(value_done, 1)
                elif stage.startswith("z_q"):
                    j = int(stage[-1])
                    pe.wait_ge((qz_vec, qz_act)[j % 2], PT // 2 * k + j // 2 + 1)
                    if j >= 2:
                        pe.wait_ge(qT_moved["z"], PT * k + j - 1)
                    for c, rows in DOWN:
                        last = t_.transpose((A, B)[j % 2][k][0:rows, c * P:(c + 1) * P], q["z"][k][:, j, c * P:c * P + rows], ident[:])
                    last.then_inc(qT_ready["z"], 1)
                elif stage == "down":
                    pe.wait_ge(qT_moved["z"], PT * (k + 1))
                    for j in range(PT):
                        for c, rows in DOWN:
                            last = t_.matmul(A[k][:, j * D:(j + 1) * D], qT_z[k][0:rows, j, c, :], down_T[0:rows, c, :],
                                             start=(c == 0), stop=(c == len(DOWN) - 1))
                    last.then_inc(down_done, 1)
                elif stage == "x1":
                    pe.wait_ge(x1_ready, PT * (k + 1))
                    transpose_tiles(B[k], x1[k]).then_inc(x1T_ready, 1)
                elif stage == "scores":
                    pe.wait_ge(x1T_moved, k + 1)
                    for j in range(PT):
                        r, h = divmod(j, TILES)
                        t_.matmul((A, B)[r][k][:, h * SEQ:(h + 1) * SEQ], x1_T[k][:, j * P:(j + 1) * P],
                                  ctx_T[k][:, r * SEQ:(r + 1) * SEQ], start=True, stop=True).then_inc(scores_done, 1)
                elif stage == "turn":
                    for j in range(PT):
                        r, h = divmod(j, TILES)
                        pe.wait_ge(prob_ready, PT * k + j + 1)
                        if h == 0:
                            pe.wait_ge(sc_ready, PT * k + (r + 1) * TILES)
                        for t in range(TILES):
                            last = t_.transpose((A, B)[r][k][:, t * SEQ + h * P:t * SEQ + (h + 1) * P],
                                                prob[k][:, j, t * P:(t + 1) * P], ident[:])
                        if h == TILES - 1:
                            last.then_inc(probT_ready, 1)
                elif stage == "attend":
                    for r in range(PAIR):
                        pe.wait_ge(probT_moved, PAIR * k + r + 1)
                        for t in range(TILES):
                            last = t_.matmul((A, B)[r][k][:, 0:SEQ], ctx[:, k, r * TILES + t, :], prob_T[k][:, r, t, :],
                                             start=(t == 0), stop=(t == TILES - 1))
                        last.then_inc(att_done, 1)
                elif stage == "ln2":
                    pe.wait_ge(attT_moved, PAIR * (k + 1))
                    for j in range(PT):
                        last = t_.matmul(A[k][:, j * D:(j + 1) * D], att_T[k][:, j * P:(j + 1) * P], xw_T[:], start=True, stop=True)
                    last.then_inc(proj_done, 1)
                elif stage == "x2":
                    pe.wait_ge(x2_ready, PT * (k + 1))
                    transpose_tiles(B[k], x2[k]).then_inc(x2T_ready, 1)
                elif stage == "router":
                    pe.wait_ge(x2T_moved, k + 1)
                    for j in range(PT):
                        last = t_.matmul(A[k][:, j * EXPERTS:(j + 1) * EXPERTS], x2_T[k][:, j * P:(j + 1) * P], wr_sb[:],
                                         start=True, stop=True)
                    last.then_inc(logits_done, 1)
                elif stage == "turn_gates":
                    pe.wait_ge(gatew_ready, k + 1)
                    for j in range(PT):
                        last = t_.transpose(B[k][0:EXPERTS, j * P:(j + 1) * P], gate_w[k][:, j, :], ident[:])
                    last.then_inc(gwT_ready, 1)
                elif stage == "bias2":
                    pe.wait_ge(gwT_moved, k + 1)
                    for j in range(PT):
                        last = t_.matmul(A[k][:, j * D:(j + 1) * D], gate_wT[k][:, j * P:(j + 1) * P], b2_sb[:], start=True, stop=True)
                    last.then_inc(b2_done, 1)

            def weights_sum(g):
                pe.wait_ge(wsq_ready, 2 * LOADS // NORM_GROUPS * (g + 1))
                pe.wait_ge(wscale_ready, 2)
                if g:
                    pe.wait_ge(wtot_moved, g)
                t_.matmul(Y[1][:, g, 0:PT], ones[:], flat(w_sumsq[:, g]), start=True, stop=True).then_inc(wsum_done, 1)

            def fc1(k, e, c):
                n = (k * EXPERTS + e) * CHUNKS + c
                if c == 0:
                    if k == 0:
                        pe.wait_ge(w_lo_ready[0], e // WLOAD + 1)
                    if e == 0:
                        pe.wait_ge(x2lo_ready, k + 1)
                hi = x2_hi[:, k].rearrange("p r t -> p (r t)")
                lo = x2_lo[:, k].rearrange("p r t -> p (r t)")
                if n >= HBANKS:
                    pe.wait_ge(gelu_done, n - HBANKS + 1)
                cols = slice(c * P, (c + 1) * P)
                bank = H[n % HBANKS]
                t_.matmul(bank[:], w_hi[0][:, e, cols], hi, start=True, stop=False)
                t_.matmul(bank[:], w_hi[0][:, e, cols], lo, start=False, stop=False)
                t_.matmul(bank[:], w_lo[0][:, e, cols], hi, start=False, stop=True).then_inc(fc1_done, 1)

            def fc2(k, e, j):
                n = k * EXPERTS + e
                if j == 0:
                    if k == 0:
                        pe.wait_ge(w_lo_ready[1], e // WLOAD + 1)
                    if n == 1:
                        pe.wait_ge(wtot_moved, NORM_GROUPS)
                    if n >= YBANKS:
                        pe.wait_ge(combined, PT * (n - YBANKS + 1))
                    for c in range(CHUNKS):
                        lo_wait(pe, n * CHUNKS + c)
                cols = slice(j * P, (j + 1) * P)
                bank = Y[n % YBANKS]
                for c in range(CHUNKS):
                    rows = slice(c * D, (c + 1) * D)
                    t_.matmul(bank[:, j, :], h_hi[:, e % 2, c, cols], w_hi[1][:, e, rows], start=(c == 0), stop=False)
                    t_.matmul(bank[:, j, :], h_hi[:, e % 2, c, cols], w_lo[1][:, e, rows], start=False, stop=False)
                    last = t_.matmul(bank[:, j, :], h_lo[:, e % 2, c, cols], w_hi[1][:, e, rows], start=False,
                                     stop=(c == CHUNKS - 1))
                if j == PT - 1:
                    last.then_inc(fc2_done, 1)

            for what in order_of("PE"):
                if what[0] == "ab":
                    ab(*what[1:])
                elif what[0] == "means":
                    ternary_sums(*what[1:])
                elif what[0] == "turn_w":
                    ternary_turn(*what[1:])
                elif what[0] == "turn_small":
                    turn_small()
                elif what[0] == "sum_w":
                    weights_sum(*what[1:])
                elif what[0] == "fc1":
                    fc1(*what[1:])
                elif what[0] == "fc2":
                    fc2(*what[1:])


_NAMES = ["x", "ctx_1024", "_lenS2", "L0_attn_lower_bound", "L0_attn_attn_norm_w", "L0_attn_w_i", "L0_attn_w_f",
          "L0_attn_w_g", "L0_attn_g_norm_w", "L0_attn_w_o", "L0_attn_mlp_norm_w", "L0_attn_w_gate",
          "L0_attn_w_down", "L0_xattn_W", "L0_xattn_b", "L0_ffn_W1", "L0_ffn_b1", "L0_ffn_W2", "L0_ffn_b2",
          "L0_ffn_Wr", "L0_ffn_br"]


def kernel(**inputs):
    import numpy as np
    import concourse.bacc as bacc
    from concourse.bass_utils import run_bass_kernel_spmd

    nc = bacc.Bacc("TRN2", target_bir_lowering=False, num_devices=1)
    arrays, args = {}, []
    for name in _NAMES:
        a = np.ascontiguousarray(inputs[name])
        arrays[f"in_{name}"] = a
        args.append(nc.dram_tensor(f"in_{name}", a.shape, mybir.dt.from_np(a.dtype), kind="ExternalInput").ap())
    out = nc.dram_tensor("out", (BATCH, SEQ, D), mybir.dt.float32, kind="ExternalOutput")
    decoder_layer(nc, *args, out.ap())
    result = run_bass_kernel_spmd(nc, [arrays], core_ids=[0])
    return result.results[0]["out"]
```
